# Optimizing a Trainium2 kernel written in Bass

```python
import numpy as np
import jax
import jax.numpy as jnp

def _softmax(x, axis=-1):
    return jax.nn.softmax(x, axis=axis)

def _gelu(x):
    return jax.nn.gelu(x, approximate=True)

def _silu(x):
    return jax.nn.silu(x)

def _sigmoid(x):
    return jax.nn.sigmoid(x)

def _layernorm(x, axis=-1, eps=1e-05):
    m = jnp.mean(x, axis=axis, keepdims=True)
    v = jnp.var(x, axis=axis, keepdims=True)
    return (x - m) / jnp.sqrt(v + eps)

def _scatter_add(tgt, idx, src, axis=0):
    return tgt.at[idx].add(src)

def _segment_sum(src, seg, n):
    return jax.ops.segment_sum(src, seg, n)
kernel_name = 'mk_hybrid_d1_jaxref_r4_2a12a3'

def setup_inputs(seed: int=0):
    np.random.seed(seed)
    _w = jnp.asarray

    def _L0_attn_a_setup():
        import jax, jax.numpy as jnp
        import numpy as np
        B, T, HM = (2, 512, 256)
        HEADS = 16
        DK = HM // 2 // HEADS
        DV = HM // HEADS
        LOW_RANK = 16
        GATE_NORM = 16.0
        EPS = 1e-05

        def _ln(x, w, b):
            m = x.mean(-1, keepdims=True)
            v = ((x - m) ** 2).mean(-1, keepdims=True)
            return (x - m) * jax.lax.rsqrt(v + EPS) * w + b

        def _rms(x, w):
            return x * jax.lax.rsqrt((x * x).mean(-1, keepdims=True) + EPS) * w

        def _gla(q, k, v, gk):

            def step(S, inp):
                qt, kt, vt, gt = inp
                S = jnp.exp(gt)[..., None] * S + kt[..., None] * vt[..., None, :]
                return (S, jnp.einsum('bhk,bhkv->bhv', qt, S))
            xs = tuple((jnp.moveaxis(a, 1, 0) for a in (q, k, v, gk)))
            S0 = jnp.zeros((q.shape[0], q.shape[2], q.shape[3], v.shape[3]), q.dtype)
            _, o = jax.lax.scan(step, S0, xs)
            return jnp.moveaxis(o, 0, 1)
        key = jax.random.key(seed)
        ks = jax.random.split(key, 12)

        def p(k, shape, s=0.02):
            return jax.random.normal(k, shape, jnp.float32) * s
        return dict(x=jax.random.normal(ks[0], (B, T, HM), jnp.float32), ln_w=jnp.ones((HM,), jnp.float32), ln_b=jnp.zeros((HM,), jnp.float32), Wq=p(ks[1], (HM, HEADS * DK)), Wk=p(ks[2], (HM, HEADS * DK)), Wv=p(ks[3], (HM, HEADS * DV)), gk_w1=p(ks[4], (HM, LOW_RANK)), gk_w2=p(ks[5], (LOW_RANK, HEADS * DK)), gk_b2=jnp.zeros((HEADS * DK,), jnp.float32), Wg=p(ks[6], (HM, HEADS * DV)), rms_w=jnp.ones((DV,), jnp.float32), Wo=p(ks[7], (HEADS * DV, HM)), W1=p(ks[8], (HM, 2 * HM)), b1=jnp.zeros((2 * HM,), jnp.float32), W2=p(ks[9], (2 * HM, HM)), b2=jnp.zeros((HM,), jnp.float32))
    _L0_attn_a_in = _L0_attn_a_setup()

    def _L0_attn_b_setup():
        import jax, jax.numpy as jnp
        import numpy as np
        key = jax.random.key(seed)
        ks = jax.random.split(key, 6)
        B_, S, D, N = (8, 1024, 256, 16)
        return {'x': jax.random.normal(ks[0], (B_, S, D), dtype=jnp.float32), 'A': jax.random.normal(ks[1], (N, N), dtype=jnp.float32), 'B': jax.random.normal(ks[2], (D, N), dtype=jnp.float32), 'C': jax.random.normal(ks[3], (N, D), dtype=jnp.float32), 'W_out': jax.random.normal(ks[4], (D, D), dtype=jnp.float32) * 0.02, 'b_out': jax.random.normal(ks[5], (D,), dtype=jnp.float32) * 0.02}
    _L0_attn_b_in = _L0_attn_b_setup()

    def _L0_ffn_setup():
        import jax, jax.numpy as jnp
        import numpy as np
        K_TOP = 2
        key = jax.random.key(seed)
        k1, k2, k3 = jax.random.split(key, 3)
        B, S, H, E = (4, 512, 256, 8)
        hidden_states = jax.random.normal(k1, (B, S, H), dtype=jnp.float32)
        router_w = jax.random.normal(k2, (E, H), dtype=jnp.float32) * 0.02
        expert_weights = jax.random.normal(k3, (E, H, H), dtype=jnp.float32) * 0.02
        return {'hidden_states': hidden_states, 'router_w': router_w, 'expert_weights': expert_weights}
    _L0_ffn_in = _L0_ffn_setup()
    _d = {'L0_attn_a_x': _L0_attn_a_in['x'], 'L0_attn_a_ln_w': _L0_attn_a_in['ln_w'], 'L0_attn_a_ln_b': _L0_attn_a_in['ln_b'], 'L0_attn_a_Wq': _L0_attn_a_in['Wq'], 'L0_attn_a_Wk': _L0_attn_a_in['Wk'], 'L0_attn_a_Wv': _L0_attn_a_in['Wv'], 'L0_attn_a_gk_w1': _L0_attn_a_in['gk_w1'], 'L0_attn_a_gk_w2': _L0_attn_a_in['gk_w2'], 'L0_attn_a_gk_b2': _L0_attn_a_in['gk_b2'], 'L0_attn_a_Wg': _L0_attn_a_in['Wg'], 'L0_attn_a_rms_w': _L0_attn_a_in['rms_w'], 'L0_attn_a_Wo': _L0_attn_a_in['Wo'], 'L0_attn_a_W1': _L0_attn_a_in['W1'], 'L0_attn_a_b1': _L0_attn_a_in['b1'], 'L0_attn_a_W2': _L0_attn_a_in['W2'], 'L0_attn_a_b2': _L0_attn_a_in['b2'], 'L0_attn_b_A': _L0_attn_b_in['A'], 'L0_attn_b_B': _L0_attn_b_in['B'], 'L0_attn_b_C': _L0_attn_b_in['C'], 'L0_attn_b_W_out': _L0_attn_b_in['W_out'], 'L0_attn_b_b_out': _L0_attn_b_in['b_out'], 'L0_ffn_router_w': _L0_ffn_in['router_w'], 'L0_ffn_expert_weights': _L0_ffn_in['expert_weights']}
    _x0 = _d['L0_attn_a_x']
    _d['L0_attn_a_x'] = jax.random.normal(jax.random.fold_in(jax.random.key(seed), 1), (8, 1024, 256), dtype=_x0.dtype)
    del _x0
    return _d

def reference(L0_attn_a_x, L0_attn_a_ln_w, L0_attn_a_ln_b, L0_attn_a_Wq, L0_attn_a_Wk, L0_attn_a_Wv, L0_attn_a_gk_w1, L0_attn_a_gk_w2, L0_attn_a_gk_b2, L0_attn_a_Wg, L0_attn_a_rms_w, L0_attn_a_Wo, L0_attn_a_W1, L0_attn_a_b1, L0_attn_a_W2, L0_attn_a_b2, L0_attn_b_A, L0_attn_b_B, L0_attn_b_C, L0_attn_b_W_out, L0_attn_b_b_out, L0_ffn_router_w, L0_ffn_expert_weights):

    def _L0_attn_a_ref(x, ln_w, ln_b, Wq, Wk, Wv, gk_w1, gk_w2, gk_b2, Wg, rms_w, Wo, W1, b1, W2, b2):
        import jax, jax.numpy as jnp
        import numpy as np
        B, T, HM = (2, 512, 256)
        HEADS = 16
        DK = HM // 2 // HEADS
        DV = HM // HEADS
        LOW_RANK = 16
        GATE_NORM = 16.0
        EPS = 1e-05

        def _ln(x, w, b):
            m = x.mean(-1, keepdims=True)
            v = ((x - m) ** 2).mean(-1, keepdims=True)
            return (x - m) * jax.lax.rsqrt(v + EPS) * w + b

        def _rms(x, w):
            return x * jax.lax.rsqrt((x * x).mean(-1, keepdims=True) + EPS) * w

        def _gla(q, k, v, gk):

            def step(S, inp):
                qt, kt, vt, gt = inp
                S = jnp.exp(gt)[..., None] * S + kt[..., None] * vt[..., None, :]
                return (S, jnp.einsum('bhk,bhkv->bhv', qt, S))
            xs = tuple((jnp.moveaxis(a, 1, 0) for a in (q, k, v, gk)))
            S0 = jnp.zeros((q.shape[0], q.shape[2], q.shape[3], v.shape[3]), q.dtype)
            _, o = jax.lax.scan(step, S0, xs)
            return jnp.moveaxis(o, 0, 1)
        Bb, Tt, _ = x.shape
        h = _ln(x, ln_w, ln_b)
        q = (h @ Wq).reshape(Bb, Tt, HEADS, DK)
        k = (h @ Wk).reshape(Bb, Tt, HEADS, DK)
        v = (h @ Wv).reshape(Bb, Tt, HEADS, DV)
        gk = jax.nn.log_sigmoid(h @ gk_w1 @ gk_w2 + gk_b2) / GATE_NORM
        gk = gk.reshape(Bb, Tt, HEADS, DK)
        o = _gla(q * DK ** (-0.5), k, v, gk)
        g = (h @ Wg).reshape(Bb, Tt, HEADS, DV)
        o = _rms(o, rms_w) * (g * jax.nn.sigmoid(g))
        x = x + o.reshape(Bb, Tt, HEADS * DV) @ Wo
        h2 = _ln(x, ln_w, ln_b)
        return x + jax.nn.gelu(h2 @ W1 + b1, approximate=False) @ W2 + b2

    def _L0_attn_b_ref(x, A, B, C, W_out, b_out):
        import jax, jax.numpy as jnp
        import numpy as np
        xB = jnp.einsum('bsd,dn->sbn', x, B)
        h0 = jnp.zeros((x.shape[0], A.shape[0]), dtype=x.dtype)

        def step(h, xb_t):
            h = jnp.tanh(xb_t + h @ A.T)
            return (h, h)
        _, hs = jax.lax.scan(step, h0, xB)
        y = jnp.einsum('sbn,nd->bsd', hs, C)
        return y @ W_out.T + b_out

    def _L0_ffn_ref(hidden_states, router_w, expert_weights):
        import jax, jax.numpy as jnp
        import numpy as np
        K_TOP = 2
        B, S, H = hidden_states.shape
        x = hidden_states.reshape(-1, H)
        logits = x @ router_w.T
        probs = jax.nn.softmax(logits, axis=-1)
        topk_vals, topk_idx = jax.lax.top_k(probs, K_TOP)
        topk_w = topk_vals / (topk_vals.sum(-1, keepdims=True) + 1e-06)
        expert_out = jnp.einsum('nh,eho->eno', x, expert_weights)
        combined = jnp.take_along_axis(expert_out.transpose(1, 0, 2), topk_idx[:, :, None], axis=1)
        combined = combined.transpose(1, 0, 2)
        remap_bias = jnp.take_along_axis(probs, topk_idx, axis=1).T[:, :, None]
        weights = topk_w.T[:, :, None]
        out = ((combined + remap_bias) * weights).sum(axis=0)
        return out.reshape(B, S, H)
    x = L0_attn_a_x
    x = x + _L0_attn_a_ref(_layernorm(x, axis=-1), L0_attn_a_ln_w, L0_attn_a_ln_b, L0_attn_a_Wq, L0_attn_a_Wk, L0_attn_a_Wv, L0_attn_a_gk_w1, L0_attn_a_gk_w2, L0_attn_a_gk_b2, L0_attn_a_Wg, L0_attn_a_rms_w, L0_attn_a_Wo, L0_attn_a_W1, L0_attn_a_b1, L0_attn_a_W2, L0_attn_a_b2)
    x = x + _L0_ffn_ref(_layernorm(x, axis=-1), L0_ffn_router_w, L0_ffn_expert_weights)
    x = x + _L0_attn_b_ref(_layernorm(x, axis=-1), L0_attn_b_A, L0_attn_b_B, L0_attn_b_C, L0_attn_b_W_out, L0_attn_b_b_out)
    x = x + _L0_ffn_ref(_layernorm(x, axis=-1), L0_ffn_router_w, L0_ffn_expert_weights)
    return x

_drawn_inputs = setup_inputs


def setup_inputs(seed=0):
    import zlib

    import numpy as np

    out = dict(_drawn_inputs(seed))
    spreads = {'L0_attn_a_ln_w': (1.0, 0.2),
     'L0_attn_a_ln_b': (0.0, 0.303),
     'L0_attn_a_gk_b2': (0.0, 0.8),
     'L0_attn_a_rms_w': (1.0, 0.6),
     'L0_attn_a_b1': (0.0, 0.1),
     'L0_attn_a_b2': (0.0, 0.1)}
    factors = {'L0_attn_a_gk_w1': 8.0, 'L0_attn_a_gk_w2': 8.0, 'L0_attn_b_b_out': 4.831}
    for name, (base, spread) in spreads.items():
        noise = np.random.default_rng([zlib.crc32(name.encode()), seed]).standard_normal(out[name].shape)
        drawn = base * np.exp(spread * noise) if base else spread * noise
        out[name] = jnp.asarray(drawn.astype(out[name].dtype))
    for name, factor in factors.items():
        out[name] = (out[name] * factor).astype(out[name].dtype)
    return out
```

```python
from contextlib import ExitStack

import concourse.bass as bass
import numpy as np
from concourse import mybir

F32 = mybir.dt.float32
U32 = mybir.dt.uint32
ALU = mybir.AluOpType
ACT = mybir.ActivationFunctionType
AX = mybir.AxisListType

P = 128
B, T, D = 8, 1024, 256
TS = 32
ROUNDS = T // TS
TOK = B * TS
TILES = TOK // P
BQ = B // TILES
KC = D // P
HEADS, DK, DV = 16, 8, 16
HQ = 4
J = HEADS // HQ
RANK = 16
GATE_NORM = 16.0
FF = 512
FB = FF // P
E, TOPK = 8, 2
N = 16
NP = 32
EPS = 1e-5
TOPK_EPS = 1e-6
QSCALE = float(DK) ** -0.5
MID = TS // 2 - 1
GMAX = 80.0 * GATE_NORM
MT = 2 * TILES
PAIRS = E // 2
GROUPS = MT * PAIRS
SKEW = 3
PEELED = SKEW + 1

C_ID, C_CAUSAL, C_HEAD, C_BLOCK, C_IOTA, C_RESET = 0, 128, 160, 164, 228, 236
C_END = C_RESET + TOK


def constants():
    c = np.zeros((P, C_END), np.float32)
    p = np.arange(P)
    c[:, C_ID:C_ID + P] = np.eye(P)
    c[:, C_CAUSAL:C_CAUSAL + TS] = (p[:, None] % TS) <= np.arange(TS)[None]
    c[:, C_HEAD:C_HEAD + HQ] = (p[:, None] // DK % HQ) == np.arange(HQ)[None]
    c[:, C_BLOCK:C_BLOCK + HQ * DV] = (p[:, None] // DK % HQ) == (np.arange(HQ * DV)[None] // DV)
    c[:, C_IOTA:C_IOTA + E] = np.arange(E)[None]
    c[:, C_RESET:] = (np.arange(TOK)[None] % TS) != 0
    return c


def build(nc, x, wts, out):
    ctx = ExitStack()
    with ctx:
        def sb(name, shape, dt=F32):
            return ctx.enter_context(nc.sbuf_tensor(name, shape, dt))

        sems = {}

        def sem(name):
            if name not in sems:
                sems[name] = ctx.enter_context(nc.semaphore(name))
            return sems[name]

        cst = sb("cst", [P, C_END])
        ident = cst[:, C_ID:C_ID + P]
        causal = cst[:, C_CAUSAL:C_CAUSAL + TS]
        headmask = cst[:, C_HEAD:C_HEAD + HQ]
        blockmask = cst[:, C_BLOCK:C_BLOCK + HQ * DV]
        iota = cst[:, C_IOTA:C_IOTA + E]
        reset = cst[:, C_RESET:C_RESET + TOK]
        lnw, lnb = sb("lnw", [P, KC]), sb("lnb", [P, KC])
        wq, wk = sb("wq", [P, KC, P]), sb("wk", [P, KC, P])
        w1g, w2g, b2g = sb("w1g", [P, KC, RANK]), sb("w2g", [RANK, P]), sb("b2g", [P, 1])
        wvg = sb("wvg", [P, KC, 2 * D])
        rmsw, rmsh = sb("rmsw", [P, 1]), sb("rmsh", [P, 1])
        wo = sb("wo", [P, KC, D])
        w1, b1 = sb("w1", [P, KC, FF]), sb("b1", [P, FB])
        w2, b2 = sb("w2", [P, FB, D]), sb("b2", [P, D])
        rw = sb("rw", [P, KC, E])
        we = sb("we", [P, KC, E * D])
        bin_ = sb("bin_", [P, KC, NP])
        aT = sb("aT", [P, NP])
        cT = sb("cT", [P, KC, N])
        woutT = sb("woutT", [P, KC, D])
        cw = sb("cw", [N, D])
        bout = sb("bout", [P, D])
        mhalf = sb("mhalf", [P, 2 * HEADS])

        xin = sb("xin", [P, TILES, D])
        st_a, mv_a = sb("st_a", [P, TILES, 6]), sb("mv_a", [P, TILES, 2])
        ra = sb("ra", [P, 7, TILES])
        xhat, y0 = sb("xhat", [P, TILES, D]), sb("y0", [P, TILES, D])
        res = sb("res", [P, TILES, D])
        hT = sb("hT", [P, KC, TOK])
        u_sb = sb("u_sb", [RANK, TOK])
        zb, nz, ge, gl = (sb(n, [P, TOK]) for n in ("zb", "nz", "ge", "gl"))
        glog, gcum, grel, gclip = (sb(n, [P, TOK]) for n in ("glog", "gcum", "grel", "gclip"))
        eq, ek = sb("eq", [P, B, TS]), sb("ek", [P, B, TS])
        emid, dec = sb("emid", [P, B]), sb("dec", [P, B])
        qt, kt = sb("qt", [P, TOK]), sb("kt", [P, TOK])
        qx = sb("qx", [P, HQ, TOK])
        ktok = sb("ktok", [P, TILES, P])
        vtok = sb("vtok", [P, TILES, D])
        th, sg = sb("th", [P, TILES, D]), sb("sg", [P, TILES, D])
        att = sb("att", [P, J, TILES * HQ, TS])
        state, smid = sb("state", [P, B, HQ * DV]), sb("smid", [P, B, HQ * DV])
        sx = sb("sx", [P, B, D])
        dstate = sb("dstate", [P, B, HQ * DV])
        osq = sb("osq", [P, TILES * HEADS, DV])
        oss, omean, orstd = (sb(n, [P, TILES * HEADS]) for n in ("oss", "omean", "orstd"))
        onorm, og = sb("onorm", [P, TILES * HEADS, DV]), sb("og", [P, TILES, D])
        oT = sb("oT", [P, KC, TOK])
        xmid = sb("xmid", [P, TILES, D])
        st_f, mv_f, rf = sb("st_f", [P, TILES, 6]), sb("mv_f", [P, TILES, 2]), sb("rf", [P, 2, TILES])
        y1 = sb("y1", [P, TILES, D])
        h2T = sb("h2T", [P, KC, TOK])
        sum2 = sb("sum2", [P, TILES, D])
        gT = sb("gT", [P, FB, TOK])

        moe_in = sb("moe_in", [P, MT, D])
        st_m, mv_m, rm = sb("st_m", [P, MT, 6]), sb("mv_m", [P, MT, 2]), sb("rm", [P, 2, MT])
        ym = sb("ym", [P, MT, D])
        yT = sb("yT", [P, KC, MT * P])
        lg = sb("lg", [P, MT, E])
        mx, ix = sb("mx", [P, MT, 8]), sb("ix", [P, MT, 8], U32)
        ixf = sb("ixf", [P, MT, TOPK])
        lsub, pe_ = sb("lsub", [P, MT, E + TOPK]), sb("pe_", [P, MT, E + TOPK])
        psum_e, pinv = sb("psum_e", [P, MT]), sb("pinv", [P, MT])
        pk, wk_, pw = (sb(n, [P, MT, TOPK]) for n in ("pk", "wk_", "pw"))
        pden, pden2, pdinv, mbias = (sb(n, [P, MT]) for n in ("pden", "pden2", "pdinv", "mbias"))
        oh = sb("oh", [P, TOPK, MT, E])
        coef = sb("coef", [P, MT, E])
        acc = sb("acc", [P, MT, D])

        st_r, mv_r, rr = sb("st_r", [P, TILES, 6]), sb("mv_r", [P, TILES, 2]), sb("rr", [P, 2, TILES])
        yr = sb("yr", [P, TILES, D])
        yrT = sb("yrT", [P, KC, TOK])
        x2b = sb("x2b", [P, TILES, D])
        hs = sb("hs", [P, B, TS])

        ps = ctx.enter_context(nc.psum_tensor("ps", [P, 8, 512], F32))
        RB, M0 = 5, 6

        loads = [
            (cst[:], wts["consts"]),
            (lnw[:], wts["ln_w"]), (lnb[:], wts["ln_b"]),
            (wq[:], wts["Wq"]), (wk[:], wts["Wk"]),
            (w1g[:], wts["gk_w1"]), (w2g[:], wts["gk_w2"]), (b2g[:], wts["gk_b2"]),
            (wvg[:, :, 0:D], wts["Wv"]), (wvg[:, :, D:2 * D], wts["Wg"]),
            (rmsw[:], wts["rms_w"]), (wo[:], wts["Wo"]),
            (w1[:], wts["W1"]), (b1[:], wts["b1"]), (w2[:], wts["W2"]), (b2[:], wts["b2"]),
            (rw[:], wts["router_w"]),
            (bin_[:, :, 0:N], wts["Bin"]), (cT[:], wts["C"]), (woutT[:], wts["W_out"]), (bout[:], wts["b_out"]),
        ] + [(we[:, :, e * D:(e + 1) * D], wts["experts"][:, :, e, :]) for e in range(E)]
        WEIGHTS = 16 * len(loads)

        def live(it, skew):
            return not isinstance(it, int) or 0 <= it - skew < ROUNDS

        def past(count):
            return max(count, 0) if isinstance(count, int) else count

        def value(eng, count):
            return past(count) if isinstance(count, int) else eng.to_reg(count)

        def rounds(eng, body):
            for it in range(PEELED):
                body(it)
            with eng.Fori(PEELED, ROUNDS) as it:
                body(it)
            for it in range(ROUNDS, ROUNDS + SKEW):
                body(it)

        block = ctx.enter_context(nc.Block())

        @block.sync
        def _(sp):
            def load_x(n):
                for b in range(B):
                    i, q = b // BQ, b % BQ
                    sp.dma_start(xin[q * TS:(q + 1) * TS, i, :], x[b, bass.ds(n * TS, TS), :])\
                        .then_inc(sem("x_loaded"), 16)

            load_x(0)
            for dst, src in loads:
                sp.dma_start(dst, src).then_inc(sem("weights"), 16)
            sp.wait_ge(sem("pads_zero"), 1)
            sp.dma_start(aT[0:N, 0:N], wts["A"]).then_inc(sem("a_loaded"), 16)

            def body(it):
                if live(it, 0) and live(it + 1, 0):
                    sp.wait_ge(sem("y0"), it + 1)
                    sp.wait_ge(sem("res"), it + 1)
                    load_x(it + 1)
                if live(it, 3):
                    for i in range(TILES):
                        sp.wait_ge(sem(f"acc{E - 1}"), it * MT + TILES + i + 1)
                        for q in range(BQ):
                            sp.dma_start(out[i * BQ + q, bass.ds((it - 3) * TS, TS), :],
                                         acc[q * TS:(q + 1) * TS, TILES + i, :]).then_inc(sem("stored"), 16)

            for it in range(PEELED):
                body(it)
            with sp.Fori(PEELED, ROUNDS - 1) as it:
                body(it)
            for it in range(ROUNDS - 1, ROUNDS + SKEW):
                body(it)
            sp.wait_ge(sem("stored"), 16 * B * ROUNDS)

        @block.gpsimd
        def _(pool):
            g = nc.gpsimd
            g.memset(mhalf[:], -0.5)
            g.memset(moe_in[:], 0.0)
            g.memset(hs[:], 0.0)
            g.memset(state[:], 0.0)
            g.memset(sx[:], 0.0)
            g.memset(bin_[:, :, N:NP], 0.0)
            g.memset(aT[:], 0.0).then_inc(sem("pads_zero"), 1)
            pool.wait_ge(sem("pads_zero"), 1)
            pool.wait_ge(sem("weights"), WEIGHTS)
            g.tensor_scalar(rmsh[:], rmsw[:], 0.5, 1.0, ALU.mult, ALU.mult).then_inc(sem("rms_half"), 1)

            def rstd(var, buf, name, it, count):
                count = value(pool, count)
                pool.wait_ge(sem("weights"), WEIGHTS)
                pool.wait_ge(sem(f"mv_{name}"), count)
                g.tensor_scalar(buf[:, 0, :], var, EPS, 1.0, ALU.add, ALU.mult).then_inc(sem(f"var_{name}"), 1)
                pool.wait_ge(sem(f"var_{name}"), past(count))
                w = var.shape[1]
                g.tensor_tensor(buf[:, 1, :], buf[:, 0, :], mhalf[:, 0:w], ALU.pow).then_inc(sem(f"rstd_{name}"), 1)

            def body(it):
                rstd(mv_m[:, :, 1], rm, "m", it, it + 1)
                if live(it, 0):
                    rstd(mv_a[:, :, 1], ra, "a", it, it + 1)
                    pool.wait_ge(sem("rstd_a"), it + 1)
                    g.tensor_tensor(ra[:, 2, :], ra[:, 1, :], ra[:, 1, :], ALU.mult).then_inc(sem("ra2"), 1)
                    pool.wait_ge(sem("ra2"), it + 1)
                    g.tensor_tensor(ra[:, 3, :], ra[:, 2, :], mv_a[:, :, 1], ALU.mult).then_inc(sem("ra3"), 1)
                    count = value(pool, it + 1)
                    pool.wait_ge(sem("weights"), WEIGHTS)
                    pool.wait_ge(sem("ra3"), count)
                    g.tensor_scalar(ra[:, 4, :], ra[:, 3, :], EPS, 1.0, ALU.add, ALU.mult).then_inc(sem("ra4"), 1)
                    pool.wait_ge(sem("ra4"), it + 1)
                    g.tensor_tensor(ra[:, 5, :], ra[:, 4, :], mhalf[:, 0:TILES], ALU.pow).then_inc(sem("ra5"), 1)
                    pool.wait_ge(sem("ra5"), it + 1)
                    g.tensor_tensor(ra[:, 6, :], ra[:, 5, :], ra[:, 1, :], ALU.mult).then_inc(sem("rstd_inner"), 1)
                    pool.wait_ge(sem("sum2"), past(it))
                    g.tensor_tensor(res[:], xin[:], b2[:].unsqueeze(1).broadcast_to([P, TILES, D]), ALU.add).then_inc(sem("res"), 1)
                    pool.wait_ge(sem("emid"), it + 1)
                    pool.wait_ge(sem("state"), past(it))
                    g.tensor_tensor(dec[:], emid[:], eq[:, :, TS - 1], ALU.mult).then_inc(sem("dec"), 1)
                    g.tensor_tensor(smid[:], state[:], emid[:].unsqueeze(2).broadcast_to([P, B, HQ * DV]), ALU.mult).then_inc(sem("smid"), 1)
                    pool.wait_ge(sem("smid"), it + 1)
                    pool.wait_ge(sem("o_ready"), past(it))
                    for j in range(J):
                        r = slice(j * 32, j * 32 + 32)
                        g.tensor_tensor(sx[r, :, j * HQ * DV:(j + 1) * HQ * DV], smid[r],
                                              blockmask[r].unsqueeze(1).broadcast_to([32, B, HQ * DV]), ALU.mult).then_inc(sem("sx"), 1)
                        pool.wait_ge(sem("sx"), it * J + j + 1)
                    pool.wait_ge(sem("dec"), it + 1)
                    g.tensor_tensor(state[:], state[:], dec[:].unsqueeze(2).broadcast_to([P, B, HQ * DV]), ALU.mult).then_inc(sem("sdec"), 1)
                    count = value(pool, it + 1)
                    pool.wait_ge(sem("weights"), WEIGHTS)
                    pool.wait_ge(sem("oss"), count)
                    g.tensor_scalar(omean[:], oss[:], 1.0 / DV, EPS, ALU.mult, ALU.add).then_inc(sem("omean"), 1)
                    pool.wait_ge(sem("omean"), it + 1)
                    g.tensor_tensor(orstd[:], omean[:], mhalf[:], ALU.pow).then_inc(sem("orstd"), 1)
                    pool.wait_ge(sem("dstate"), it + 1)
                    pool.wait_ge(sem("sdec"), it + 1)
                    g.tensor_tensor(state[:], state[:], dstate[:], ALU.add).then_inc(sem("state"), 1)
                    rstd(mv_f[:, :, 1], rf, "f", it, it + 1)
                    pool.wait_ge(sem("x1"), past(it))
                    pool.wait_ge(sem("res"), it + 1)
                    g.tensor_tensor(sum2[:], res[:], xmid[:], ALU.add).then_inc(sem("sum2"), 1)
                if live(it, 1):
                    rstd(mv_r[:, :, 1], rr, "r", it, it)
                    pool.wait_ge(sem("x3"), past(it - 2))
                    if live(it, 2):
                        pool.wait_ge(sem("x3"), past(it - 1))
                    g.tensor_tensor(x2b[:], acc[:, 0:TILES, :], bout[:].unsqueeze(1).broadcast_to([P, TILES, D]), ALU.add).then_inc(sem("x2b"), 1)

            rounds(pool, body)

        @block.scalar
        def _(act):
            a = nc.scalar
            act.wait_ge(sem("weights"), WEIGHTS)
            act.wait_ge(sem("cw_psum"), 1)
            a.activation(cw[:], ps[0:N, 0, 0:D], ACT.Copy).then_inc(sem("cw"), 1)
            act.wait_ge(sem("pads_zero"), 1)
            act.wait_ge(sem("rms_half"), 1)

            def rnn(it, k):
                if live(it, 2):
                    act.wait_ge(sem("rnn_mm"), (it - 2) * TS + k + 1)
                    a.activation(hs[0:N, :, k], ps[0:N, RB, 0:TOK].rearrange("p (b t) -> p b t", t=TS)[:, :, k], ACT.Tanh).then_inc(sem("rnn_h"), 1)

            def body(it):
                a.preload_act_table_set("natural_log_exp_and_others")
                for half in range(2):
                    act.wait_ge(sem("ymT"), it * 2 + half + 1)
                    a.activation(yT[:, :, half * TOK:(half + 1) * TOK],
                                      ps[:, M0 + half, :].rearrange("p (k t) -> p k t", k=KC), ACT.Copy).then_inc(sem("yT"), 1)
                if live(it, 0):
                    act.wait_ge(sem("y0T"), it + 1)
                    for c in range(KC):
                        ins = a.activation(hT[:, c, :], ps[:, 0, c * TOK:(c + 1) * TOK], ACT.Identity,
                                           bias=lnb[:, c:c + 1], scale=lnw[:, c:c + 1])
                    ins.then_inc(sem("hT"), 1)
                    act.wait_ge(sem("u_psum"), it + 1)
                    a.activation(u_sb[:], ps[0:RANK, 2, 0:TOK], ACT.Copy).then_inc(sem("u"), 1)
                    act.wait_ge(sem("nz"), it + 1)
                    a.activation(ge[:], nz[:], ACT.Exp).then_inc(sem("ge"), 1)
                    act.wait_ge(sem("ge"), it + 1)
                    a.activation(gl[:], ge[:], ACT.Ln, bias=1.0).then_inc(sem("gl"), 1)
                act.wait_ge(sem("lsub"), it + 1)
                a.activation(pe_[:], lsub[:], ACT.Exp).then_inc(sem("pe_"), 1)
                if live(it, 0):
                    act.wait_ge(sem("gclip"), it + 1)
                    act.wait_ge(sem("dstate"), past(it))
                    act.wait_ge(sem("dec"), past(it))
                    a.activation(eq[:], gclip[:].rearrange("p (b t) -> p b t", t=TS), ACT.Exp, scale=1.0 / GATE_NORM).then_inc(sem("eq"), 1)
                    a.activation(ek[:], gclip[:].rearrange("p (b t) -> p b t", t=TS), ACT.Exp, scale=-1.0 / GATE_NORM).then_inc(sem("ek"), 1)
                    act.wait_ge(sem("sx"), past(it * J))
                    a.activation(emid[:], gcum[:].rearrange("p (b t) -> p b t", t=TS)[:, :, MID], ACT.Exp, scale=1.0 / GATE_NORM).then_inc(sem("emid"), 1)
                a.preload_act_table_set("gelu_and_others")
                if live(it, 0):
                    act.wait_ge(sem("vg_psum"), it + 1)
                    a.activation(th[:], ps[:, 3:5, D:2 * D], ACT.Tanh, scale=0.5).then_inc(sem("th"), 1)
                    a.activation(vtok[:], ps[:, 3:5, 0:D], ACT.Copy).then_inc(sem("vtok"), 1)
                    act.wait_ge(sem("ktT"), it + 1)
                    a.activation(ktok[:], ps[:, 0, 0:TOK].rearrange("p (i c) -> p i c", c=P), ACT.Copy).then_inc(sem("ktok"), 1)
                for k in range(0, 10):
                    rnn(it, k)
                if live(it, 0):
                    act.wait_ge(sem("o_ready"), it + 1)
                    a.activation(osq[:], ps[:, 0, :].rearrange("p (h v) -> p h v", v=DV), ACT.Square).then_inc(sem("osq"), 1)
                for k in range(10, 16):
                    rnn(it, k)
                if live(it, 0):
                    act.wait_ge(sem("ogT"), it + 1)
                    a.activation(oT[:].rearrange("p c t -> p (c t)"), ps[:, 1, :], ACT.Copy, scale=rmsh[:]).then_inc(sem("oT"), 1)
                for k in range(16, 22):
                    rnn(it, k)
                if live(it, 0):
                    act.wait_ge(sem("y1T"), it + 1)
                    for c in range(KC):
                        ins = a.activation(h2T[:, c, :], ps[:, 3, c * TOK:(c + 1) * TOK], ACT.Identity,
                                           bias=lnb[:, c:c + 1], scale=lnw[:, c:c + 1])
                    ins.then_inc(sem("h2T"), 1)
                for k in range(22, 24):
                    rnn(it, k)
                if live(it, 0):
                    for f in range(FB):
                        act.wait_ge(sem("ff1_psum"), it * 2 + f // 2 + 1)
                        bank = (1, 4)[f // 2]
                        a.activation(gT[:, f, :], ps[:, bank, (f % 2) * TOK:(f % 2 + 1) * TOK], ACT.Gelu,
                                          bias=b1[:, f:f + 1]).then_inc(sem("gT"), 1)
                for k in range(24, TS):
                    rnn(it, k)
                if live(it, 1):
                    act.wait_ge(sem("yrT_psum"), past(it))
                    a.activation(yrT[:], ps[:, M0, :].rearrange("p (k t) -> p k t", k=KC), ACT.Copy).then_inc(sem("yrT"), 1)

            rounds(act, body)

        @block.vector
        def _(dve):
            v = nc.vector
            dve.wait_ge(sem("weights"), WEIGHTS)
            dve.wait_ge(sem("pads_zero"), 1)
            dve.wait_ge(sem("rms_half"), 1)

            def stats(src, tiles, st, mv, name, count):
                for i in range(tiles):
                    v.bn_stats(st[:, i, :], src[:, i, :]).then_inc(sem(f"st_{name}"), 1)
                count = value(dve, count * tiles)
                dve.wait_ge(sem("weights"), WEIGHTS)
                dve.wait_ge(sem(f"st_{name}"), count)
                for i in range(tiles):
                    ins = v.bn_aggr(mv[:, i, :], st[:, i, :])
                ins.then_inc(sem(f"mv_{name}"), 1)

            def normed(dst, src, tiles, mv, scale, i0=0):
                for i in range(tiles):
                    ins = v.tensor_scalar(dst[:, i, :], src[:, i, :], mv[:, i, 0:1], scale[:, i:i + 1], ALU.subtract, ALU.mult)
                return ins

            def combine(it, g):
                i, pr = g // PAIRS, g % PAIRS
                dve.wait_ge(sem(f"moe_psum{pr}"), it * MT + i + 1)
                for e in (2 * pr, 2 * pr + 1):
                    if e == 0:
                        dve.wait_ge(sem("acc_start"), it + 1)
                    else:
                        dve.wait_ge(sem(f"acc{e - 1}"), it * MT + i + 1)
                    v.scalar_tensor_tensor(acc[:, i, :], ps[:, M0 + g % 2, e % 2 * D:(e % 2 + 1) * D], coef[:, i, e:e + 1],
                                                acc[:, i, :], ALU.mult, ALU.add).then_inc(sem(f"acc{e}"), 1)

            def bt(ap):
                return ap.rearrange("p (b t) -> p b t", t=TS)

            def body(it):
                if isinstance(it, int) and it == 0:
                    pass
                dve.wait_ge(sem("x1"), past(min(it, ROUNDS) if isinstance(it, int) else it))
                if isinstance(it, int):
                    dve.wait_ge(sem("x3"), past(min(max(it - 2, 0), ROUNDS)))
                else:
                    dve.wait_ge(sem("x3"), past(it - 2))
                stats(moe_in, MT, st_m, mv_m, "m", it + 1)
                if live(it, 0):
                    dve.wait_ge(sem("x_loaded"), past((it + 1) * 16 * B))
                    stats(xin, TILES, st_a, mv_a, "a", it + 1)
                dve.wait_ge(sem("rstd_m"), it + 1)
                normed(ym, moe_in, MT, mv_m, rm[:, 1, :]).then_inc(sem("ym"), 1)
                if live(it, 0):
                    dve.wait_ge(sem("rstd_a"), it + 1)
                    dve.wait_ge(sem("mv_a"), it + 1)
                    normed(xhat, xin, TILES, mv_a, ra[:, 1, :]).then_inc(sem("xhat"), 1)
                    dve.wait_ge(sem("rstd_inner"), it + 1)
                    normed(y0, xin, TILES, mv_a, ra[:, 6, :]).then_inc(sem("y0"), 1)
                dve.wait_ge(sem("lg_psum"), it + 1)
                v.tensor_copy(lg[:], ps[:, 0, 0:MT * E].rearrange("p (i e) -> p i e", e=E)).then_inc(sem("lg"), 1)
                count = value(dve, it + 1)
                dve.wait_ge(sem("weights"), WEIGHTS)
                dve.wait_ge(sem("lg"), count)
                for i in range(MT):
                    ins = v.max(mx[:, i, :], lg[:, i, :])
                ins.then_inc(sem("mx"), 1)
                count = value(dve, it + 1)
                dve.wait_ge(sem("weights"), WEIGHTS)
                dve.wait_ge(sem("mx"), count)
                for i in range(MT):
                    ins = v.max_index(ix[:, i, :], mx[:, i, :], lg[:, i, :])
                ins.then_inc(sem("ix"), 1)
                top = mx[:, :, 0:1]
                v.tensor_tensor(lsub[:, :, 0:E], lg[:], top.broadcast_to([P, MT, E]), ALU.subtract)
                v.tensor_tensor(lsub[:, :, E:E + TOPK], mx[:, :, 0:TOPK], top.broadcast_to([P, MT, TOPK]), ALU.subtract).then_inc(sem("lsub"), 1)
                dve.wait_ge(sem("ix"), it + 1)
                v.tensor_copy(ixf[:], ix[:, :, 0:TOPK]).then_inc(sem("ixf"), 1)
                if live(it, 0):
                    dve.wait_ge(sem("z_psum"), it + 1)
                    v.tensor_scalar(zb[:], ps[:, 2, TOK:2 * TOK], b2g[:, 0:1], None, ALU.add).then_inc(sem("zb"), 1)
                    dve.wait_ge(sem("zb"), it + 1)
                    v.scalar_tensor_tensor(nz[:], zb[:], -1.0, zb[:], ALU.mult, ALU.min).then_inc(sem("nz"), 1)
                    dve.wait_ge(sem("gl"), it + 1)
                    v.scalar_tensor_tensor(glog[:], zb[:], 0.0, gl[:], ALU.min, ALU.subtract).then_inc(sem("glog"), 1)
                    dve.wait_ge(sem("glog"), it + 1)
                    v.tensor_tensor_scan(gcum[:], reset, glog[:], 0.0, ALU.mult, ALU.add).then_inc(sem("gcum"), 1)
                    dve.wait_ge(sem("gcum"), it + 1)
                    v.tensor_tensor(bt(grel[:]), bt(gcum[:]), bt(gcum[:])[:, :, MID:MID + 1].broadcast_to([P, B, TS]), ALU.subtract).then_inc(sem("grel"), 1)
                    dve.wait_ge(sem("grel"), it + 1)
                    v.tensor_scalar(gclip[:], grel[:], -GMAX, GMAX, ALU.max, ALU.min).then_inc(sem("gclip"), 1)
                dve.wait_ge(sem("pe_"), it + 1)
                v.tensor_reduce(psum_e[:], pe_[:, :, 0:E], AX.X, ALU.add).then_inc(sem("psum_e"), 1)
                dve.wait_ge(sem("psum_e"), it + 1)
                v.reciprocal(pinv[:], psum_e[:]).then_inc(sem("pinv"), 1)
                dve.wait_ge(sem("pinv"), it + 1)
                v.tensor_tensor(pk[:], pe_[:, :, E:E + TOPK], pinv[:].unsqueeze(2).broadcast_to([P, MT, TOPK]), ALU.mult).then_inc(sem("pk"), 1)
                dve.wait_ge(sem("pk"), it + 1)
                v.tensor_reduce(pden[:], pk[:], AX.X, ALU.add).then_inc(sem("pden"), 1)
                dve.wait_ge(sem("pden"), it + 1)
                v.tensor_scalar(pden2[:], pden[:], TOPK_EPS, None, ALU.add).then_inc(sem("pden2"), 1)
                dve.wait_ge(sem("pden2"), it + 1)
                v.reciprocal(pdinv[:], pden2[:]).then_inc(sem("pdinv"), 1)
                dve.wait_ge(sem("pdinv"), it + 1)
                v.tensor_tensor(wk_[:], pk[:], pdinv[:].unsqueeze(2).broadcast_to([P, MT, TOPK]), ALU.mult).then_inc(sem("wk_"), 1)
                dve.wait_ge(sem("wk_"), it + 1)
                v.tensor_tensor(pw[:], pk[:], wk_[:], ALU.mult).then_inc(sem("pw"), 1)
                dve.wait_ge(sem("ixf"), it + 1)
                for i in range(MT):
                    for k in range(TOPK):
                        ins = v.tensor_scalar(oh[:, k, i, :], iota, ixf[:, i, k:k + 1], wk_[:, i, k:k + 1], ALU.is_equal, ALU.mult)
                ins.then_inc(sem("oh"), 1)
                dve.wait_ge(sem("pw"), it + 1)
                v.tensor_reduce(mbias[:], pw[:], AX.X, ALU.add).then_inc(sem("mbias"), 1)
                dve.wait_ge(sem("oh"), it + 1)
                v.tensor_tensor(coef[:], oh[:, 0], oh[:, 1], ALU.add).then_inc(sem("coef"), 1)
                dve.wait_ge(sem("mbias"), it + 1)
                if isinstance(it, int):
                    dve.wait_ge(sem("stored"), past(max(it - 3, 0) * 16 * B))
                else:
                    dve.wait_ge(sem("stored"), past((it - 3) * 16 * B))
                if live(it - 1, 1):
                    dve.wait_ge(sem("x2b"), past(min(it - 1, ROUNDS) if isinstance(it, int) else it - 1))
                for i in range(MT):
                    ins = v.tensor_scalar(acc[:, i, :], moe_in[:, i, :], mbias[:, i:i + 1], None, ALU.add)
                ins.then_inc(sem("acc_start"), 1)
                dve.wait_ge(sem("coef"), it + 1)
                combine(it, 0)
                combine(it, 1)
                if live(it, 0):
                    dve.wait_ge(sem("eq"), it + 1)
                    v.scalar_tensor_tensor(qt[:], ps[:, 1, 0:TOK], QSCALE, eq[:].rearrange("p b t -> p (b t)"), ALU.mult, ALU.mult).then_inc(sem("qt"), 1)
                    dve.wait_ge(sem("ek"), it + 1)
                    v.tensor_tensor(kt[:], ps[:, 1, TOK:2 * TOK], ek[:].rearrange("p b t -> p (b t)"), ALU.mult).then_inc(sem("kt"), 1)
                    dve.wait_ge(sem("qt"), it + 1)
                    for h in range(HQ):
                        ins = v.tensor_scalar(qx[:, h, :], qt[:], headmask[:, h:h + 1], None, ALU.mult)
                    ins.then_inc(sem("qx"), 1)
                    dve.wait_ge(sem("vtok"), it + 1)
                    v.scalar_tensor_tensor(sg[:], th[:], 1.0, ps[:, 3:5, D:2 * D], ALU.add, ALU.mult).then_inc(sem("sg"), 1)
                combine(it, 2)
                if live(it, 0):
                    dve.wait_ge(sem("scores"), it + 1)
                    v.tensor_tensor(att[:], ps[:, 1:5, 0:TILES * P].rearrange("p j (g t) -> p j g t", t=TS),
                                         causal.unsqueeze(1).unsqueeze(1).broadcast_to([P, J, TILES * HQ, TS]), ALU.mult).then_inc(sem("att"), 1)
                combine(it, 3)
                combine(it, 4)
                combine(it, 5)
                if live(it, 0):
                    dve.wait_ge(sem("dS_psum"), it + 1)
                    dve.wait_ge(sem("state"), past(it))
                    v.tensor_tensor(dstate[:].rearrange("p (i q) c -> p i q c", q=BQ),
                                         ps[:, 1:5, TOK:TOK + TILES * HQ * DV].rearrange("p q (i c) -> p i q c", i=TILES),
                                         eq[:, :, TS - 1:TS].rearrange("p (i q) o -> p i q o", q=BQ).broadcast_to([P, TILES, BQ, HQ * DV]),
                                         ALU.mult).then_inc(sem("dstate"), 1)
                    dve.wait_ge(sem("osq"), it + 1)
                    v.tensor_reduce(oss[:], osq[:], AX.X, ALU.add).then_inc(sem("oss"), 1)
                combine(it, 6)
                combine(it, 7)
                if live(it, 1):
                    dve.wait_ge(sem(f"acc{E - 1}"), past(it * MT + TILES))
                    stats(acc, TILES, st_r, mv_r, "r", it)
                if live(it, 0):
                    dve.wait_ge(sem("orstd"), it + 1)
                    v.tensor_tensor(onorm[:], ps[:, 0, :].rearrange("p (h v) -> p h v", v=DV),
                                         orstd[:].unsqueeze(2).broadcast_to([P, TILES * HEADS, DV]), ALU.mult).then_inc(sem("onorm"), 1)
                    dve.wait_ge(sem("onorm"), it + 1)
                    v.tensor_tensor(og[:].rearrange("p i d -> p (i d)"), onorm[:].rearrange("p h v -> p (h v)"),
                                         sg[:].rearrange("p i d -> p (i d)"), ALU.mult).then_inc(sem("og"), 1)
                combine(it, 8)
                if live(it, 0):
                    dve.wait_ge(sem("attn_psum"), it + 1)
                    dve.wait_ge(sem("sum2"), past(it))
                    v.tensor_tensor(xmid[:].rearrange("p i d -> p (i d)"), ps[:, 2, :], xhat[:].rearrange("p i d -> p (i d)"), ALU.add).then_inc(sem("xmid"), 1)
                    dve.wait_ge(sem("xmid"), it + 1)
                    stats(xmid, TILES, st_f, mv_f, "f", it + 1)
                combine(it, 9)
                if live(it, 0):
                    dve.wait_ge(sem("rstd_f"), it + 1)
                    normed(y1, xmid, TILES, mv_f, rf[:, 1, :]).then_inc(sem("y1"), 1)
                combine(it, 10)
                combine(it, 11)
                combine(it, 12)
                combine(it, 13)
                if live(it, 0):
                    dve.wait_ge(sem("ff2_psum"), it + 1)
                    dve.wait_ge(sem("sum2"), it + 1)
                    v.tensor_tensor(moe_in[:, 0:TILES, :].rearrange("p i d -> p (i d)"), ps[:, 2, :],
                                         sum2[:].rearrange("p i d -> p (i d)"), ALU.add).then_inc(sem("x1"), 1)
                combine(it, 14)
                combine(it, 15)
                if live(it, 1):
                    dve.wait_ge(sem("rstd_r"), past(it))
                    normed(yr, acc, TILES, mv_r, rr[:, 1, :]).then_inc(sem("yr"), 1)
                if live(it, 2):
                    dve.wait_ge(sem("rout_psum"), past(it - 1))
                    dve.wait_ge(sem("x2b"), past(it - 1))
                    v.tensor_tensor(moe_in[:, TILES:MT, :].rearrange("p i d -> p (i d)"), ps[:, M0 + 1, :],
                                         x2b[:].rearrange("p i d -> p (i d)"), ALU.add).then_inc(sem("x3"), 1)

            rounds(dve, body)

        @block.tensor
        def _(pe):
            t = nc.tensor
            pe.wait_ge(sem("weights"), WEIGHTS)
            pe.wait_ge(sem("pads_zero"), 1)
            for c in range(KC):
                ins = t.matmul(ps[0:N, 0, 0:D], cT[:, c, :], woutT[:, c, :], start=(c == 0), stop=(c == KC - 1))
            ins.then_inc(sem("cw_psum"), 1)
            pe.wait_ge(sem("a_loaded"), 16)
            pe.wait_ge(sem("cw"), 1)

            def moe(it, g):
                i, pr = g // PAIRS, g % PAIRS
                if g >= 2:
                    pe.wait_ge(sem(f"acc{2 * ((g - 2) % PAIRS) + 1}"), it * MT + (g - 2) // PAIRS + 1)
                for c in range(KC):
                    ins = t.matmul(ps[:, M0 + g % 2, :], yT[:, c, i * P:(i + 1) * P], we[:, c, pr * 2 * D:(pr + 1) * 2 * D],
                                   start=(c == 0), stop=(c == KC - 1))
                ins.then_inc(sem(f"moe_psum{pr}"), 1)

            def rnn(it, k):
                if live(it, 2):
                    count = value(pe, (it - 2) * TS + k)
                    pe.wait_ge(sem("weights"), WEIGHTS)
                    pe.wait_ge(sem("rnn_h"), count)
                    t.matmul(ps[0:NP, RB, 0:TOK].rearrange("p (b t) -> p b t", t=TS)[:, :, k], aT[:],
                                  hs[:, :, (k - 1) % TS], start=False, stop=True, skip_group_check=True).then_inc(sem("rnn_mm"), 1)

            def body(it):
                pe.wait_ge(sem("ym"), it + 1)
                if live(it - 1, 1):
                    pe.wait_ge(sem("yrT"), past(min(it - 1, ROUNDS) if isinstance(it, int) else it - 1))
                pe.wait_ge(sem(f"acc{E - 1}"), past(it * MT))
                for half in range(2):
                    for c in range(KC):
                        for i in range(TILES):
                            ins = t.transpose(ps[:, M0 + half, c * TOK + i * P:c * TOK + (i + 1) * P],
                                              ym[:, half * TILES + i, c * P:(c + 1) * P], ident)
                    ins.then_inc(sem("ymT"), 1)
                if live(it, 0):
                    pe.wait_ge(sem("y0"), it + 1)
                    pe.wait_ge(sem("onorm"), past(it))
                    for c in range(KC):
                        for i in range(TILES):
                            ins = t.transpose(ps[:, 0, c * TOK + i * P:c * TOK + (i + 1) * P], y0[:, i, c * P:(c + 1) * P], ident)
                    ins.then_inc(sem("y0T"), 1)
                pe.wait_ge(sem("yT"), past(2 * it + 2))
                if live(it, 0):
                    pe.wait_ge(sem("hT"), it + 1)
                for i in range(MT):
                    for c in range(KC):
                        ins = t.matmul(ps[:, 0, i * E:(i + 1) * E], yT[:, c, i * P:(i + 1) * P], rw[:, c, :],
                                       start=(c == 0), stop=(c == KC - 1))
                ins.then_inc(sem("lg_psum"), 1)
                if live(it, 0):
                    pe.wait_ge(sem("x1"), past(it))
                    for c in range(KC):
                        ins = t.matmul(ps[0:RANK, 2, 0:TOK], w1g[:, c, :], hT[:, c, :], start=(c == 0), stop=(c == KC - 1))
                    ins.then_inc(sem("u_psum"), 1)
                    pe.wait_ge(sem("gT"), past(it * FB))
                    for w, col in ((wq, 0), (wk, TOK)):
                        for c in range(KC):
                            ins = t.matmul(ps[:, 1, col:col + TOK], w[:, c, :], hT[:, c, :], start=(c == 0), stop=(c == KC - 1))
                    ins.then_inc(sem("qk_psum"), 1)
                    pe.wait_ge(sem("u"), it + 1)
                    t.matmul(ps[:, 2, TOK:2 * TOK], w2g[:], u_sb[:], start=True, stop=True).then_inc(sem("z_psum"), 1)
                    for i in range(TILES):
                        for c in range(KC):
                            ins = t.matmul(ps[:, 3 + i, :], hT[:, c, i * P:(i + 1) * P], wvg[:, c, :], start=(c == 0), stop=(c == KC - 1))
                    ins.then_inc(sem("vg_psum"), 1)
                moe(it, 0)
                moe(it, 1)
                if live(it, 0):
                    pe.wait_ge(sem("lg"), it + 1)
                    pe.wait_ge(sem("kt"), it + 1)
                    for i in range(TILES):
                        ins = t.transpose(ps[:, 0, i * P:(i + 1) * P], kt[:, i * P:(i + 1) * P], ident)
                    ins.then_inc(sem("ktT"), 1)
                moe(it, 2)
                rnn(it, 0), rnn(it, 1)
                if live(it, 0):
                    count = value(pe, it + 1)
                    pe.wait_ge(sem("weights"), WEIGHTS)
                    pe.wait_ge(sem("qx"), count)
                    pe.wait_ge(sem("zb"), it + 1)
                    pe.wait_ge(sem("sg"), it + 1)
                    pe.wait_ge(sem("vtok"), it + 1)
                    for b in range(B):
                        i, q = b // BQ, b % BQ
                        for j in range(J):
                            r = slice(32 * j, 32 * j + 32)
                            ins = t.matmul(ps[q * 32:q * 32 + 32, 1 + j, i * P:(i + 1) * P], kt[r, b * TS:(b + 1) * TS],
                                           qx[r, :, b * TS:(b + 1) * TS], start=True, stop=True)
                    ins.then_inc(sem("scores"), 1)
                moe(it, 3)
                rnn(it, 2), rnn(it, 3)
                moe(it, 4)
                rnn(it, 4), rnn(it, 5)
                if live(it, 0):
                    pe.wait_ge(sem("att"), it + 1)
                    pe.wait_ge(sem("ktok"), it + 1)
                    pe.wait_ge(sem("sx"), past((it + 1) * J))
                    for b in range(B):
                        i, q = b // BQ, b % BQ
                        r = slice(q * 32, q * 32 + 32)
                        t.matmul(ps[r, 0, i * D:(i + 1) * D], qt[:, b * TS:(b + 1) * TS], sx[:, b, :],
                                 start=True, stop=False, skip_group_check=True)
                        for h in range(HEADS):
                            ins = t.matmul(ps[r, 0, i * D + h * DV:i * D + (h + 1) * DV], att[r, h // HQ, i * HQ + h % HQ, :],
                                           vtok[r, i, h * DV:(h + 1) * DV], start=False, stop=(h == HEADS - 1), skip_group_check=True)
                    ins.then_inc(sem("o_ready"), 1)
                moe(it, 5)
                rnn(it, 6), rnn(it, 7)
                if live(it, 0):
                    for b in range(B):
                        i, q = b // BQ, b % BQ
                        r = slice(q * 32, q * 32 + 32)
                        for j in range(J):
                            ins = t.matmul(ps[32 * j:32 * j + 32, 1 + q, TOK + i * HQ * DV:TOK + (i + 1) * HQ * DV],
                                           ktok[r, i, 32 * j:32 * j + 32], vtok[r, i, j * HQ * DV:(j + 1) * HQ * DV], start=True, stop=True)
                    ins.then_inc(sem("dS_psum"), 1)
                moe(it, 6)
                rnn(it, 8), rnn(it, 9)
                moe(it, 7)
                rnn(it, 10), rnn(it, 11)
                if live(it, 0):
                    pe.wait_ge(sem("og"), it + 1)
                    pe.wait_ge(sem("dstate"), it + 1)
                    for c in range(KC):
                        for i in range(TILES):
                            ins = t.transpose(ps[:, 1, c * TOK + i * P:c * TOK + (i + 1) * P], og[:, i, c * P:(c + 1) * P], ident)
                    ins.then_inc(sem("ogT"), 1)
                moe(it, 8)
                for k in range(12, 16):
                    rnn(it, k)
                if live(it, 0):
                    pe.wait_ge(sem("oT"), it + 1)
                    for i in range(TILES):
                        for c in range(KC):
                            ins = t.matmul(ps[:, 2, i * D:(i + 1) * D], oT[:, c, i * P:(i + 1) * P], wo[:, c, :], start=(c == 0), stop=(c == KC - 1))
                    ins.then_inc(sem("attn_psum"), 1)
                moe(it, 9)
                rnn(it, 16), rnn(it, 17), rnn(it, 18)
                moe(it, 10)
                rnn(it, 19), rnn(it, 20), rnn(it, 21)
                if live(it, 0):
                    pe.wait_ge(sem("y1"), it + 1)
                    for c in range(KC):
                        for i in range(TILES):
                            ins = t.transpose(ps[:, 3, c * TOK + i * P:c * TOK + (i + 1) * P], y1[:, i, c * P:(c + 1) * P], ident)
                    ins.then_inc(sem("y1T"), 1)
                moe(it, 11)
                rnn(it, 22), rnn(it, 23)
                if live(it, 0):
                    pe.wait_ge(sem("h2T"), it + 1)
                    for f in range(FB):
                        for c in range(KC):
                            ins = t.matmul(ps[:, (1, 4)[f // 2], (f % 2) * TOK:(f % 2 + 1) * TOK], w1[:, c, f * P:(f + 1) * P], h2T[:, c, :],
                                           start=(c == 0), stop=(c == KC - 1))
                        if f % 2:
                            ins.then_inc(sem("ff1_psum"), 1)
                moe(it, 12)
                rnn(it, 24), rnn(it, 25)
                moe(it, 13)
                rnn(it, 26), rnn(it, 27)
                if live(it, 0):
                    pe.wait_ge(sem("gT"), past((it + 1) * FB))
                    pe.wait_ge(sem("xmid"), it + 1)
                    for i in range(TILES):
                        for f in range(FB):
                            ins = t.matmul(ps[:, 2, i * D:(i + 1) * D], gT[:, f, i * P:(i + 1) * P], w2[:, f, :], start=(f == 0), stop=(f == FB - 1))
                    ins.then_inc(sem("ff2_psum"), 1)
                moe(it, 14)
                rnn(it, 28), rnn(it, 29)
                moe(it, 15)
                rnn(it, 30), rnn(it, 31)
                if live(it, 1):
                    pe.wait_ge(sem("yr"), past(it))
                    pe.wait_ge(sem(f"acc{E - 1}"), past((it + 1) * MT))
                    for c in range(KC):
                        for i in range(TILES):
                            ins = t.transpose(ps[:, M0, c * TOK + i * P:c * TOK + (i + 1) * P], yr[:, i, c * P:(c + 1) * P], ident)
                    ins.then_inc(sem("yrT_psum"), 1)
                if live(it, 2):
                    pe.wait_ge(sem("rnn_h"), past((it - 1) * TS))
                    pe.wait_ge(sem(f"acc{E - 1}"), past((it + 1) * MT))
                    for i in range(TILES):
                        ins = t.matmul(ps[:, M0 + 1, i * D:(i + 1) * D],
                                       hs[0:N, i * BQ:(i + 1) * BQ, :].rearrange("p b t -> p (b t)"), cw[:], start=True, stop=True)
                    ins.then_inc(sem("rout_psum"), 1)
                if live(it, 1):
                    pe.wait_ge(sem("yrT"), past(it))
                    for c in range(KC):
                        t.matmul(ps[0:NP, RB, 0:TOK], bin_[:, c, :], yrT[:, c, :], start=(c == 0), stop=(c == KC - 1), skip_group_check=True)

            rounds(pe, body)


def kernel(**inputs):
    import numpy as _np
    import concourse.bacc as _bacc
    from concourse import mybir as _mybir
    from concourse.bass_utils import run_bass_kernel_spmd as _run

    a = {k.replace("L0_attn_a_", "").replace("L0_attn_b_", "rnn_").replace("L0_ffn_", ""): _np.asarray(v) for k, v in inputs.items()}

    def rows(w):
        return _np.ascontiguousarray(w.reshape(-1, P, w.shape[1]).transpose(1, 0, 2))

    def cols(b):
        return _np.ascontiguousarray(b.reshape(-1, P).T)

    def everywhere(b):
        return _np.ascontiguousarray(_np.broadcast_to(b, (P, b.shape[0])))

    arrays = {
        "x": a["x"], "consts": constants(), "ln_w": cols(a["ln_w"]), "ln_b": cols(a["ln_b"]),
        "Wq": rows(a["Wq"]), "Wk": rows(a["Wk"]), "Wv": rows(a["Wv"]), "Wg": rows(a["Wg"]),
        "gk_w1": rows(a["gk_w1"]), "gk_w2": a["gk_w2"], "gk_b2": cols(a["gk_b2"]),
        "rms_w": _np.ascontiguousarray(_np.broadcast_to(a["rms_w"], (P // DV, DV)).reshape(P, 1)),
        "Wo": rows(a["Wo"]), "W1": rows(a["W1"]), "b1": cols(a["b1"]), "W2": rows(a["W2"]), "b2": everywhere(a["b2"]),
        "router_w": rows(a["router_w"].T),
        "experts": _np.ascontiguousarray(a["expert_weights"].reshape(E, KC, P, D).transpose(2, 1, 0, 3)),
        "Bin": rows(a["rnn_B"]), "A": _np.ascontiguousarray(a["rnn_A"].T), "C": rows(a["rnn_C"].T),
        "W_out": rows(a["rnn_W_out"].T), "b_out": everywhere(a["rnn_b_out"]),
    }
    nc = _bacc.Bacc("TRN2", target_bir_lowering=False, num_devices=1)
    arrays = {f"in_{k}": _np.ascontiguousarray(v) for k, v in arrays.items()}
    drams = {k[3:]: nc.dram_tensor(k, v.shape, _mybir.dt.from_np(v.dtype), kind="ExternalInput").ap() for k, v in arrays.items()}
    out = nc.dram_tensor("out", (B, T, D), _mybir.dt.float32, kind="ExternalOutput").ap()
    x = drams.pop("x")
    build(nc, x, drams, out)
    r = _run(nc, [arrays], core_ids=[0])
    return r.results[0]["out"]
```

```python
from contextlib import ExitStack

import concourse.bass as bass
import numpy as np
from concourse import mybir

F32 = mybir.dt.float32
F32R = mybir.dt.float32r
U32 = mybir.dt.uint32
ALU = mybir.AluOpType
ACT = mybir.ActivationFunctionType
AX = mybir.AxisListType

P = 128
B, T, D = 8, 1024, 256
TS = 32
ROUNDS = T // TS
TOK = B * TS
TILES = TOK // P
BQ = B // TILES
KC = D // P
HEADS, DK, DV = 16, 8, 16
HQ = 4
J = HEADS // HQ
RANK = 16
GATE_NORM = 16.0
FF = 512
FB = FF // P
E, TOPK = 8, 2
N = 16
NP = 32
EPS = 1e-5
TOPK_EPS = 1e-6
QSCALE = float(DK) ** -0.5
MID = TS // 2 - 1
GMAX = 80.0 * GATE_NORM
PAIRS = E // 2
GROUPS = TILES * PAIRS
ATTN, FFN, MIX1, RNN, MIX2 = range(5)
SKEW = MIX2
PEELED = SKEW + 1
SLOTS = ["G0", "G1", "G2", "T2", "G3", "G4", "L2", "G5", "G6", "G7", "G8", "G9", "TR", "G10", "G11", "G12",
         "T1", "G13", "L1", "G14", "G15", "RO"]

C_ID, C_CAUSAL, C_HEAD, C_BLOCK, C_IOTA, C_RESET = 0, 128, 160, 164, 228, 236
C_END = C_RESET + TOK


def constants():
    c = np.zeros((P, C_END), np.float32)
    p = np.arange(P)
    c[:, C_ID:C_ID + P] = np.eye(P)
    c[:, C_CAUSAL:C_CAUSAL + TS] = (p[:, None] % TS) <= np.arange(TS)[None]
    c[:, C_HEAD:C_HEAD + HQ] = (p[:, None] // DK % HQ) == np.arange(HQ)[None]
    c[:, C_BLOCK:C_BLOCK + HQ * DV] = (p[:, None] // DK % HQ) == (np.arange(HQ * DV)[None] // DV)
    c[:, C_IOTA:C_IOTA + E] = np.arange(E)[None]
    c[:, C_RESET:] = (np.arange(TOK)[None] % TS) != 0
    return c


def build(nc, x, wts, out):
    ctx = ExitStack()
    with ctx:
        def sb(name, shape, dt=F32):
            return ctx.enter_context(nc.sbuf_tensor(name, shape, dt))

        sems = {}

        def sem(name):
            if name not in sems:
                sems[name] = ctx.enter_context(nc.semaphore(name))
            return sems[name]

        cst = sb("cst", [P, C_END])
        ident = cst[:, C_ID:C_ID + P]
        causal = cst[:, C_CAUSAL:C_CAUSAL + TS]
        headmask = cst[:, C_HEAD:C_HEAD + HQ]
        blockmask = cst[:, C_BLOCK:C_BLOCK + HQ * DV]
        iota = cst[:, C_IOTA:C_IOTA + E]
        reset = cst[:, C_RESET:C_RESET + TOK]
        stage = sb("stage", [P, KC * E * D])
        lnw, lnb = sb("lnw", [P, KC]), sb("lnb", [P, KC])
        w1g, w2g, b2g = sb("w1g", [P, KC, RANK]), sb("w2g", [RANK, P]), sb("b2g", [P, 1])
        rmsw, rmsh = sb("rmsw", [P, 1]), sb("rmsh", [P, 1])
        b1, b2, bout = sb("b1", [P, FB]), sb("b2", [P, D]), sb("bout", [P, D])
        bin_, aT = sb("bin_", [P, KC, NP]), sb("aT", [P, NP])
        cT, woutT, cw = sb("cT", [P, KC, N]), sb("woutT", [P, KC, D]), sb("cw", [N, D])
        mhalf = sb("mhalf", [P, TILES * HEADS])
        W_Q, W_K, W_VG, W_O, W_1, W_2 = (0, KC * P, 2 * KC * P, 2 * KC * P + KC * 2 * D,
                                         2 * KC * P + KC * 3 * D, 2 * KC * P + KC * 3 * D + KC * FF)
        W_R = W_2 + FB * D
        W_END = W_R
        wa = sb("wa", [P, 2, W_END], F32R)
        we = sb("we", [P, 2, KC * E * D], F32R)
        rw, rws = sb("rw", [P, KC, E]), sb("rws", [P, 2, KC, E], F32R)

        def wcols(base, part, c, width, at, n):
            o = base + c * width + at
            return wa[:, part, o:o + n]

        xin = sb("xin", [P, TILES, D])
        st_a, mv_a, ra = sb("st_a", [P, TILES, 6]), sb("mv_a", [P, TILES, 2]), sb("ra", [P, 7, TILES])
        xhat, y0, res = (sb(n, [P, TILES, D]) for n in ("xhat", "y0", "res"))
        hT, hTs = sb("hT", [P, KC, TOK]), sb("hTs", [P, 2, KC, TOK], F32R)
        u_sb = sb("u_sb", [RANK, TOK])
        zb, nz, ge = (sb(n, [P, TOK]) for n in ("zb", "nz", "ge"))
        glog, gcum, grel = (sb(n, [P, TOK]) for n in ("glog", "gcum", "grel"))
        eq, ek = sb("eq", [P, B, TS]), sb("ek", [P, B, TS])
        emid, dec = sb("emid", [P, B]), sb("dec", [P, B])
        qt, kt = sb("qt", [P, TOK]), sb("kt", [P, TOK])
        qx = sb("qx", [P, HQ, TOK])
        ktok = sb("ktok", [P, TILES, P])
        vtok, th, sg = (sb(n, [P, TILES, D]) for n in ("vtok", "th", "sg"))
        att = sb("att", [P, J, TILES * HQ, TS])
        state, smid, dstate = (sb(n, [P, B, HQ * DV]) for n in ("state", "smid", "dstate"))
        sx = sb("sx", [P, B, D])
        osq, onorm = (sb(n, [P, TILES * HEADS, DV]) for n in ("osq", "onorm"))
        oss, omean, orstd = (sb(n, [P, TILES * HEADS]) for n in ("oss", "omean", "orstd"))
        og = sb("og", [P, TILES, D])
        oTs = sb("oTs", [P, 2, KC, TOK], F32R)

        xmid, y1, sum2 = (sb(n, [P, TILES, D]) for n in ("xmid", "y1", "sum2"))
        st_f, mv_f, rf = sb("st_f", [P, TILES, 6]), sb("mv_f", [P, TILES, 2]), sb("rf", [P, 3, TILES])
        h2T, h2Ts = sb("h2T", [P, KC, TOK]), sb("h2Ts", [P, 2, KC, TOK], F32R)
        gT, gTs = sb("gT", [P, FB, TOK]), sb("gTs", [P, 2, FB, TOK], F32R)

        class Mix:
            def __init__(self, s):
                self.s = s
                self.x = sb(f"mx_in{s}", [P, TILES, D])
                self.st, self.mv = sb(f"st_{s}", [P, TILES, 6]), sb(f"mv_{s}", [P, TILES, 2])
                self.r = sb(f"r_{s}", [P, 3, TILES])
                self.y, self.yT = sb(f"ym{s}", [P, TILES, D]), sb(f"yT{s}", [P, 2, KC, TOK], F32R)
                self.lg, self.mx = sb(f"lg{s}", [P, TILES, E]), sb(f"mx{s}", [P, TILES, 8])
                self.ix, self.ixf = sb(f"ix{s}", [P, TILES, 8], U32), sb(f"ixf{s}", [P, TILES, TOPK])
                self.sub, self.p = sb(f"sub{s}", [P, TILES, E + TOPK]), sb(f"p{s}", [P, TILES, E + TOPK])
                self.sum, self.inv, self.den, self.den2, self.dinv, self.bias = (
                    sb(f"{n}{s}", [P, TILES]) for n in ("psum", "pinv", "den", "deneps", "dinv", "bias"))
                self.pk, self.wk, self.pw = (sb(f"{n}{s}", [P, TILES, TOPK]) for n in ("pk", "wk", "pw"))
                self.oh = sb(f"oh{s}", [P, TOPK, TILES, E])
                self.coef, self.acc = sb(f"coef{s}", [P, TILES, E]), sb(f"acc{s}", [P, TILES, D])

        m1, m2 = Mix(1), Mix(2)

        st_r, mv_r, rr = sb("st_r", [P, TILES, 6]), sb("mv_r", [P, TILES, 2]), sb("rr", [P, 3, TILES])
        yr, yrT = sb("yr", [P, TILES, D]), sb("yrT", [P, KC, TOK])
        x2b = sb("x2b", [P, TILES, D])
        hs = sb("hs", [P, B, TS])

        ps = ctx.enter_context(nc.psum_tensor("ps", [P, 8, 512], F32))
        RB, ALT = 5, 6

        def bank(slot):
            return ALT + SLOTS.index(slot) % 2

        def stg(base, n):
            return stage[:, base:base + n]

        first = [(cst[:], wts["consts"]), (lnw[:], wts["ln_w"]), (lnb[:], wts["ln_b"]),
                 (stg(W_Q, KC * P), wts["Wq"]), (stg(W_K, KC * P), wts["Wk"]), (stg(W_VG, KC * 2 * D), wts["Wvg"]),
                 (stg(W_O, KC * D), wts["Wo"]), (stg(W_1, KC * FF), wts["W1"]), (stg(W_2, FB * D), wts["W2"]),
                 (w1g[:], wts["gk_w1"]), (w2g[:], wts["gk_w2"]), (b2g[:], wts["gk_b2"]), (rmsw[:], wts["rms_w"]),
                 (b1[:], wts["b1"]), (b2[:], wts["b2"]), (rw[:], wts["router_w"]),
                 (bin_[:, :, 0:N], wts["Bin"]), (cT[:], wts["C"]), (woutT[:], wts["W_out"]), (bout[:], wts["b_out"])]
        WEIGHTS = 16 * len(first)

        def live(it, stage):
            return not isinstance(it, int) or 0 <= it - stage < ROUNDS

        def cnt(it, stage):
            n = it - stage + 1
            return min(max(n, 0), ROUNDS) if isinstance(it, int) else n

        def past(count):
            return max(count, 0) if isinstance(count, int) else count

        def value(eng, count):
            return past(count) if isinstance(count, int) else eng.to_reg(count)

        def rounds(eng, body, after_first=None):
            for it in range(PEELED):
                body(it)
                if it == 0 and after_first is not None:
                    after_first()
            with eng.Fori(PEELED, ROUNDS) as it:
                body(it)
            for it in range(ROUNDS, ROUNDS + SKEW):
                body(it)

        block = ctx.enter_context(nc.Block())

        @block.sync
        def _(sp):
            def load_x(n):
                for b in range(B):
                    i, q = b // BQ, b % BQ
                    sp.dma_start(xin[q * TS:(q + 1) * TS, i, :], x[b, bass.ds(n * TS, TS), :])\
                        .then_inc(sem("x_loaded"), 16)

            load_x(0)
            for dst, src in first:
                sp.dma_start(dst, src).then_inc(sem("weights"), 16)
            sp.wait_ge(sem("pads_zero"), 1)
            sp.dma_start(aT[0:N, 0:N], wts["A"]).then_inc(sem("a_loaded"), 16)
            sp.wait_ge(sem("wa_split"), 1)
            sp.dma_start(stage[:].rearrange("p (c e d) -> p c e d", c=KC, e=E), wts["experts"]).then_inc(sem("experts"), 16)

            def body(it, more):
                if live(it, ATTN) and more:
                    sp.wait_ge(sem("xhat"), cnt(it, ATTN))
                    sp.wait_ge(sem("y0"), cnt(it, ATTN))
                    sp.wait_ge(sem("res"), cnt(it, ATTN))
                    load_x(it + 1)
                if live(it, MIX2):
                    for i in range(TILES):
                        sp.wait_ge(sem("acc2"), past((cnt(it, MIX2) - 1) * TILES * E + (i + 1) * E))
                        for q in range(BQ):
                            sp.dma_start(out[i * BQ + q, bass.ds((it - MIX2) * TS, TS), :],
                                         m2.acc[q * TS:(q + 1) * TS, i, :]).then_inc(sem("stored"), 16)

            for it in range(PEELED):
                body(it, True)
            with sp.Fori(PEELED, ROUNDS - 1) as it:
                body(it, True)
            for it in range(ROUNDS - 1, ROUNDS + SKEW):
                body(it, False)
            sp.wait_ge(sem("stored"), 16 * B * ROUNDS)

        @block.gpsimd
        def _(pool):
            g = nc.gpsimd
            g.memset(mhalf[:], -0.5)
            g.memset(hs[:], 0.0)
            g.memset(state[:], 0.0)
            g.memset(sx[:], 0.0)
            g.memset(bin_[:, :, N:NP], 0.0)
            g.memset(aT[:], 0.0).then_inc(sem("pads_zero"), 1)
            pool.wait_ge(sem("pads_zero"), 1)
            pool.wait_ge(sem("weights"), WEIGHTS)
            g.tensor_scalar(rmsh[:], rmsw[:], 0.5, 1.0, ALU.mult, ALU.mult).then_inc(sem("rms_half"), 1)

            def rstd(mv, buf, name, count, shift=False):
                count = value(pool, count)
                pool.wait_ge(sem("weights"), WEIGHTS)
                pool.wait_ge(sem(f"mv_{name}"), count)
                g.tensor_scalar(buf[:, 0, :], mv[:, :, 1], EPS, 1.0, ALU.add, ALU.mult).then_inc(sem(f"var_{name}"), 1)
                pool.wait_ge(sem(f"var_{name}"), count)
                g.tensor_tensor(buf[:, 1, :], buf[:, 0, :], mhalf[:, 0:TILES], ALU.pow).then_inc(sem(f"rstd_{name}"), 1)
                if shift:
                    pool.wait_ge(sem(f"rstd_{name}"), count)
                    g.tensor_tensor(buf[:, 0, :], buf[:, 1, :], mv[:, :, 0], ALU.mult).then_inc(sem(f"mr_{name}"), 1)
                    count = value(pool, count)
                    pool.wait_ge(sem("weights"), WEIGHTS)
                    pool.wait_ge(sem(f"mr_{name}"), count)
                    g.tensor_scalar(buf[:, 2, :], buf[:, 0, :], -1.0, 1.0, ALU.mult, ALU.mult).then_inc(sem(f"shift_{name}"), 1)

            def body(it):
                cA, cB, cM, cR, cF = (cnt(it, k) for k in range(5))
                if live(it, ATTN):
                    rstd(mv_a, ra, "a", cA)
                    pool.wait_ge(sem("rstd_a"), cA)
                    g.tensor_tensor(ra[:, 2, :], ra[:, 1, :], ra[:, 1, :], ALU.mult).then_inc(sem("inner_step"), 1)
                    pool.wait_ge(sem("inner_step"), past((cA - 1) * 4 + 1))
                    g.tensor_tensor(ra[:, 3, :], ra[:, 2, :], mv_a[:, :, 1], ALU.mult).then_inc(sem("inner_step"), 1)
                    count = value(pool, (cA - 1) * 4 + 2)
                    pool.wait_ge(sem("weights"), WEIGHTS)
                    pool.wait_ge(sem("inner_step"), count)
                    g.tensor_scalar(ra[:, 4, :], ra[:, 3, :], EPS, 1.0, ALU.add, ALU.mult).then_inc(sem("inner_step"), 1)
                    pool.wait_ge(sem("inner_step"), past((cA - 1) * 4 + 3))
                    g.tensor_tensor(ra[:, 5, :], ra[:, 4, :], mhalf[:, 0:TILES], ALU.pow).then_inc(sem("inner_step"), 1)
                    pool.wait_ge(sem("inner_step"), past((cA - 1) * 4 + 4))
                    g.tensor_tensor(ra[:, 6, :], ra[:, 5, :], ra[:, 1, :], ALU.mult).then_inc(sem("rstd_inner"), 1)
                if live(it, MIX2):
                    rstd(m2.mv, m2.r, "m2", cF, True)
                if live(it, FFN):
                    rstd(mv_f, rf, "f", cB)
                    pool.wait_ge(sem("x1"), past(cB - 1))
                    pool.wait_ge(sem("xmid"), cB)
                    g.tensor_tensor(sum2[:], res[:], xmid[:], ALU.add).then_inc(sem("sum2"), 1)
                if live(it, ATTN):
                    pool.wait_ge(sem("x_loaded"), cA * 16 * B)
                    pool.wait_ge(sem("sum2"), past(cA - 1))
                    g.tensor_tensor(res[:], xin[:], b2[:].unsqueeze(1).broadcast_to([P, TILES, D]), ALU.add).then_inc(sem("res"), 1)
                    pool.wait_ge(sem("emid"), cA)
                    pool.wait_ge(sem("state"), past(cA - 1))
                    g.tensor_tensor(dec[:], emid[:], eq[:, :, TS - 1], ALU.mult).then_inc(sem("dec"), 1)
                    g.tensor_tensor(smid[:], state[:], emid[:].unsqueeze(2).broadcast_to([P, B, HQ * DV]), ALU.mult).then_inc(sem("smid"), 1)
                    pool.wait_ge(sem("smid"), cA)
                    pool.wait_ge(sem("o_ready"), past(cA - 1))
                    for j in range(J):
                        r = slice(j * 32, j * 32 + 32)
                        g.tensor_tensor(sx[r, :, j * HQ * DV:(j + 1) * HQ * DV], smid[r],
                                             blockmask[r].unsqueeze(1).broadcast_to([32, B, HQ * DV]), ALU.mult).then_inc(sem("sx"), 1)
                        pool.wait_ge(sem("sx"), past((cA - 1) * J + j + 1))
                    pool.wait_ge(sem("dec"), cA)
                    g.tensor_tensor(state[:], state[:], dec[:].unsqueeze(2).broadcast_to([P, B, HQ * DV]), ALU.mult).then_inc(sem("sdec"), 1)
                if live(it, MIX1):
                    rstd(mv_r, rr, "r", cM, True)
                if live(it, FFN):
                    rstd(m1.mv, m1.r, "m1", cB, True)
                if live(it, ATTN):
                    count = value(pool, cA)
                    pool.wait_ge(sem("weights"), WEIGHTS)
                    pool.wait_ge(sem("oss"), count)
                    g.tensor_scalar(omean[:], oss[:], 1.0 / DV, EPS, ALU.mult, ALU.add).then_inc(sem("omean"), 1)
                    pool.wait_ge(sem("omean"), cA)
                    g.tensor_tensor(orstd[:], omean[:], mhalf[:], ALU.pow).then_inc(sem("orstd"), 1)
                    pool.wait_ge(sem("dstate"), cA)
                    pool.wait_ge(sem("sdec"), cA)
                    g.tensor_tensor(state[:], state[:], dstate[:], ALU.add).then_inc(sem("state"), 1)
                if live(it, MIX1):
                    pool.wait_ge(sem("x3"), cR)
                    pool.wait_ge(sem("acc1"), past(cM * TILES * E))
                    g.tensor_tensor(x2b[:], m1.acc[:], bout[:].unsqueeze(1).broadcast_to([P, TILES, D]), ALU.add).then_inc(sem("x2b"), 1)

            rounds(pool, body)

        @block.scalar
        def _(act):
            a = nc.scalar
            a.preload_act_table_set("exp_and_others")
            act.wait_ge(sem("weights"), WEIGHTS)
            act.wait_ge(sem("wo_scaled"), 1)
            a.activation(wa[:, 0, :], stage[:, 0:W_END], ACT.Copy).then_inc(sem("wa_lead"), 1)
            a.activation(rws[:, 0], rw[:], ACT.Copy).then_inc(sem("rw_lead"), 1)
            act.wait_ge(sem("cw_psum"), 1)
            a.activation(cw[:], ps[0:N, 0, 0:D], ACT.Copy).then_inc(sem("cw"), 1)
            act.wait_ge(sem("pads_zero"), 1)

            def split_experts():
                act.wait_ge(sem("experts"), 16)
                a.activation(we[:, 0, :], stage[:], ACT.Copy).then_inc(sem("we_lead"), 1)

            def rnn(it, *ks):
                if live(it, RNN):
                    for k in ks:
                        act.wait_ge(sem("rnn_mm"), past((cnt(it, RNN) - 1) * TS + k + 1))
                        a.activation(hs[0:N, :, k], ps[0:N, RB, 0:TOK].rearrange("p (b t) -> p b t", t=TS)[:, :, k], ACT.Tanh).then_inc(sem("rnn_h"), 1)

            def normed(dst, src, mv, r, name, count):
                act.wait_ge(sem(f"shift_{name}"), count)
                for i in range(TILES):
                    ins = a.activation(dst[:, i, :], src[:, i, :], ACT.Identity, bias=r[:, 2, i:i + 1], scale=r[:, 1, i:i + 1])
                return ins

            def affine(dst, bank_, name):
                for c in range(KC):
                    ins = a.activation(dst[:, c, :], ps[:, bank_, c * TOK:(c + 1) * TOK], ACT.Identity,
                                       bias=lnb[:, c:c + 1], scale=lnw[:, c:c + 1])
                ins.then_inc(sem(name), 1)

            def start_acc(m, count):
                act.wait_ge(sem(f"bias{m.s}"), count)
                for i in range(TILES):
                    ins = a.activation(m.acc[:, i, :], m.x[:, i, :], ACT.Identity, bias=m.bias[:, i:i + 1])
                ins.then_inc(sem(f"acc_start{m.s}"), 1)

            def body(it):
                cA, cB, cM, cR, cF = (cnt(it, k) for k in range(5))
                if live(it, MIX1):
                    act.wait_ge(sem("x2b"), past(cM - 1))
                    act.wait_ge(sem("yr"), past(cM - 1))
                    start_acc(m1, cM)
                rnn(it, 0, 1)
                if live(it, MIX2):
                    normed(m2.y, m2.x, m2.mv, m2.r, "m2", cF).then_inc(sem("ym2"), 1)
                rnn(it, 2, 3)
                if live(it, ATTN):
                    act.wait_ge(sem("y0T"), cA)
                    affine(hT, 0, "hT")
                rnn(it, 4, 5)
                if live(it, MIX2):
                    act.wait_ge(sem("T2"), cF)
                    a.activation(m2.yT[:, 0], ps[:, bank("T2"), :].rearrange("p (c t) -> p c t", c=KC), ACT.Copy).then_inc(sem("y2lead"), 1)
                rnn(it, 6, 7)
                if live(it, FFN):
                    act.wait_ge(sem("y1T"), cB)
                    affine(h2T, 3, "h2T")
                if live(it, ATTN):
                    act.wait_ge(sem("u_psum"), cA)
                    a.activation(u_sb[:], ps[0:RANK, 2, 0:TOK], ACT.Copy).then_inc(sem("u"), 1)
                rnn(it, 8, 9)
                if live(it, ATTN):
                    act.wait_ge(sem("nz"), cA)
                    a.activation(ge[:], nz[:], ACT.Exp).then_inc(sem("ge"), 1)
                    a.preload_act_table_set("natural_log_exp_and_others")
                    act.wait_ge(sem("ge"), cA)
                    a.activation(ge[:], ge[:], ACT.Ln, bias=1.0).then_inc(sem("gl"), 1)
                    a.preload_act_table_set("exp_and_others")
                if live(it, MIX2):
                    act.wait_ge(sem("sub2"), cF)
                    a.activation(m2.p[:], m2.sub[:], ACT.Exp).then_inc(sem("p2"), 1)
                rnn(it, 10, 11)
                if live(it, ATTN):
                    act.wait_ge(sem("gclip"), cA)
                    act.wait_ge(sem("dstate"), past(cA - 1))
                    act.wait_ge(sem("dec"), past(cA - 1))
                    a.activation(eq[:], grel[:].rearrange("p (b t) -> p b t", t=TS), ACT.Exp, scale=1.0 / GATE_NORM).then_inc(sem("eq"), 1)
                    a.activation(ek[:], grel[:].rearrange("p (b t) -> p b t", t=TS), ACT.Exp, scale=-1.0 / GATE_NORM).then_inc(sem("ek"), 1)
                    act.wait_ge(sem("sx"), past((cA - 1) * J))
                    a.activation(emid[:], gcum[:].rearrange("p (b t) -> p b t", t=TS)[:, :, MID], ACT.Exp, scale=1.0 / GATE_NORM).then_inc(sem("emid"), 1)
                if live(it, FFN):
                    a.preload_act_table_set("gelu_and_others")
                    act.wait_ge(sem("gTs"), past(cB - 1))
                    for f in range(FB):
                        act.wait_ge(sem("ff1_psum"), past((cB - 1) * 2 + f // 2 + 1))
                        a.activation(gT[:, f, :], ps[:, (4, 3)[f // 2], (f % 2) * TOK:(f % 2 + 1) * TOK], ACT.Gelu,
                                          bias=b1[:, f:f + 1]).then_inc(sem("gT"), 1)
                    a.preload_act_table_set("exp_and_others")
                rnn(it, 12, 13)
                if live(it, ATTN):
                    for i in range(TILES):
                        act.wait_ge(sem("vg_psum"), past((cA - 1) * TILES + i + 1))
                        a.activation(th[:, i, :], ps[:, (0, 3)[i], D:2 * D], ACT.Tanh, scale=0.5).then_inc(sem("th"), 1)
                        a.activation(vtok[:, i, :], ps[:, (0, 3)[i], 0:D], ACT.Copy).then_inc(sem("vtok"), 1)
                        if i == 0:
                            rnn(it, 14, 15)
                else:
                    rnn(it, 14, 15)
                if live(it, MIX1):
                    normed(yr, m1.acc, mv_r, rr, "r", cM).then_inc(sem("yr"), 1)
                if live(it, MIX2):
                    act.wait_ge(sem("stored"), past((cF - 1) * 16 * B))
                    start_acc(m2, cF)
                rnn(it, 16, 17)
                if live(it, ATTN):
                    act.wait_ge(sem("ktT"), cA)
                    a.activation(ktok[:], ps[:, 2, 0:TOK].rearrange("p (i c) -> p i c", c=P), ACT.Copy).then_inc(sem("ktok"), 1)
                rnn(it, 18, 19)
                if live(it, MIX1):
                    act.wait_ge(sem("TR"), cM)
                    a.activation(yrT[:], ps[:, bank("TR"), :].rearrange("p (c t) -> p c t", c=KC), ACT.Copy).then_inc(sem("yrT"), 1)
                rnn(it, 20, 21)
                if live(it, FFN):
                    normed(m1.y, m1.x, m1.mv, m1.r, "m1", cB).then_inc(sem("ym1"), 1)
                rnn(it, 22, 23)
                if live(it, ATTN):
                    act.wait_ge(sem("o_ready"), cA)
                    a.activation(osq[:], ps[:, 0, :].rearrange("p (h v) -> p h v", v=DV), ACT.Square).then_inc(sem("osq"), 1)
                rnn(it, 24, 25)
                if live(it, FFN):
                    act.wait_ge(sem("T1"), cB)
                    a.activation(m1.yT[:, 0], ps[:, bank("T1"), :].rearrange("p (c t) -> p c t", c=KC), ACT.Copy).then_inc(sem("y1lead"), 1)
                rnn(it, 26, 27)
                if live(it, FFN):
                    act.wait_ge(sem("sub1"), cB)
                    a.activation(m1.p[:], m1.sub[:], ACT.Exp).then_inc(sem("p1"), 1)
                rnn(it, 28, 29)
                if live(it, ATTN):
                    act.wait_ge(sem("ogT"), cA)
                    a.activation(oTs[:, 0], ps[:, 1, :].rearrange("p (c t) -> p c t", c=KC), ACT.Copy).then_inc(sem("oT_lead"), 1)
                rnn(it, 30, 31)

            rounds(act, body, split_experts)

        @block.vector
        def _(dve):
            v = nc.vector
            dve.wait_ge(sem("weights"), WEIGHTS)
            dve.wait_ge(sem("rms_half"), 1)
            v.tensor_scalar(stg(W_O, KC * D), stg(W_O, KC * D), rmsh[:], None, ALU.mult).then_inc(sem("wo_scaled"), 1)
            dve.wait_ge(sem("wa_lead"), 1)
            v.tensor_tensor(wa[:, 1, :], stage[:, 0:W_END], wa[:, 0, :].bitcast(F32), ALU.subtract).then_inc(sem("wa_split"), 1)
            dve.wait_ge(sem("rw_lead"), 1)
            v.tensor_tensor(rws[:, 1], rw[:], rws[:, 0].bitcast(F32), ALU.subtract).then_inc(sem("rw_split"), 1)
            dve.wait_ge(sem("pads_zero"), 1)

            def split_experts():
                dve.wait_ge(sem("we_lead"), 1)
                v.tensor_tensor(we[:, 1, :], stage[:], we[:, 0, :].bitcast(F32), ALU.subtract).then_inc(sem("we_split"), 1)

            def stats(src, st, mv, name, count):
                for i in range(TILES):
                    ins = v.bn_stats(st[:, i, :], src[:, i, :])
                ins.then_inc(sem(f"st_{name}"), 1)
                count = value(dve, count)
                dve.wait_ge(sem("weights"), WEIGHTS)
                dve.wait_ge(sem(f"st_{name}"), count)
                for i in range(TILES):
                    ins = v.bn_aggr(mv[:, i, :], st[:, i, :])
                ins.then_inc(sem(f"mv_{name}"), 1)

            def normed(dst, src, mv, scale):
                for i in range(TILES):
                    ins = v.tensor_scalar(dst[:, i, :], src[:, i, :], mv[:, i, 0:1], scale[:, i:i + 1], ALU.subtract, ALU.mult)
                return ins

            def combine(it, m, k):
                stage_ = MIX1 if m is m1 else MIX2
                if not live(it, stage_):
                    return
                i, pr = k // PAIRS, k % PAIRS
                slot = f"G{k if m is m1 else GROUPS + k}"
                before = (cnt(it, stage_) - 1) * GROUPS + k
                if k == 0:
                    dve.wait_ge(sem(f"acc_start{m.s}"), cnt(it, stage_))
                dve.wait_ge(sem(f"moe{m.s}"), past(before + 1))
                for e in (2 * pr, 2 * pr + 1):
                    if e > 0:
                        dve.wait_ge(sem(f"acc{m.s}"), past(before * 2 + e % 2))
                    v.scalar_tensor_tensor(m.acc[:, i, :], ps[:, bank(slot), e % 2 * D:(e % 2 + 1) * D], m.coef[:, i, e:e + 1],
                                                m.acc[:, i, :], ALU.mult, ALU.add).then_inc(sem(f"acc{m.s}"), 1)

            def route(m, count):
                dve.wait_ge(sem(f"L{m.s}"), count)
                v.tensor_copy(m.lg[:], ps[:, bank(f"L{m.s}"), 0:TILES * E].rearrange("p (i e) -> p i e", e=E)).then_inc(sem(f"lg{m.s}"), 1)
                count = value(dve, count)
                dve.wait_ge(sem("weights"), WEIGHTS)
                dve.wait_ge(sem(f"lg{m.s}"), count)
                for i in range(TILES):
                    ins = v.max(m.mx[:, i, :], m.lg[:, i, :])
                ins.then_inc(sem(f"mx{m.s}"), 1)
                count = value(dve, count)
                dve.wait_ge(sem("weights"), WEIGHTS)
                dve.wait_ge(sem(f"mx{m.s}"), count)
                for i in range(TILES):
                    ins = v.max_index(m.ix[:, i, :], m.mx[:, i, :], m.lg[:, i, :])
                ins.then_inc(sem(f"ix{m.s}"), 1)
                top = m.mx[:, :, 0:1]
                v.tensor_tensor(m.sub[:, :, 0:E], m.lg[:], top.broadcast_to([P, TILES, E]), ALU.subtract)
                v.tensor_tensor(m.sub[:, :, E:E + TOPK], m.mx[:, :, 0:TOPK], top.broadcast_to([P, TILES, TOPK]), ALU.subtract).then_inc(sem(f"sub{m.s}"), 1)
                dve.wait_ge(sem(f"ix{m.s}"), count)
                v.tensor_copy(m.ixf[:], m.ix[:, :, 0:TOPK]).then_inc(sem(f"ixf{m.s}"), 1)

            def weigh(m, count):
                STEPS = 7
                dve.wait_ge(sem(f"p{m.s}"), count)
                v.tensor_reduce(m.sum[:], m.p[:, :, 0:E], AX.X, ALU.add).then_inc(sem(f"weigh{m.s}"), 1)
                dve.wait_ge(sem(f"weigh{m.s}"), past((count - 1) * STEPS + 1))
                v.reciprocal(m.inv[:], m.sum[:]).then_inc(sem(f"weigh{m.s}"), 1)
                dve.wait_ge(sem(f"weigh{m.s}"), past((count - 1) * STEPS + 2))
                v.tensor_tensor(m.pk[:], m.p[:, :, E:E + TOPK], m.inv[:].unsqueeze(2).broadcast_to([P, TILES, TOPK]), ALU.mult).then_inc(sem(f"weigh{m.s}"), 1)
                dve.wait_ge(sem(f"weigh{m.s}"), past((count - 1) * STEPS + 3))
                v.tensor_reduce(m.den[:], m.pk[:], AX.X, ALU.add).then_inc(sem(f"weigh{m.s}"), 1)
                dve.wait_ge(sem(f"weigh{m.s}"), past((count - 1) * STEPS + 4))
                v.tensor_scalar(m.den2[:], m.den[:], TOPK_EPS, None, ALU.add).then_inc(sem(f"weigh{m.s}"), 1)
                dve.wait_ge(sem(f"weigh{m.s}"), past((count - 1) * STEPS + 5))
                v.reciprocal(m.dinv[:], m.den2[:]).then_inc(sem(f"weigh{m.s}"), 1)
                dve.wait_ge(sem(f"weigh{m.s}"), past((count - 1) * STEPS + 6))
                v.tensor_tensor(m.wk[:], m.pk[:], m.dinv[:].unsqueeze(2).broadcast_to([P, TILES, TOPK]), ALU.mult).then_inc(sem(f"weigh{m.s}"), 1)
                dve.wait_ge(sem(f"ixf{m.s}"), count)
                dve.wait_ge(sem(f"weigh{m.s}"), past((count - 1) * STEPS + 7))
                v_pw = v.tensor_tensor(m.pw[:], m.pk[:], m.wk[:], ALU.mult)
                v_pw.then_inc(sem(f"pw{m.s}"), 1)
                for i in range(TILES):
                    for k in range(TOPK):
                        ins = v.tensor_scalar(m.oh[:, k, i, :], iota, m.ixf[:, i, k:k + 1], m.wk[:, i, k:k + 1], ALU.is_equal, ALU.mult)
                ins.then_inc(sem(f"oh{m.s}"), 1)
                dve.wait_ge(sem(f"pw{m.s}"), count)
                dve.wait_ge(sem(f"acc_start{m.s}"), past(count - 1))
                v.tensor_reduce(m.bias[:], m.pw[:], AX.X, ALU.add).then_inc(sem(f"bias{m.s}"), 1)
                dve.wait_ge(sem(f"oh{m.s}"), count)
                v.tensor_tensor(m.coef[:], m.oh[:, 0], m.oh[:, 1], ALU.add).then_inc(sem(f"coef{m.s}"), 1)

            def rest(parts, whole, name):
                v.tensor_tensor(parts[:, 1], whole, parts[:, 0].bitcast(F32), ALU.subtract).then_inc(sem(name), 1)

            def bt(ap):
                return ap.rearrange("p (b t) -> p b t", t=TS)

            def body(it):
                cA, cB, cM, cR, cF = (cnt(it, k) for k in range(5))
                if live(it, ATTN):
                    dve.wait_ge(sem("x_loaded"), cA * 16 * B)
                    stats(xin, st_a, mv_a, "a", cA)
                if live(it, MIX2):
                    dve.wait_ge(sem("x3"), cF)
                    stats(m2.x, m2.st, m2.mv, "m2", cF)
                if live(it, FFN):
                    dve.wait_ge(sem("attn_psum"), cB)
                    dve.wait_ge(sem("sum2"), past(cB - 1))
                    v.tensor_tensor(xmid[:].rearrange("p i d -> p (i d)"), ps[:, 4, :], xhat[:].rearrange("p i d -> p (i d)"), ALU.add).then_inc(sem("xmid"), 1)
                    dve.wait_ge(sem("xmid"), cB)
                    stats(xmid, st_f, mv_f, "f", cB)
                if live(it, MIX1):
                    dve.wait_ge(sem("coef1"), cM)
                combine(it, m1, 0)
                if live(it, ATTN):
                    dve.wait_ge(sem("mv_a"), cA)
                    dve.wait_ge(sem("rstd_inner"), cA)
                    normed(y0, xin, mv_a, ra[:, 6, :]).then_inc(sem("y0"), 1)
                combine(it, m1, 1)
                if live(it, FFN):
                    dve.wait_ge(sem("mv_f"), cB)
                    dve.wait_ge(sem("rstd_f"), cB)
                    normed(y1, xmid, mv_f, rf[:, 1, :]).then_inc(sem("y1"), 1)
                combine(it, m1, 2)
                if live(it, ATTN):
                    normed(xhat, xin, mv_a, ra[:, 1, :]).then_inc(sem("xhat"), 1)
                    dve.wait_ge(sem("hT"), cA)
                    v.tensor_copy(hTs[:, 0], hT[:]).then_inc(sem("hT_lead"), 1)
                    dve.wait_ge(sem("hT_lead"), cA)
                    rest(hTs, hT[:], "hTs")
                combine(it, m1, 3)
                if live(it, MIX2):
                    dve.wait_ge(sem("y2lead"), cF)
                    rest(m2.yT, ps[:, bank("T2"), :].rearrange("p (c t) -> p c t", c=KC), "yT2")
                if live(it, FFN):
                    dve.wait_ge(sem("h2T"), cB)
                    v.tensor_copy(h2Ts[:, 0], h2T[:]).then_inc(sem("h2T_lead"), 1)
                    dve.wait_ge(sem("h2T_lead"), cB)
                    rest(h2Ts, h2T[:], "h2Ts")
                combine(it, m1, 4)
                if live(it, ATTN):
                    dve.wait_ge(sem("z_psum"), cA)
                    v.tensor_scalar(zb[:], ps[:, 2, TOK:2 * TOK], b2g[:, 0:1], None, ALU.add).then_inc(sem("zb"), 1)
                    dve.wait_ge(sem("zb"), cA)
                    v.scalar_tensor_tensor(nz[:], zb[:], -1.0, zb[:], ALU.mult, ALU.min).then_inc(sem("nz"), 1)
                if live(it, MIX2):
                    route(m2, cF)
                combine(it, m1, 5)
                if live(it, ATTN):
                    dve.wait_ge(sem("gl"), cA)
                    v.scalar_tensor_tensor(glog[:], zb[:], 0.0, ge[:], ALU.min, ALU.subtract).then_inc(sem("glog"), 1)
                    dve.wait_ge(sem("glog"), cA)
                    v.tensor_tensor_scan(gcum[:], reset, glog[:], 0.0, ALU.mult, ALU.add).then_inc(sem("gcum"), 1)
                    dve.wait_ge(sem("gcum"), cA)
                    v.tensor_tensor(bt(grel[:]), bt(gcum[:]), bt(gcum[:])[:, :, MID:MID + 1].broadcast_to([P, B, TS]), ALU.subtract).then_inc(sem("grel"), 1)
                    dve.wait_ge(sem("grel"), cA)
                    v.tensor_scalar(grel[:], grel[:], -GMAX, GMAX, ALU.max, ALU.min).then_inc(sem("gclip"), 1)
                combine(it, m1, 6)
                if live(it, MIX2):
                    weigh(m2, cF)
                combine(it, m1, 7)
                if live(it, MIX1):
                    dve.wait_ge(sem("acc1"), past(cM * TILES * E))
                    stats(m1.acc, st_r, mv_r, "r", cM)
                if live(it, ATTN):
                    dve.wait_ge(sem("eq"), cA)
                    v.scalar_tensor_tensor(qt[:], ps[:, 1, 0:TOK], QSCALE, eq[:].rearrange("p b t -> p (b t)"), ALU.mult, ALU.mult).then_inc(sem("qt"), 1)
                    dve.wait_ge(sem("ek"), cA)
                    v.tensor_tensor(kt[:], ps[:, 1, TOK:2 * TOK], ek[:].rearrange("p b t -> p (b t)"), ALU.mult).then_inc(sem("kt"), 1)
                    dve.wait_ge(sem("qt"), cA)
                    for h in range(HQ):
                        ins = v.tensor_scalar(qx[:, h, :], qt[:], headmask[:, h:h + 1], None, ALU.mult)
                    ins.then_inc(sem("qx"), 1)
                if live(it, FFN):
                    dve.wait_ge(sem("gT"), cB * FB)
                    v.tensor_copy(gTs[:, 0], gT[:]).then_inc(sem("gT_lead"), 1)
                    dve.wait_ge(sem("gT_lead"), cB)
                    rest(gTs, gT[:], "gTs")
                if live(it, ATTN):
                    for i in range(TILES):
                        dve.wait_ge(sem("vtok"), past((cA - 1) * TILES + i + 1))
                        v.scalar_tensor_tensor(sg[:, i, :], th[:, i, :], 1.0, ps[:, (0, 3)[i], D:2 * D], ALU.add, ALU.mult).then_inc(sem("sg"), 1)
                if live(it, MIX2):
                    dve.wait_ge(sem("coef2"), cF)
                combine(it, m2, 0)
                if live(it, FFN):
                    dve.wait_ge(sem("ff2_psum"), cB)
                    dve.wait_ge(sem("sum2"), cB)
                    v.tensor_tensor(m1.x[:].rearrange("p i d -> p (i d)"), ps[:, 4, :],
                                         sum2[:].rearrange("p i d -> p (i d)"), ALU.add).then_inc(sem("x1"), 1)
                    dve.wait_ge(sem("x1"), cB)
                    stats(m1.x, m1.st, m1.mv, "m1", cB)
                combine(it, m2, 1)
                if live(it, ATTN):
                    dve.wait_ge(sem("scores"), cA)
                    v.tensor_tensor(att[:], ps[:, 1:5, 0:TILES * P].rearrange("p j (g t) -> p j g t", t=TS),
                                         causal.unsqueeze(1).unsqueeze(1).broadcast_to([P, J, TILES * HQ, TS]), ALU.mult).then_inc(sem("att"), 1)
                combine(it, m2, 2)
                combine(it, m2, 3)
                if live(it, ATTN):
                    dve.wait_ge(sem("osq"), cA)
                    v.tensor_reduce(oss[:], osq[:], AX.X, ALU.add).then_inc(sem("oss"), 1)
                    dve.wait_ge(sem("dS_psum"), cA)
                    dve.wait_ge(sem("state"), past(cA - 1))
                    v.tensor_tensor(dstate[:].rearrange("p (i q) c -> p i q c", q=BQ),
                                         ps[:, 1:5, TOK:TOK + TILES * HQ * DV].rearrange("p q (i c) -> p i q c", i=TILES),
                                         eq[:, :, TS - 1:TS].rearrange("p (i q) o -> p i q o", q=BQ).broadcast_to([P, TILES, BQ, HQ * DV]),
                                         ALU.mult).then_inc(sem("dstate"), 1)
                combine(it, m2, 4)
                if live(it, FFN):
                    dve.wait_ge(sem("y1lead"), cB)
                    rest(m1.yT, ps[:, bank("T1"), :].rearrange("p (c t) -> p c t", c=KC), "yT1")
                combine(it, m2, 5)
                if live(it, FFN):
                    route(m1, cB)
                if live(it, ATTN):
                    dve.wait_ge(sem("orstd"), cA)
                    v.tensor_tensor(onorm[:], ps[:, 0, :].rearrange("p (h v) -> p h v", v=DV),
                                         orstd[:].unsqueeze(2).broadcast_to([P, TILES * HEADS, DV]), ALU.mult).then_inc(sem("onorm"), 1)
                    dve.wait_ge(sem("onorm"), cA)
                    v.tensor_tensor(og[:].rearrange("p i d -> p (i d)"), onorm[:].rearrange("p h v -> p (h v)"),
                                         sg[:].rearrange("p i d -> p (i d)"), ALU.mult).then_inc(sem("og"), 1)
                combine(it, m2, 6)
                if live(it, FFN):
                    weigh(m1, cB)
                if live(it, ATTN):
                    dve.wait_ge(sem("oT_lead"), cA)
                    rest(oTs, ps[:, 1, :].rearrange("p (c t) -> p c t", c=KC), "oTs")
                combine(it, m2, 7)
                if live(it, RNN):
                    dve.wait_ge(sem("RO"), cR)
                    dve.wait_ge(sem("x2b"), cR)
                    dve.wait_ge(sem("acc_start2"), cF)
                    v.tensor_tensor(m2.x[:].rearrange("p i d -> p (i d)"), ps[:, bank("RO"), :],
                                         x2b[:].rearrange("p i d -> p (i d)"), ALU.add).then_inc(sem("x3"), 1)

            rounds(dve, body, split_experts)

        @block.tensor
        def _(pe):
            t = nc.tensor
            pe.wait_ge(sem("weights"), WEIGHTS)
            pe.wait_ge(sem("pads_zero"), 1)
            for c in range(KC):
                ins = t.matmul(ps[0:N, 0, 0:D], cT[:, c, :], woutT[:, c, :], start=(c == 0), stop=(c == KC - 1))
            ins.then_inc(sem("cw_psum"), 1)
            pe.wait_ge(sem("a_loaded"), 16)
            pe.wait_ge(sem("cw"), 1)
            pe.wait_ge(sem("wa_split"), 1)
            pe.wait_ge(sem("rw_split"), 1)

            def product(dst, left, right, chunks):
                n = 0
                for c in range(chunks):
                    for lp, rp in ((0, 0), (0, 1), (1, 0)):
                        n += 1
                        ins = t.matmul(dst, left(lp, c), right(rp, c), start=(n == 1), stop=(n == 3 * chunks))
                return ins

            def transposed(dst_bank, src, tiles=TILES):
                for c in range(KC):
                    for i in range(TILES):
                        ins = t.transpose(ps[:, dst_bank, c * TOK + i * P:c * TOK + (i + 1) * P], src[:, i, c * P:(c + 1) * P], ident)
                return ins

            def slot_free(it, slot):
                k, at = SLOTS.index(slot), it
                while not isinstance(at, int) or at >= 0:
                    k, at = (k - 2, at) if k >= 2 else (k - 2 + len(SLOTS), at - 1)
                    prev = SLOTS[k]
                    if prev[0] == "G":
                        g = int(prev[1:])
                        s, stage_, g = (1, MIX1, g) if g < GROUPS else (2, MIX2, g - GROUPS)
                        if live(at, stage_):
                            pe.wait_ge(sem(f"acc{s}"), past(((cnt(at, stage_) - 1) * GROUPS + g + 1) * 2))
                            return
                    else:
                        name, stage_ = {"T1": ("yT1", FFN), "T2": ("yT2", MIX2), "L1": ("lg1", FFN), "L2": ("lg2", MIX2),
                                        "TR": ("yrT", MIX1), "RO": ("x3", RNN)}[prev]
                        if live(at, stage_):
                            pe.wait_ge(sem(name), past(cnt(at, stage_)))
                            return

            def moe(it, g):
                m, stage_, k = (m1, MIX1, g) if g < GROUPS else (m2, MIX2, g - GROUPS)
                i, pr = k // PAIRS, k % PAIRS
                if live(it, stage_):
                    slot_free(it, f"G{g}")
                    for c in range(KC):
                        for n, (lp, rp) in enumerate(((0, 0), (0, 1), (1, 0))):
                            o = c * E * D + pr * 2 * D
                            ins = t.matmul(ps[:, bank(f"G{g}"), :], m.yT[:, lp, c, i * P:(i + 1) * P], we[:, rp, o:o + 2 * D],
                                           start=(c == 0 and n == 0), stop=(c == KC - 1 and n == 2))
                        if c == KC - 1:
                            ins.then_inc(sem(f"moe{m.s}"), 1)
                        rnn(it, 2 * g + c)
                else:
                    rnn(it, 2 * g)
                    rnn(it, 2 * g + 1)

            def rnn(it, k):
                if live(it, RNN):
                    count = value(pe, (cnt(it, RNN) - 1) * TS + k)
                    pe.wait_ge(sem("weights"), WEIGHTS)
                    pe.wait_ge(sem("rnn_h"), count)
                    t.matmul(ps[0:NP, RB, 0:TOK].rearrange("p (b t) -> p b t", t=TS)[:, :, k], aT[:],
                                  hs[:, :, (k - 1) % TS], start=False, stop=True, skip_group_check=True).then_inc(sem("rnn_mm"), 1)

            def logits(it, m, stage_):
                slot_free(it, f"L{m.s}")
                pe.wait_ge(sem(f"yT{m.s}"), cnt(it, stage_))
                for i in range(TILES):
                    ins = product(ps[:, bank(f"L{m.s}"), i * E:(i + 1) * E], lambda p, c: m.yT[:, p, c, i * P:(i + 1) * P],
                                  lambda p, c: rws[:, p, c, :], KC)
                ins.then_inc(sem(f"L{m.s}"), 1)

            def body(it):
                cA, cB, cM, cR, cF = (cnt(it, k) for k in range(5))
                if live(it, FFN):
                    pe.wait_ge(sem("oTs"), cB)
                    pe.wait_ge(sem("dstate"), cB)
                    for i in range(TILES):
                        ins = product(ps[:, 4, i * D:(i + 1) * D], lambda p, c: oTs[:, p, c, i * P:(i + 1) * P],
                                      lambda p, c: wcols(W_O, p, c, D, 0, D), KC)
                    ins.then_inc(sem("attn_psum"), 1)
                if live(it, MIX1):
                    pe.wait_ge(sem("yT1"), cM)
                    pe.wait_ge(sem("we_split"), 1)
                moe(it, 0)
                moe(it, 1)
                if live(it, ATTN):
                    pe.wait_ge(sem("y0"), cA)
                    pe.wait_ge(sem("onorm"), past(cA - 1))
                    transposed(0, y0).then_inc(sem("y0T"), 1)
                moe(it, 2)
                if live(it, MIX2):
                    slot_free(it, "T2")
                    pe.wait_ge(sem("ym2"), cF)
                    transposed(bank("T2"), m2.y).then_inc(sem("T2"), 1)
                moe(it, 3)
                if live(it, FFN):
                    pe.wait_ge(sem("y1"), cB)
                    transposed(3, y1).then_inc(sem("y1T"), 1)
                if live(it, ATTN):
                    pe.wait_ge(sem("hT"), cA)
                    pe.wait_ge(sem("dstate"), past(cA - 1))
                    for c in range(KC):
                        ins = t.matmul(ps[0:RANK, 2, 0:TOK], w1g[:, c, :], hT[:, c, :], start=(c == 0), stop=(c == KC - 1))
                    ins.then_inc(sem("u_psum"), 1)
                    pe.wait_ge(sem("hTs"), cA)
                    pe.wait_ge(sem("oTs"), past(cA - 1))
                    for w, col in ((W_Q, 0), (W_K, TOK)):
                        ins = product(ps[:, 1, col:col + TOK], lambda p, c: wcols(w, p, c, P, 0, P), lambda p, c: hTs[:, p, c, :], KC)
                    ins.then_inc(sem("qk_psum"), 1)
                moe(it, 4)
                if live(it, ATTN):
                    pe.wait_ge(sem("u"), cA)
                    t.matmul(ps[:, 2, TOK:2 * TOK], w2g[:], u_sb[:], start=True, stop=True).then_inc(sem("z_psum"), 1)
                if live(it, MIX2):
                    logits(it, m2, MIX2)
                moe(it, 5)
                if live(it, FFN):
                    pe.wait_ge(sem("h2Ts"), cB)
                    pe.wait_ge(sem("xmid"), cB)
                    for f in range(FB):
                        ins = product(ps[:, (4, 3)[f // 2], (f % 2) * TOK:(f % 2 + 1) * TOK],
                                      lambda p, c: wcols(W_1, p, c, FF, f * P, P), lambda p, c: h2Ts[:, p, c, :], KC)
                        if f % 2:
                            ins.then_inc(sem("ff1_psum"), 1)
                moe(it, 6)

                def values(i):
                    product(ps[:, (0, 3)[i], :], lambda p, c: hTs[:, p, c, i * P:(i + 1) * P],
                                 lambda p, c: wcols(W_VG, p, c, 2 * D, 0, 2 * D), KC).then_inc(sem("vg_psum"), 1)

                if live(it, ATTN):
                    values(0)
                moe(it, 7)
                if live(it, FFN):
                    pe.wait_ge(sem("gT"), cB * FB)
                if live(it, ATTN):
                    values(1)
                moe(it, 8)
                if live(it, FFN):
                    pe.wait_ge(sem("gTs"), cB)
                    for i in range(TILES):
                        ins = product(ps[:, 4, i * D:(i + 1) * D], lambda p, f: gTs[:, p, f, i * P:(i + 1) * P],
                                      lambda p, f: wcols(W_2, p, f, D, 0, D), FB)
                    ins.then_inc(sem("ff2_psum"), 1)
                if live(it, ATTN):
                    pe.wait_ge(sem("zb"), cA)
                    pe.wait_ge(sem("kt"), cA)
                    for i in range(TILES):
                        ins = t.transpose(ps[:, 2, i * P:(i + 1) * P], kt[:, i * P:(i + 1) * P], ident)
                    ins.then_inc(sem("ktT"), 1)
                moe(it, 9)
                if live(it, MIX1):
                    slot_free(it, "TR")
                    pe.wait_ge(sem("yr"), cM)
                    transposed(bank("TR"), yr).then_inc(sem("TR"), 1)
                if live(it, ATTN):
                    count = value(pe, cA * TILES)
                    pe.wait_ge(sem("weights"), WEIGHTS)
                    pe.wait_ge(sem("sg"), count)
                    pe.wait_ge(sem("qx"), cA)
                    pe.wait_ge(sem("ktok"), cA)
                    pe.wait_ge(sem("x1"), cB)
                    for b in range(B):
                        i, q = b // BQ, b % BQ
                        for j in range(J):
                            r = slice(32 * j, 32 * j + 32)
                            ins = t.matmul(ps[q * 32:q * 32 + 32, 1 + j, i * P:(i + 1) * P], kt[r, b * TS:(b + 1) * TS],
                                           qx[r, :, b * TS:(b + 1) * TS], start=True, stop=True)
                    ins.then_inc(sem("scores"), 1)
                moe(it, 10)
                if live(it, ATTN):
                    pe.wait_ge(sem("att"), cA)
                    pe.wait_ge(sem("sx"), cA * J)
                    for b in range(B):
                        i, q = b // BQ, b % BQ
                        r = slice(q * 32, q * 32 + 32)
                        t.matmul(ps[r, 0, i * D:(i + 1) * D], qt[:, b * TS:(b + 1) * TS], sx[:, b, :],
                                 start=True, stop=False, skip_group_check=True)
                        for h in range(HEADS):
                            ins = t.matmul(ps[r, 0, i * D + h * DV:i * D + (h + 1) * DV], att[r, h // HQ, i * HQ + h % HQ, :],
                                           vtok[r, i, h * DV:(h + 1) * DV], start=False, stop=(h == HEADS - 1), skip_group_check=True)
                    ins.then_inc(sem("o_ready"), 1)
                moe(it, 11)
                if live(it, ATTN):
                    for b in range(B):
                        i, q = b // BQ, b % BQ
                        r = slice(q * 32, q * 32 + 32)
                        for j in range(J):
                            ins = t.matmul(ps[32 * j:32 * j + 32, 1 + q, TOK + i * HQ * DV:TOK + (i + 1) * HQ * DV],
                                           ktok[r, i, 32 * j:32 * j + 32], vtok[r, i, j * HQ * DV:(j + 1) * HQ * DV], start=True, stop=True)
                    ins.then_inc(sem("dS_psum"), 1)
                moe(it, 12)
                if live(it, FFN):
                    slot_free(it, "T1")
                    pe.wait_ge(sem("ym1"), cB)
                    transposed(bank("T1"), m1.y).then_inc(sem("T1"), 1)
                moe(it, 13)
                if live(it, FFN):
                    logits(it, m1, FFN)
                moe(it, 14)
                if live(it, ATTN):
                    pe.wait_ge(sem("og"), cA)
                    pe.wait_ge(sem("dstate"), cA)
                    transposed(1, og).then_inc(sem("ogT"), 1)
                moe(it, 15)
                if live(it, RNN):
                    slot_free(it, "RO")
                    pe.wait_ge(sem("rnn_h"), past(cR * TS))
                    pe.wait_ge(sem("x3"), past(cR - 1))
                    for i in range(TILES):
                        ins = t.matmul(ps[:, bank("RO"), i * D:(i + 1) * D],
                                       hs[0:N, i * BQ:(i + 1) * BQ, :].rearrange("p b t -> p (b t)"), cw[:], start=True, stop=True)
                    ins.then_inc(sem("RO"), 1)
                if live(it, MIX1):
                    pe.wait_ge(sem("yrT"), cM)
                    for c in range(KC):
                        t.matmul(ps[0:NP, RB, 0:TOK], bin_[:, c, :], yrT[:, c, :], start=(c == 0), stop=(c == KC - 1), skip_group_check=True)

            rounds(pe, body)


def kernel(**inputs):
    import numpy as _np
    import concourse.bacc as _bacc
    from concourse import mybir as _mybir
    from concourse.bass_utils import run_bass_kernel_spmd as _run

    a = {k.replace("L0_attn_a_", "").replace("L0_attn_b_", "rnn_").replace("L0_ffn_", ""): _np.asarray(v) for k, v in inputs.items()}

    def rows(w):
        return _np.ascontiguousarray(w.reshape(-1, P, w.shape[1]).transpose(1, 0, 2))

    def cols(b):
        return _np.ascontiguousarray(b.reshape(-1, P).T)

    def everywhere(b):
        return _np.ascontiguousarray(_np.broadcast_to(b, (P, b.shape[0])))

    arrays = {
        "x": a["x"], "consts": constants(), "ln_w": cols(a["ln_w"]), "ln_b": cols(a["ln_b"]),
        "Wq": rows(a["Wq"]), "Wk": rows(a["Wk"]), "Wvg": rows(_np.concatenate([a["Wv"], a["Wg"]], axis=1)),
        "gk_w1": rows(a["gk_w1"]), "gk_w2": a["gk_w2"], "gk_b2": cols(a["gk_b2"]),
        "rms_w": _np.ascontiguousarray(_np.broadcast_to(a["rms_w"], (P // DV, DV)).reshape(P, 1)),
        "Wo": rows(a["Wo"]), "W1": rows(a["W1"]), "b1": cols(a["b1"]), "W2": rows(a["W2"]), "b2": everywhere(a["b2"]),
        "router_w": rows(a["router_w"].T),
        "experts": _np.ascontiguousarray(a["expert_weights"].reshape(E, KC, P, D).transpose(2, 1, 0, 3)),
        "Bin": rows(a["rnn_B"]), "A": _np.ascontiguousarray(a["rnn_A"].T), "C": rows(a["rnn_C"].T),
        "W_out": rows(a["rnn_W_out"].T), "b_out": everywhere(a["rnn_b_out"]),
    }
    nc = _bacc.Bacc("TRN2", target_bir_lowering=False, num_devices=1)
    arrays = {f"in_{k}": _np.ascontiguousarray(v) for k, v in arrays.items()}
    drams = {k[3:]: nc.dram_tensor(k, v.shape, _mybir.dt.from_np(v.dtype), kind="ExternalInput").ap() for k, v in arrays.items()}
    out = nc.dram_tensor("out", (B, T, D), _mybir.dt.float32, kind="ExternalOutput").ap()
    x = drams.pop("x")
    build(nc, x, drams, out)
    r = _run(nc, [arrays], core_ids=[0])
    return r.results[0]["out"]
```

```python
from contextlib import ExitStack

import concourse.bass as bass
import numpy as np
from concourse import mybir

F32 = mybir.dt.float32
F32R = mybir.dt.float32r
U32 = mybir.dt.uint32
ALU = mybir.AluOpType
ACT = mybir.ActivationFunctionType
AX = mybir.AxisListType

P = 128
B, T, D = 8, 1024, 256
TS = 32
ROUNDS = T // TS
TOK = B * TS
TILES = TOK // P
BQ = B // TILES
KC = D // P
HEADS, DK, DV = 16, 8, 16
HQ = 4
J = HEADS // HQ
RANK = 16
GATE_NORM = 16.0
FF = 512
FB = FF // P
E, TOPK = 8, 2
N = 16
NP = 32
EPS = 1e-5
TOPK_EPS = 1e-6
QSCALE = float(DK) ** -0.5
MID = TS // 2 - 1
GMAX = 80.0 * GATE_NORM
PAIRS = E // 2
GROUPS = TILES * PAIRS
VECTOR_GROUPS = TILES * (PAIRS - 1)
STAGES = 8
SKEW = STAGES - 1
EXPERTS_SPLIT = 2
PEELED = STAGES

BANK = {"Y0": 3, "Z": 2, "QK": 6, "VG0": 2, "VG1": 0, "KT": 6, "SD": 0, "O": 4, "OG": 7, "WO": 7, "Y1": 6, "F1A": 3,
    "F1B": 6, "F2": 6, "T1": 2, "L1": 1, "G1_0": 7, "G1_1": 2, "G1_2": 3, "G1_3": 1, "G1_4": 7, "G1_5": 6, "G1_6": 0,
    "G1_7": 7, "TR": 3, "RB": 5, "RO": 4, "T2": 0, "L2": 0, "G2_0": 2, "G2_1": 1, "G2_2": 7, "G2_3": 3, "G2_4": 2, "G2_5": 1,
    "G2_6": 0, "G2_7": 6}
BANK_ORDER = {
    0: [("G1_6", 5, ("acc1", 2 * VECTOR_GROUPS, 10)), ("VG1", 2, 'sg1'), ("G2_6", 7, ("acc2", 2 * VECTOR_GROUPS, 10)),
            ("SD", 2, 'dstate'), ("T2", 6, 'yT2'), ("L2", 6, 'sub2')],
    1: [("G2_1", 7, ("acc2", 2 * VECTOR_GROUPS, 2)), ("G2_5", 7, ("acc2", 2 * VECTOR_GROUPS, 8)), ("SD", 2, 'dstate'),
            ("L1", 4, 'sub1'), ("G1_3", 4, ("acc1", 2 * VECTOR_GROUPS, 6))],
    2: [("Z", 2, 'zb'), ("G2_0", 7, ("scaled2", TILES, 1)), ("G2_4", 7, ("scaled2", TILES, 2)), ("VG0", 2, 'sg0'),
            ("SD", 2, 'dstate'), ("T1", 4, 'yT1'), ("G1_1", 4, ("acc1", 2 * VECTOR_GROUPS, 2))],
    3: [("F1A", 4, 'gT'), ("G2_3", 7, ("acc2", 2 * VECTOR_GROUPS, 6)), ("TR", 5, 'yrT'), ("SD", 2, 'dstate'),
            ("Y0", 1, 'hT'), ("G1_2", 4, ("acc1", 2 * VECTOR_GROUPS, 4))],
    4: [("RO", 6, 'mv_m2'), ("O", 2, 'onorm')],
    5: [("RB", 5, ("rnn_h", TS, TS))],
    6: [("G1_5", 5, ("acc1", 2 * VECTOR_GROUPS, 8)), ("F1B", 4, 'gT'), ("QK", 2, 'qx'), ("KT", 2, 'ktok'),
            ("F2", 4, 'mv_m1'), ("G2_7", 7, ("acc2", 2 * VECTOR_GROUPS, 12)), ("Y1", 3, 'h2T')],
    7: [("G1_7", 5, ("acc1", 2 * VECTOR_GROUPS, 12)), ("G2_2", 7, ("acc2", 2 * VECTOR_GROUPS, 4)), ("OG", 3, 'oTs'),
            ("WO", 3, 'mv_f'), ("G1_0", 4, ("scaled1", TILES, 1)), ("G1_4", 4, ("scaled1", TILES, 2))],
}

C_ID, C_CAUSAL, C_HEAD, C_BLOCK, C_IOTA, C_RESET = 0, 128, 160, 164, 228, 236
C_END = C_RESET + TOK


def constants():
    c = np.zeros((P, C_END), np.float32)
    p = np.arange(P)
    c[:, C_ID:C_ID + P] = np.eye(P)
    c[:, C_CAUSAL:C_CAUSAL + TS] = (p[:, None] % TS) <= np.arange(TS)[None]
    c[:, C_HEAD:C_HEAD + HQ] = (p[:, None] // DK % HQ) == np.arange(HQ)[None]
    c[:, C_BLOCK:C_BLOCK + HQ * DV] = (p[:, None] // DK % HQ) == (np.arange(HQ * DV)[None] // DV)
    c[:, C_IOTA:C_IOTA + E] = np.arange(E)[None]
    c[:, C_RESET:] = (np.arange(TOK)[None] % TS) != 0
    return c


def build(nc, x, wts, out):
    ctx = ExitStack()
    with ctx:
        def sb(name, shape, dt=F32):
            return ctx.enter_context(nc.sbuf_tensor(name, shape, dt))

        sems = {}

        def sem(name):
            if name not in sems:
                sems[name] = ctx.enter_context(nc.semaphore(name))
            return sems[name]

        cst = sb("cst", [P, C_END])
        ident = cst[:, C_ID:C_ID + P]
        causal = cst[:, C_CAUSAL:C_CAUSAL + TS]
        headmask = cst[:, C_HEAD:C_HEAD + HQ]
        blockmask = cst[:, C_BLOCK:C_BLOCK + HQ * DV]
        iota = cst[:, C_IOTA:C_IOTA + E]
        reset = cst[:, C_RESET:C_RESET + TOK]
        stage = sb("stage", [P, KC * E * D])
        lnw, lnb = sb("lnw", [P, KC]), sb("lnb", [P, KC])
        w1T, w2g, b2g = sb("w1T", [RANK, D]), sb("w2g", [RANK, P]), sb("b2g", [P, 1])
        rmsw, rmsh = sb("rmsw", [P, 1]), sb("rmsh", [P, 1])
        b1, b2, bout = sb("b1", [P, FB]), sb("b2", [P, D]), sb("bout", [P, D])
        bin_, aT = sb("bin_", [P, KC, NP]), sb("aT", [P, NP])
        cT, woutT, cw = sb("cT", [P, KC, N]), sb("woutT", [P, KC, D]), sb("cw", [N, D])
        mhalf, one = sb("mhalf", [P, TILES * HEADS]), sb("one", [P, TILES])
        W_Q, W_K, W_VG, W_O, W_1, W_2 = (0, KC * P, 2 * KC * P, 2 * KC * P + KC * 2 * D,
                                         2 * KC * P + KC * 3 * D, 2 * KC * P + KC * 3 * D + KC * FF)
        W_END = W_2 + FB * D
        wa = sb("wa", [P, 2, W_END], F32R)
        we = sb("we", [P, 2, KC * E * D], F32R)
        wz = sb("wz", [P, 2, KC, P], F32R)
        rw, rws = sb("rw", [P, KC, E]), sb("rws", [P, KC, 2, E], F32R)

        def wcols(base, part, c, width, at, n):
            o = base + c * width + at
            return wa[:, part, o:o + n]

        xin = sb("xin", [P, TILES, D])
        st_a, mv_a, ra = sb("st_a", [P, TILES, 6]), sb("mv_a", [P, TILES, 2]), sb("ra", [P, 7, TILES])
        y0, nrm = sb("y0", [P, TILES, D]), sb("nrm", [P, 2, TILES])
        hT, hTs = sb("hT", [P, KC, TOK]), sb("hTs", [P, 2, KC, TOK], F32R)
        zb, nz, ge, glog, gcum, grel = (sb(n, [P, TOK]) for n in ("zb", "nz", "ge", "glog", "gcum", "grel"))
        eq, ek = sb("eq", [P, B, TS]), sb("ek", [P, B, TS])
        emid, dec = sb("emid", [P, B]), sb("dec", [P, B])
        qt, kt = sb("qt", [P, TOK]), sb("kt", [P, TOK])
        qx = sb("qx", [P, HQ, TOK])
        ktok = sb("ktok", [P, TILES, P])
        vtok, th, sg = (sb(n, [P, TILES, D]) for n in ("vtok", "th", "sg"))
        att = sb("att", [P, J, TILES * HQ, TS])
        state, smid, dstate = (sb(n, [P, B, HQ * DV]) for n in ("state", "smid", "dstate"))
        sx = sb("sx", [P, B, D])
        osq, onorm = (sb(n, [P, TILES * HEADS, DV]) for n in ("osq", "onorm"))
        oss, omean, orstd = (sb(n, [P, TILES * HEADS]) for n in ("oss", "omean", "orstd"))
        og = sb("og", [P, TILES, D])
        oTs = sb("oTs", [P, 2, KC, TOK], F32R)

        xag, xhat, res, xmid, y1 = (sb(n, [P, TILES, D]) for n in ("xag", "xhat", "res", "xmid", "y1"))
        st_f, mv_f, rf = sb("st_f", [P, TILES, 6]), sb("mv_f", [P, TILES, 2]), sb("rf", [P, 3, TILES])
        h2T, h2Ts = sb("h2T", [P, KC, TOK]), sb("h2Ts", [P, 2, KC, TOK], F32R)
        gT, gTs = sb("gT", [P, FB, TOK]), sb("gTs", [P, 2, FB, TOK], F32R)

        used = [0]

        def staged(shape):
            n = int(np.prod(shape))
            used[0] += n
            names = " ".join(f"x{k}" for k in range(len(shape)))
            return stage[:, used[0] - n:used[0]].rearrange(f"p ({names}) -> p {names}", **{f"x{k}": d for k, d in enumerate(shape)})

        class Mix:
            def __init__(self, s):
                self.s = s
                buffer = (lambda name, shape: staged(shape)) if s == 2 else (lambda name, shape: sb(f"{name}{s}", [P] + shape))
                self.x, self.y, self.acc = (buffer(n, [TILES, D]) for n in ("mx_in", "ym", "acc"))
                self.part = buffer("part", [TILES, 2, D])
                self.yT = sb(f"yT{s}", [P, 2, KC, TOK], F32R)
                self.st, self.mv = sb(f"st_{s}", [P, TILES, 6]), sb(f"mv_{s}", [P, TILES, 2])
                self.r = sb(f"r_{s}", [P, 3, TILES])
                self.lg, self.mx = sb(f"lg{s}", [P, TILES, E]), sb(f"mx{s}", [P, TILES, 8])
                self.ix, self.ixf = sb(f"ix{s}", [P, TILES, 8], U32), sb(f"ixf{s}", [P, TILES, TOPK])
                self.sub, self.p = sb(f"sub{s}", [P, TILES, E + TOPK]), sb(f"p{s}", [P, TILES, E + TOPK])
                self.two, self.dens, self.invs = sb(f"two{s}", [P, TILES]), sb(f"dens{s}", [P, 2, TILES]), sb(f"invs{s}", [P, 2, TILES])
                self.bias, self.half = sb(f"bias{s}", [P, TILES]), sb(f"half{s}", [P, TILES, E])
                self.pk, self.wk, self.pw = (sb(f"{n}{s}", [P, TILES, TOPK]) for n in ("pk", "wk", "pw"))
                self.oh = sb(f"oh{s}", [P, TOPK, TILES, E])
                self.coef = sb(f"coef{s}", [P, TILES, E])

        m1, m2 = Mix(1), Mix(2)

        st_r, mv_r, rr = sb("st_r", [P, TILES, 6]), sb("mv_r", [P, TILES, 2]), sb("rr", [P, 3, TILES])
        yr, yrT = staged([TILES, D]), sb("yrT", [P, KC, TOK])
        x2b = staged([TILES, D])
        hs = sb("hs", [P, B, TS])

        ps = ctx.enter_context(nc.psum_tensor("ps", [P, 8, 512], F32))
        SD = BANK["SD"]

        def by_chunk(use):
            return ps[:, BANK[use], :].rearrange("p (c t) -> p c t", c=KC)

        def bt(ap):
            return ap.rearrange("p (b t) -> p b t", t=TS)

        def stg(base, n):
            return stage[:, base:base + n]

        first = [(cst[:], wts["consts"]), (lnw[:], wts["ln_w"]), (lnb[:], wts["ln_b"]),
                 (stg(W_Q, KC * P), wts["Wq"]), (stg(W_K, KC * P), wts["Wk"]), (stg(W_VG, KC * 2 * D), wts["Wvg"]),
                 (stg(W_O, KC * D), wts["Wo"]), (stg(W_1, KC * FF), wts["W1"]), (stg(W_2, FB * D), wts["W2"]),
                 (w1T[:], wts["gk_w1T"]), (w2g[:], wts["gk_w2"]), (b2g[:], wts["gk_b2"]), (rmsw[:], wts["rms_w"]),
                 (b1[:], wts["b1"]), (b2[:], wts["b2"]), (rw[:], wts["router_w"]),
                 (bin_[:, :, 0:N], wts["Bin"]), (cT[:], wts["C"]), (woutT[:], wts["W_out"]), (bout[:], wts["b_out"])]
        WEIGHTS = 16 * len(first)

        def live(it, stage):
            return not isinstance(it, int) or 0 <= it - stage < ROUNDS

        def cnt(it, stage):
            n = it - stage + 1
            return min(max(n, 0), ROUNDS) if isinstance(it, int) else n

        def readers(it, use):
            found = {}
            for order in BANK_ORDER.values():
                uses = [u for u, _, _ in order]
                if use in uses:
                    k, at, back = uses.index(use), it, 0
                    while not isinstance(at, int) or at >= 0:
                        k, at, back = (k - 1, at, back) if k else (len(order) - 1, at - 1, back + 1)
                        _, stage_, reader = order[k]
                        if live(at, stage_):
                            name, count = done_by(reader, cnt(at, stage_))
                            age = (back + stage_, -reader[2] if isinstance(reader, tuple) else 0)
                            if name not in found or age < found[name][0]:
                                found[name] = age, count
                            break
            return [(name, count) for name, (_, count) in found.items()]

        def done_by(reader, n):
            if isinstance(reader, tuple):
                name, of_round, k = reader
                return name, (n - 1) * of_round + k
            return reader, n

        def past(count):
            return max(count, 0) if isinstance(count, int) else count

        def value(eng, count):
            return past(count) if isinstance(count, int) else eng.to_reg(count)

        def rounds(eng, body, split=None):
            for it in range(PEELED):
                body(it)
                if it == EXPERTS_SPLIT and split is not None:
                    split()
            with eng.Fori(PEELED, ROUNDS) as it:
                body(it)
            for it in range(ROUNDS, ROUNDS + SKEW):
                body(it)

        block = ctx.enter_context(nc.Block())

        @block.sync
        def _(sp):
            def load_x(dst, n, name):
                for b in range(B):
                    i, q = b // BQ, b % BQ
                    sp.dma_start(dst[q * TS:(q + 1) * TS, i, :], x[b, bass.ds(n * TS, TS), :]).then_inc(sem(name), 16)

            def store(n):
                for b in range(B):
                    i, q = b // BQ, b % BQ
                    sp.dma_start(out[b, bass.ds(n * TS, TS), :], m2.acc[q * TS:(q + 1) * TS, i, :]).then_inc(sem("stored"), 16)

            for dst, src in first[1::2]:
                sp.dma_start(dst, src).then_inc(sem("weights"), 16)
            sp.wait_ge(sem("pads_zero"), 1)
            sp.dma_start(aT[0:N, 0:N], wts["A"]).then_inc(sem("a_loaded"), 16)
            sp.wait_ge(sem("wa_split"), 1)
            sp.dma_start(stage[:].rearrange("p (c e d) -> p c e d", c=KC, e=E), wts["experts"]).then_inc(sem("experts"), 16)

            def body(it):
                c0, c1, c7 = (cnt(it, k) for k in (0, 1, 7))
                if live(it, 0):
                    sp.wait_ge(sem("y0"), past(c0 - 1))
                    load_x(xin, it, "x_loaded")
                if live(it, 7):
                    sp.wait_ge(sem("acc2"), c7 * VECTOR_GROUPS * 2)
                    store(it - 7)
                if live(it, 1):
                    sp.wait_ge(sem("res"), past(c1 - 1))
                    load_x(xag, it - 1, "x_again")

            rounds(sp, body)
            sp.wait_ge(sem("stored"), 16 * B * ROUNDS)

        @block.gpsimd
        def _(pool):
            g = nc.gpsimd
            g.memset(mhalf[:], -0.5)
            g.memset(hs[:], 0.0)
            g.memset(state[:], 0.0)
            g.memset(sx[:], 0.0)
            g.memset(one[:], 1.0)
            g.memset(bin_[:, :, N:NP], 0.0)
            g.memset(aT[:], 0.0).then_inc(sem("pads_zero"), 1)
            pool.wait_ge(sem("pads_zero"), 1)
            pool.wait_ge(sem("weights"), WEIGHTS)
            g.tensor_scalar(rmsh[:], rmsw[:], 0.5, 1.0, ALU.mult, ALU.mult).then_inc(sem("rms_half"), 1)

            def rstd(mv, buf, name, count, shift=False):
                g.tensor_scalar(buf[:, 0, :], mv[:, :, 1], EPS, 1.0, ALU.add, ALU.mult).then_inc(sem(f"var_{name}"), 1)
                pool.wait_ge(sem(f"var_{name}"), count)
                g.tensor_tensor(buf[:, 1, :], buf[:, 0, :], mhalf[:, 0:TILES], ALU.pow).then_inc(sem(f"rstd_{name}"), 1)
                if shift:
                    pool.wait_ge(sem(f"rstd_{name}"), count)
                    g.tensor_tensor(buf[:, 0, :], buf[:, 1, :], mv[:, :, 0], ALU.mult).then_inc(sem(f"mr_{name}"), 1)
                    target = value(pool, count)
                    pool.wait_ge(sem("weights"), WEIGHTS)
                    pool.wait_ge(sem(f"mr_{name}"), target)
                    g.tensor_scalar(buf[:, 2, :], buf[:, 0, :], -1.0, 1.0, ALU.mult, ALU.mult).then_inc(sem(f"shift_{name}"), 1)

            def inner_rstd(count):
                STEPS = 4
                rstd(mv_a, ra, "a", count)
                pool.wait_ge(sem("rstd_a"), count)
                g.tensor_tensor(ra[:, 2, :], ra[:, 1, :], ra[:, 1, :], ALU.mult).then_inc(sem("inner_step"), 1)
                pool.wait_ge(sem("inner_step"), past((count - 1) * STEPS + 1))
                g.tensor_tensor(ra[:, 3, :], ra[:, 2, :], mv_a[:, :, 1], ALU.mult).then_inc(sem("inner_step"), 1)
                target = value(pool, (count - 1) * STEPS + 2)
                pool.wait_ge(sem("weights"), WEIGHTS)
                pool.wait_ge(sem("inner_step"), target)
                g.tensor_scalar(ra[:, 4, :], ra[:, 3, :], EPS, 1.0, ALU.add, ALU.mult).then_inc(sem("inner_step"), 1)
                pool.wait_ge(sem("inner_step"), past((count - 1) * STEPS + 3))
                g.tensor_tensor(ra[:, 5, :], ra[:, 4, :], mhalf[:, 0:TILES], ALU.pow).then_inc(sem("inner_step"), 1)
                pool.wait_ge(sem("inner_step"), past(count * STEPS))
                g.tensor_tensor(ra[:, 6, :], ra[:, 5, :], ra[:, 1, :], ALU.mult).then_inc(sem("rstd_inner"), 1)

            def start_acc(m, i, count):
                g.tensor_tensor(m.part[:, i, 0, :], m.part[:, i, 0, :], m.part[:, i, 1, :], ALU.add).then_inc(sem(f"part{m.s}"), 1)
                pool.wait_ge(sem(f"part{m.s}"), past((count - 1) * TILES + i + 1))
                g.tensor_tensor(m.acc[:, i, :], m.x[:, i, :], m.part[:, i, 0, :], ALU.add).then_inc(sem(f"acc_start{m.s}"), 1)

            def body(it):
                c1, c2, c3, c4, c5, c6, c7 = (cnt(it, k) for k in (1, 2, 3, 4, 5, 6, 7))
                if live(it, 4):
                    target = value(pool, c4)
                    pool.wait_ge(sem("weights"), WEIGHTS)
                    pool.wait_ge(sem("mv_f"), target)
                    rstd(mv_f, rf, "f", c4)
                if live(it, 5):
                    pool.wait_ge(sem("scaled1"), past((c5 - 1) * TILES + 1))
                    start_acc(m1, 0, c5)
                    pool.wait_ge(sem("scaled1"), c5 * TILES)
                    start_acc(m1, 1, c5)
                if live(it, 3):
                    target = value(pool, c3)
                    pool.wait_ge(sem("weights"), WEIGHTS)
                    pool.wait_ge(sem("oss"), target)
                    g.tensor_scalar(omean[:], oss[:], 1.0 / DV, EPS, ALU.mult, ALU.add).then_inc(sem("omean"), 1)
                    pool.wait_ge(sem("omean"), c3)
                    g.tensor_tensor(orstd[:], omean[:], mhalf[:], ALU.pow).then_inc(sem("orstd"), 1)
                if live(it, 7):
                    pool.wait_ge(sem("scaled2"), past((c7 - 1) * TILES + 1))
                    pool.wait_ge(sem("stored"), past((c7 - 1) * 16 * B))
                    start_acc(m2, 0, c7)
                if live(it, 5):
                    target = value(pool, c5)
                    pool.wait_ge(sem("weights"), WEIGHTS)
                    pool.wait_ge(sem("mv_r"), target)
                    rstd(mv_r, rr, "r", c5, True)
                if live(it, 4):
                    g.tensor_tensor(res[:], res[:], xmid[:], ALU.add)
                if live(it, 2):
                    pool.wait_ge(sem("rstd_inner"), c2)
                    pool.wait_ge(sem("xhat"), past(c2 - 1))
                    g.tensor_tensor(nrm[:, 1, :], ra[:, 1, :], one[:, 0:TILES], ALU.mult)
                    g.tensor_tensor(nrm[:, 0, :], mv_a[:, :, 0], one[:, 0:TILES], ALU.mult).then_inc(sem("nrm"), 1)
                if live(it, 3):
                    pool.wait_ge(sem("onorm"), c3)
                    g.tensor_tensor(og[:].rearrange("p i d -> p (i d)"), onorm[:].rearrange("p h v -> p (h v)"),
                                         sg[:].rearrange("p i d -> p (i d)"), ALU.mult).then_inc(sem("og"), 1)
                    g.tensor_tensor(state[:], state[:], dstate[:], ALU.add).then_inc(sem("state"), 1)
                if live(it, 7):
                    pool.wait_ge(sem("scaled2"), c7 * TILES)
                    start_acc(m2, 1, c7)
                if live(it, 2):
                    pool.wait_ge(sem("emid"), c2)
                    pool.wait_ge(sem("state"), past(c2 - 1))
                    g.tensor_tensor(smid[:], state[:], emid[:].unsqueeze(2).broadcast_to([P, B, HQ * DV]), ALU.mult).then_inc(sem("smid"), 1)
                    pool.wait_ge(sem("smid"), c2)
                    for j in range(J):
                        r = slice(j * 32, j * 32 + 32)
                        g.tensor_tensor(sx[r, :, j * HQ * DV:(j + 1) * HQ * DV], smid[r],
                                             blockmask[r].unsqueeze(1).broadcast_to([32, B, HQ * DV]), ALU.mult).then_inc(sem("sx"), 1)
                        pool.wait_ge(sem("sx"), past((c2 - 1) * J + j + 1))
                    g.tensor_tensor(dec[:], emid[:], eq[:, :, TS - 1], ALU.mult).then_inc(sem("dec"), 1)
                if live(it, 1):
                    target = value(pool, c1)
                    pool.wait_ge(sem("weights"), WEIGHTS)
                    pool.wait_ge(sem("mv_a"), target)
                    inner_rstd(c1)
                if live(it, 6):
                    target = value(pool, c6)
                    pool.wait_ge(sem("weights"), WEIGHTS)
                    pool.wait_ge(sem("mv_m2"), target)
                    rstd(m2.mv, m2.r, "m2", c6, True)
                if live(it, 5):
                    g.tensor_tensor(x2b[:], m1.acc[:], bout[:].unsqueeze(1).broadcast_to([P, TILES, D]), ALU.add)
                if live(it, 4):
                    target = value(pool, c4)
                    pool.wait_ge(sem("weights"), WEIGHTS)
                    pool.wait_ge(sem("mv_m1"), target)
                    rstd(m1.mv, m1.r, "m1", c4, True)
                if live(it, 2):
                    pool.wait_ge(sem("dec"), c2)
                    g.tensor_tensor(state[:], state[:], dec[:].unsqueeze(2).broadcast_to([P, B, HQ * DV]), ALU.mult)
                if live(it, 3):
                    g.tensor_tensor(res[:], xag[:], b2[:].unsqueeze(1).broadcast_to([P, TILES, D]), ALU.add).then_inc(sem("res"), 1)

            rounds(pool, body)

        @block.scalar
        def _(act):
            a = nc.scalar
            for dst, src in first[0::2]:
                act.dma_start(dst, src).then_inc(sem("weights"), 16)
            a.preload_act_table_set("exp_and_others")
            act.wait_ge(sem("weights"), WEIGHTS)
            act.wait_ge(sem("wo_scaled"), 1)
            a.activation(wa[:, 0, :], stage[:, 0:W_END], ACT.Copy).then_inc(sem("wa_lead"), 1)
            a.activation(rws[:, :, 0, :], rw[:], ACT.Copy).then_inc(sem("rw_lead"), 1)
            act.wait_ge(sem("cw_psum"), 1)
            a.activation(cw[:], ps[0:N, 0, 0:D], ACT.Copy).then_inc(sem("cw"), 1)
            act.wait_ge(sem("wz_psum"), 1)
            a.activation(wz[:, 0], ps[:, 1, 0:D].rearrange("p (c n) -> p c n", c=KC), ACT.Copy).then_inc(sem("wz_lead"), 1)
            act.wait_ge(sem("pads_zero"), 1)

            def split_experts():
                act.wait_ge(sem("experts"), 16)
                a.activation(we[:, 0, :], stage[:], ACT.Copy).then_inc(sem("we_lead"), 1)

            def state_of(k):
                return a.activation(hs[0:N, :, k], bt(ps[0:N, BANK["RB"], 0:TOK])[:, :, k], ACT.Tanh)

            def normed(dst, src, r):
                for i in range(TILES):
                    ins = a.activation(dst[:, i, :], src[:, i, :], ACT.Identity, bias=r[:, 2, i:i + 1], scale=r[:, 1, i:i + 1])
                return ins

            def affine(dst, bank, name):
                for c in range(KC):
                    ins = a.activation(dst[:, c, :], ps[:, bank, c * TOK:(c + 1) * TOK], ACT.Identity,
                                       bias=lnb[:, c:c + 1], scale=lnw[:, c:c + 1])
                ins.then_inc(sem(name), 1)

            def scaled(m, i, bank):
                a.activation(m.part[:, i, 0, :], ps[:, bank, 0:D], ACT.Identity, bias=m.bias[:, i:i + 1], scale=m.coef[:, i, 0:1])
                return a.activation(m.part[:, i, 1, :], ps[:, bank, D:2 * D], ACT.Identity, scale=m.coef[:, i, 1:2])

            def body(it):
                c1, c2, c3, c4, c5, c6, c7 = (cnt(it, k) for k in (1, 2, 3, 4, 5, 6, 7))
                if live(it, 6):
                    act.wait_ge(sem("rnn_mm"), past((c6 - 1) * TS + 15))
                    state_of(14).then_inc(sem("rnn_h"), 1)
                    act.wait_ge(sem("rnn_mm"), past((c6 - 1) * TS + 16))
                    state_of(15).then_inc(sem("rnn_h"), 1)
                if live(it, 4):
                    act.wait_ge(sem("Y1"), c4)
                    affine(h2T, BANK["Y1"], "h2T")
                if live(it, 6):
                    act.wait_ge(sem("rnn_mm"), past((c6 - 1) * TS + 17))
                    state_of(16).then_inc(sem("rnn_h"), 1)
                if live(it, 4):
                    act.wait_ge(sem("h2T"), c4)
                    a.activation(h2Ts[:, 0], h2T[:], ACT.Copy).then_inc(sem("h2T0"), 1)
                if live(it, 7):
                    act.wait_ge(sem("sub2"), c7)
                    a.activation(m2.p[:], m2.sub[:], ACT.Exp).then_inc(sem("p2"), 1)
                if live(it, 6):
                    act.wait_ge(sem("rnn_mm"), past((c6 - 1) * TS + 18))
                    state_of(17).then_inc(sem("rnn_h"), 1)
                if live(it, 5):
                    act.wait_ge(sem("moe1"), past((c5 - 1) * GROUPS + 5))
                    scaled(m1, 1, BANK["G1_4"]).then_inc(sem("scaled1"), 1)
                if live(it, 3):
                    act.wait_ge(sem("O11"), c3)
                    a.activation(osq[:], ps[:, BANK["O"], :].rearrange("p (h v) -> p h v", v=DV), ACT.Square).then_inc(sem("osq"), 1)
                if live(it, 6):
                    act.wait_ge(sem("rnn_mm"), past((c6 - 1) * TS + 19))
                    state_of(18).then_inc(sem("rnn_h"), 1)
                    act.wait_ge(sem("rnn_mm"), past((c6 - 1) * TS + 20))
                    state_of(19).then_inc(sem("rnn_h"), 1)
                if live(it, 2):
                    act.wait_ge(sem("Z"), c2)
                    a.activation(zb[:], ps[:, BANK["Z"], 0:TOK], ACT.Identity, bias=b2g[:, 0:1]).then_inc(sem("zb"), 1)
                if live(it, 6):
                    act.wait_ge(sem("rnn_mm"), past((c6 - 1) * TS + 21))
                    state_of(20).then_inc(sem("rnn_h"), 1)
                    act.wait_ge(sem("rnn_mm"), past((c6 - 1) * TS + 22))
                    state_of(21).then_inc(sem("rnn_h"), 1)
                if live(it, 2):
                    act.wait_ge(sem("nz"), c2)
                    a.activation(ge[:], nz[:], ACT.Exp).then_inc(sem("ge"), 1)
                    a.preload_act_table_set("natural_log_exp_and_others")
                    act.wait_ge(sem("ge"), c2)
                    a.activation(ge[:], ge[:], ACT.Ln, bias=1.0).then_inc(sem("gl"), 1)
                    a.preload_act_table_set("exp_and_others")
                if live(it, 6):
                    act.wait_ge(sem("rnn_mm"), past((c6 - 1) * TS + 23))
                    state_of(22).then_inc(sem("rnn_h"), 1)
                if live(it, 7):
                    act.wait_ge(sem("coef2"), c7)
                    act.wait_ge(sem("moe2"), past((c7 - 1) * GROUPS + 1))
                    scaled(m2, 0, BANK["G2_0"]).then_inc(sem("scaled2"), 1)
                if live(it, 6):
                    act.wait_ge(sem("rnn_mm"), past((c6 - 1) * TS + 24))
                    state_of(23).then_inc(sem("rnn_h"), 1)
                if live(it, 4):
                    a.preload_act_table_set("gelu_and_others")
                    act.wait_ge(sem("F1B"), c4)
                    for f in range(FB):
                        ins = a.activation(gT[:, f, :], ps[:, BANK["F1A" if f < 2 else "F1B"], f % 2 * TOK:(f % 2 + 1) * TOK], ACT.Gelu, bias=b1[:, f:f + 1])
                    ins.then_inc(sem("gT"), 1)
                    a.preload_act_table_set("exp_and_others")
                if live(it, 6):
                    act.wait_ge(sem("rnn_mm"), past((c6 - 1) * TS + 25))
                    state_of(24).then_inc(sem("rnn_h"), 1)
                if live(it, 2):
                    act.wait_ge(sem("VG1"), c2)
                    a.activation(th[:, 1, :], ps[:, BANK["VG1"], D:2 * D], ACT.Tanh, scale=0.5)
                    a.activation(vtok[:, 1, :], ps[:, BANK["VG1"], 0:D], ACT.Copy).then_inc(sem("vt1"), 1)
                if live(it, 6):
                    act.wait_ge(sem("rnn_mm"), past((c6 - 1) * TS + 26))
                    state_of(25).then_inc(sem("rnn_h"), 1)
                if live(it, 5):
                    act.wait_ge(sem("shift_r"), c5)
                    normed(yr, m1.acc, rr).then_inc(sem("yr"), 1)
                if live(it, 6):
                    act.wait_ge(sem("rnn_mm"), past((c6 - 1) * TS + 27))
                    state_of(26).then_inc(sem("rnn_h"), 1)
                if live(it, 7):
                    act.wait_ge(sem("moe2"), past((c7 - 1) * GROUPS + 5))
                    scaled(m2, 1, BANK["G2_4"]).then_inc(sem("scaled2"), 1)
                if live(it, 6):
                    act.wait_ge(sem("rnn_mm"), past((c6 - 1) * TS + 28))
                    state_of(27).then_inc(sem("rnn_h"), 1)
                    act.wait_ge(sem("rnn_mm"), past((c6 - 1) * TS + 29))
                    state_of(28).then_inc(sem("rnn_h"), 1)
                    act.wait_ge(sem("rnn_mm"), past((c6 - 1) * TS + 30))
                    state_of(29).then_inc(sem("rnn_h"), 1)
                if live(it, 2):
                    act.wait_ge(sem("gclip"), c2)
                    a.activation(eq[:], bt(grel[:]), ACT.Exp, scale=1.0 / GATE_NORM)
                    a.activation(ek[:], bt(grel[:]), ACT.Exp, scale=-1.0 / GATE_NORM)
                    a.activation(emid[:], bt(gcum[:])[:, :, MID], ACT.Exp, scale=1.0 / GATE_NORM).then_inc(sem("emid"), 1)
                if live(it, 5):
                    act.wait_ge(sem("TR"), c5)
                    a.activation(yrT[:], by_chunk("TR"), ACT.Copy).then_inc(sem("yrT"), 1)
                if live(it, 6):
                    act.wait_ge(sem("rnn_mm"), past((c6 - 1) * TS + 31))
                    state_of(30).then_inc(sem("rnn_h"), 1)
                    act.wait_ge(sem("rnn_mm"), c6 * TS)
                    state_of(31).then_inc(sem("rnn_h"), 1)
                if live(it, 3):
                    act.wait_ge(sem("OG"), c3)
                    a.activation(oTs[:, 0], by_chunk("OG"), ACT.Copy).then_inc(sem("oT_lead"), 1)
                if live(it, 4):
                    a.activation(gTs[:, 0], gT[:], ACT.Copy).then_inc(sem("gT0"), 1)
                if live(it, 2):
                    act.wait_ge(sem("VG0"), c2)
                    a.activation(th[:, 0, :], ps[:, BANK["VG0"], D:2 * D], ACT.Tanh, scale=0.5)
                    a.activation(vtok[:, 0, :], ps[:, BANK["VG0"], 0:D], ACT.Copy).then_inc(sem("vt0"), 1)
                if live(it, 5):
                    act.wait_ge(sem("rnn_mm"), past((c5 - 1) * TS + 1))
                    state_of(0).then_inc(sem("rnn_h"), 1)
                if live(it, 2):
                    act.wait_ge(sem("KT"), c2)
                    a.activation(ktok[:], ps[:, BANK["KT"], 0:TOK].rearrange("p (i c) -> p i c", c=P), ACT.Copy).then_inc(sem("ktok"), 1)
                if live(it, 5):
                    act.wait_ge(sem("rnn_mm"), past((c5 - 1) * TS + 2))
                    state_of(1).then_inc(sem("rnn_h"), 1)
                    act.wait_ge(sem("rnn_mm"), past((c5 - 1) * TS + 3))
                    state_of(2).then_inc(sem("rnn_h"), 1)
                    act.wait_ge(sem("rnn_mm"), past((c5 - 1) * TS + 4))
                    state_of(3).then_inc(sem("rnn_h"), 1)
                    act.wait_ge(sem("rnn_mm"), past((c5 - 1) * TS + 5))
                    state_of(4).then_inc(sem("rnn_h"), 1)
                    act.wait_ge(sem("rnn_mm"), past((c5 - 1) * TS + 6))
                    state_of(5).then_inc(sem("rnn_h"), 1)
                if live(it, 6):
                    act.wait_ge(sem("shift_m2"), c6)
                    normed(m2.y, m2.x, m2.r).then_inc(sem("ym2"), 1)
                if live(it, 4):
                    act.wait_ge(sem("shift_m1"), c4)
                    normed(m1.y, m1.x, m1.r).then_inc(sem("ym1"), 1)
                if live(it, 5):
                    act.wait_ge(sem("rnn_mm"), past((c5 - 1) * TS + 7))
                    state_of(6).then_inc(sem("rnn_h"), 1)
                    act.wait_ge(sem("rnn_mm"), past((c5 - 1) * TS + 8))
                    state_of(7).then_inc(sem("rnn_h"), 1)
                if live(it, 4):
                    act.wait_ge(sem("T1"), c4)
                    a.activation(m1.yT[:, 0], by_chunk("T1"), ACT.Copy).then_inc(sem("lead1"), 1)
                if live(it, 5):
                    act.wait_ge(sem("rnn_mm"), past((c5 - 1) * TS + 9))
                    state_of(8).then_inc(sem("rnn_h"), 1)
                if live(it, 1):
                    act.wait_ge(sem("Y0"), c1)
                    affine(hT, BANK["Y0"], "hT")
                    act.wait_ge(sem("hT"), c1)
                    a.activation(hTs[:, 0], hT[:], ACT.Copy).then_inc(sem("hT0"), 1)
                if live(it, 6):
                    act.wait_ge(sem("T2"), c6)
                    a.activation(m2.yT[:, 0], by_chunk("T2"), ACT.Copy).then_inc(sem("lead2"), 1)
                if live(it, 5):
                    act.wait_ge(sem("rnn_mm"), past((c5 - 1) * TS + 10))
                    state_of(9).then_inc(sem("rnn_h"), 1)
                    act.wait_ge(sem("rnn_mm"), past((c5 - 1) * TS + 11))
                    state_of(10).then_inc(sem("rnn_h"), 1)
                    act.wait_ge(sem("rnn_mm"), past((c5 - 1) * TS + 12))
                    state_of(11).then_inc(sem("rnn_h"), 1)
                if live(it, 4):
                    act.wait_ge(sem("sub1"), c4)
                    a.activation(m1.p[:], m1.sub[:], ACT.Exp).then_inc(sem("p1"), 1)
                if live(it, 5):
                    act.wait_ge(sem("rnn_mm"), past((c5 - 1) * TS + 13))
                    state_of(12).then_inc(sem("rnn_h"), 1)
                    act.wait_ge(sem("rnn_mm"), past((c5 - 1) * TS + 14))
                    state_of(13).then_inc(sem("rnn_h"), 1)
                if live(it, 4):
                    act.wait_ge(sem("coef1"), c4)
                    scaled(m1, 0, BANK["G1_0"]).then_inc(sem("scaled1"), 1)

            rounds(act, body, split_experts)

        @block.vector
        def _(dve):
            v = nc.vector
            dve.wait_ge(sem("weights"), WEIGHTS)
            dve.wait_ge(sem("rms_half"), 1)
            v.tensor_scalar(stg(W_O, KC * D), stg(W_O, KC * D), rmsh[:], None, ALU.mult).then_inc(sem("wo_scaled"), 1)
            dve.wait_ge(sem("wa_lead"), 1)
            v.tensor_tensor(wa[:, 1, :], stage[:, 0:W_END], wa[:, 0, :].bitcast(F32), ALU.subtract).then_inc(sem("wa_split"), 1)
            dve.wait_ge(sem("rw_lead"), 1)
            v.tensor_tensor(rws[:, :, 1, :], rw[:], rws[:, :, 0, :].bitcast(F32), ALU.subtract).then_inc(sem("rw_split"), 1)
            dve.wait_ge(sem("wz_lead"), 1)
            v.tensor_tensor(wz[:, 1], ps[:, 1, 0:D].rearrange("p (c n) -> p c n", c=KC), wz[:, 0].bitcast(F32), ALU.subtract).then_inc(sem("wz_split"), 1)
            dve.wait_ge(sem("pads_zero"), 1)

            def split_experts():
                dve.wait_ge(sem("we_lead"), 1)
                v.tensor_tensor(we[:, 1, :], stage[:], we[:, 0, :].bitcast(F32), ALU.subtract).then_inc(sem("we_split"), 1)

            def stats(src, st, mv, name, count):
                for i in range(TILES):
                    ins = v.bn_stats(st[:, i, :], src[:, i, :])
                ins.then_inc(sem(f"st_{name}"), 1)
                target = value(dve, count)
                dve.wait_ge(sem("weights"), WEIGHTS)
                dve.wait_ge(sem(f"st_{name}"), target)
                for i in range(TILES):
                    ins = v.bn_aggr(mv[:, i, :], st[:, i, :])
                ins.then_inc(sem(f"mv_{name}"), 1)

            def normed(dst, src, mean, scale):
                for i in range(TILES):
                    ins = v.tensor_scalar(dst[:, i, :], src[:, i, :], mean[:, i:i + 1], scale[:, i:i + 1], ALU.subtract, ALU.mult)
                return ins

            def combine(m, k, bank, count):
                i, pr = k // PAIRS, k % PAIRS
                before = (count - 1) * VECTOR_GROUPS + i * (PAIRS - 1) + pr - 1
                for e in (2 * pr, 2 * pr + 1):
                    if e > 2:
                        dve.wait_ge(sem(f"acc{m.s}"), past(before * 2 + e % 2))
                    v.scalar_tensor_tensor(m.acc[:, i, :], ps[:, bank, e % 2 * D:(e % 2 + 1) * D], m.coef[:, i, e:e + 1],
                                                m.acc[:, i, :], ALU.mult, ALU.add).then_inc(sem(f"acc{m.s}"), 1)

            def route(m, bank, count):
                halves = ps[:, bank, 0:TILES * 2 * E].rearrange("p (i s e) -> p i s e", s=2, e=E)
                v.tensor_copy(m.half[:], halves[:, :, 0, :]).then_inc(sem(f"half{m.s}"), 1)
                dve.wait_ge(sem(f"half{m.s}"), count)
                v.tensor_tensor(m.lg[:], m.half[:], halves[:, :, 1, :], ALU.add).then_inc(sem(f"lg{m.s}"), 1)
                target = value(dve, count)
                dve.wait_ge(sem("weights"), WEIGHTS)
                dve.wait_ge(sem(f"lg{m.s}"), target)
                for i in range(TILES):
                    ins = v.max(m.mx[:, i, :], m.lg[:, i, :])
                ins.then_inc(sem(f"mx{m.s}"), 1)
                target = value(dve, count)
                dve.wait_ge(sem("weights"), WEIGHTS)
                dve.wait_ge(sem(f"mx{m.s}"), target)
                for i in range(TILES):
                    ins = v.max_index(m.ix[:, i, :], m.mx[:, i, :], m.lg[:, i, :])
                top = m.mx[:, :, 0:1]
                v.tensor_tensor(m.sub[:, :, 0:E], m.lg[:], top.broadcast_to([P, TILES, E]), ALU.subtract)
                v.tensor_tensor(m.sub[:, :, E:E + TOPK], m.mx[:, :, 0:TOPK], top.broadcast_to([P, TILES, TOPK]), ALU.subtract).then_inc(sem(f"sub{m.s}"), 1)

            def weigh(m, count):
                STEPS = 5
                v.tensor_reduce(m.dens[:, 0, :], m.p[:, :, 0:E], AX.X, ALU.add).then_inc(sem(f"weigh{m.s}"), 1)
                v.tensor_tensor(m.two[:], m.p[:, :, E], m.p[:, :, E + 1], ALU.add)
                dve.wait_ge(sem(f"weigh{m.s}"), past((count - 1) * STEPS + 1))
                v.tensor_copy(m.ixf[:], m.ix[:, :, 0:TOPK]).then_inc(sem(f"weigh{m.s}"), 1)
                dve.wait_ge(sem(f"weigh{m.s}"), past((count - 1) * STEPS + 2))
                v.scalar_tensor_tensor(m.dens[:, 1, :], m.dens[:, 0, :], TOPK_EPS, m.two[:], ALU.mult, ALU.add).then_inc(sem(f"weigh{m.s}"), 1)
                dve.wait_ge(sem(f"weigh{m.s}"), past((count - 1) * STEPS + 3))
                v.reciprocal(m.invs[:], m.dens[:]).then_inc(sem(f"weigh{m.s}"), 1)
                dve.wait_ge(sem(f"weigh{m.s}"), past((count - 1) * STEPS + 4))
                v.tensor_tensor(m.pk[:], m.p[:, :, E:E + TOPK], m.invs[:, 0, :].unsqueeze(2).broadcast_to([P, TILES, TOPK]), ALU.mult)
                v.tensor_tensor(m.wk[:], m.p[:, :, E:E + TOPK], m.invs[:, 1, :].unsqueeze(2).broadcast_to([P, TILES, TOPK]), ALU.mult).then_inc(sem(f"weigh{m.s}"), 1)
                dve.wait_ge(sem(f"weigh{m.s}"), past(count * STEPS))
                v.tensor_tensor(m.pw[:], m.pk[:], m.wk[:], ALU.mult).then_inc(sem(f"pw{m.s}"), 1)
                for i in range(TILES):
                    for k in range(TOPK):
                        ins = v.tensor_scalar(m.oh[:, k, i, :], iota, m.ixf[:, i, k:k + 1], m.wk[:, i, k:k + 1], ALU.is_equal, ALU.mult)
                ins.then_inc(sem(f"oh{m.s}"), 1)
                dve.wait_ge(sem(f"pw{m.s}"), count)
                v.tensor_reduce(m.bias[:], m.pw[:], AX.X, ALU.add)
                dve.wait_ge(sem(f"oh{m.s}"), count)
                v.tensor_tensor(m.coef[:], m.oh[:, 0], m.oh[:, 1], ALU.add).then_inc(sem(f"coef{m.s}"), 1)

            def rest(parts, whole, name):
                v.tensor_tensor(parts[:, 1], whole, parts[:, 0].bitcast(F32), ALU.subtract).then_inc(sem(name), 1)

            def body(it):
                c1, c2, c3, c4, c6, c7 = (cnt(it, k) for k in (1, 2, 3, 4, 6, 7))
                if live(it, 7):
                    dve.wait_ge(sem("acc_start2"), past((c7 - 1) * TILES + 1))
                    dve.wait_ge(sem("moe2"), past((c7 - 1) * GROUPS + 2))
                    combine(m2, 1, BANK["G2_1"], c7)
                if live(it, 2):
                    dve.wait_ge(sem("gl"), c2)
                    v.scalar_tensor_tensor(glog[:], zb[:], 0.0, ge[:], ALU.min, ALU.subtract).then_inc(sem("glog"), 1)
                    dve.wait_ge(sem("glog"), c2)
                    v.tensor_tensor_scan(gcum[:], reset, glog[:], 0.0, ALU.mult, ALU.add).then_inc(sem("gcum"), 1)
                    dve.wait_ge(sem("gcum"), c2)
                    v.tensor_tensor(bt(grel[:]), bt(gcum[:]), bt(gcum[:])[:, :, MID:MID + 1].broadcast_to([P, B, TS]), ALU.subtract).then_inc(sem("grel"), 1)
                    dve.wait_ge(sem("grel"), c2)
                    v.tensor_scalar(grel[:], grel[:], -GMAX, GMAX, ALU.max, ALU.min).then_inc(sem("gclip"), 1)
                if live(it, 3):
                    dve.wait_ge(sem("orstd"), c3)
                    v.tensor_tensor(onorm[:], ps[:, BANK["O"], :].rearrange("p (h v) -> p h v", v=DV),
                                         orstd[:].unsqueeze(2).broadcast_to([P, TILES * HEADS, DV]), ALU.mult).then_inc(sem("onorm"), 1)
                if live(it, 7):
                    dve.wait_ge(sem("moe2"), past((c7 - 1) * GROUPS + 3))
                    combine(m2, 2, BANK["G2_2"], c7)
                    dve.wait_ge(sem("moe2"), past((c7 - 1) * GROUPS + 4))
                    combine(m2, 3, BANK["G2_3"], c7)
                if live(it, 2):
                    dve.wait_ge(sem("vt1"), c2)
                    dve.wait_ge(sem("og"), past(c2 - 1))
                    v.scalar_tensor_tensor(sg[:, 1, :], th[:, 1, :], 1.0, ps[:, BANK["VG1"], D:2 * D], ALU.add, ALU.mult).then_inc(sem("sg1"), 1)
                if live(it, 7):
                    dve.wait_ge(sem("acc_start2"), c7 * TILES)
                    dve.wait_ge(sem("moe2"), past((c7 - 1) * GROUPS + 6))
                    combine(m2, 5, BANK["G2_5"], c7)
                if live(it, 2):
                    dve.wait_ge(sem("emid"), c2)
                    dve.wait_ge(sem("QK"), c2)
                    v.scalar_tensor_tensor(qt[:], ps[:, BANK["QK"], 0:TOK], QSCALE, eq[:].rearrange("p b t -> p (b t)"), ALU.mult, ALU.mult).then_inc(sem("qt"), 1)
                    v.tensor_tensor(kt[:], ps[:, BANK["QK"], TOK:2 * TOK], ek[:].rearrange("p b t -> p (b t)"), ALU.mult)
                    dve.wait_ge(sem("qt"), c2)
                    for h in range(HQ):
                        ins = v.tensor_scalar(qx[:, h, :], qt[:], headmask[:, h:h + 1], None, ALU.mult)
                    ins.then_inc(sem("qx"), 1)
                if live(it, 3):
                    dve.wait_ge(sem("oT_lead"), c3)
                    rest(oTs, by_chunk("OG"), "oTs")
                if live(it, 7):
                    dve.wait_ge(sem("moe2"), past((c7 - 1) * GROUPS + 7))
                    combine(m2, 6, BANK["G2_6"], c7)
                if live(it, 2):
                    dve.wait_ge(sem("vt0"), c2)
                    v.scalar_tensor_tensor(sg[:, 0, :], th[:, 0, :], 1.0, ps[:, BANK["VG0"], D:2 * D], ALU.add, ALU.mult).then_inc(sem("sg0"), 1)
                if live(it, 4):
                    dve.wait_ge(sem("gT0"), c4)
                    rest(gTs, gT[:], "gTs")
                if live(it, 1):
                    dve.wait_ge(sem("x_loaded"), c1 * 16 * B)
                    dve.wait_ge(sem("nrm"), past(c1 - 1))
                    stats(xin, st_a, mv_a, "a", c1)
                if live(it, 6):
                    dve.wait_ge(sem("RO"), c6)
                    v.tensor_tensor(m2.x[:].rearrange("p i d -> p (i d)"), ps[:, BANK["RO"], :], x2b[:].rearrange("p i d -> p (i d)"), ALU.add).then_inc(sem("x3"), 1)
                    dve.wait_ge(sem("x3"), c6)
                    stats(m2.x, m2.st, m2.mv, "m2", c6)
                if live(it, 4):
                    dve.wait_ge(sem("F2"), c4)
                    v.tensor_tensor(m1.x[:].rearrange("p i d -> p (i d)"), ps[:, BANK["F2"], :], res[:].rearrange("p i d -> p (i d)"), ALU.add).then_inc(sem("x1"), 1)
                    dve.wait_ge(sem("x1"), c4)
                    stats(m1.x, m1.st, m1.mv, "m1", c4)
                if live(it, 2):
                    dve.wait_ge(sem("DS1"), c2)
                    v.tensor_tensor(att[:], ps[:, SD:SD + J, 0:TILES * P].rearrange("p j (g t) -> p j g t", t=TS),
                                         causal.unsqueeze(1).unsqueeze(1).broadcast_to([P, J, TILES * HQ, TS]), ALU.mult).then_inc(sem("att"), 1)
                if live(it, 1):
                    dve.wait_ge(sem("rstd_inner"), c1)
                    normed(y0, xin, mv_a[:, :, 0], ra[:, 6, :]).then_inc(sem("y0"), 1)
                if live(it, 2):
                    dve.wait_ge(sem("att"), c2)
                    v.tensor_tensor(dstate[:].rearrange("p (i q) c -> p i q c", q=BQ),
                                         ps[:, SD:SD + BQ, TOK:TOK + TILES * HQ * DV].rearrange("p q (i c) -> p i q c", i=TILES),
                                         eq[:, :, TS - 1:TS].rearrange("p (i q) o -> p i q o", q=BQ).broadcast_to([P, TILES, BQ, HQ * DV]),
                                         ALU.mult).then_inc(sem("dstate"), 1)
                if live(it, 3):
                    v.tensor_tensor(xmid[:].rearrange("p i d -> p (i d)"), ps[:, BANK["WO"], :], xhat[:].rearrange("p i d -> p (i d)"), ALU.add).then_inc(sem("xmid"), 1)
                    dve.wait_ge(sem("xmid"), c3)
                    stats(xmid, st_f, mv_f, "f", c3)
                if live(it, 4):
                    dve.wait_ge(sem("lead1"), c4)
                    rest(m1.yT, by_chunk("T1"), "yT1")
                if live(it, 6):
                    dve.wait_ge(sem("lead2"), c6)
                    rest(m2.yT, by_chunk("T2"), "yT2")
                if live(it, 3):
                    dve.wait_ge(sem("rstd_f"), c3)
                    normed(y1, xmid, mv_f[:, :, 0], rf[:, 1, :]).then_inc(sem("y1"), 1)
                if live(it, 4):
                    dve.wait_ge(sem("L1"), c4)
                    route(m1, BANK["L1"], c4)
                    dve.wait_ge(sem("p1"), c4)
                    weigh(m1, c4)
                if live(it, 7):
                    dve.wait_ge(sem("moe2"), c7 * GROUPS)
                    combine(m2, 7, BANK["G2_7"], c7)
                if live(it, 6):
                    dve.wait_ge(sem("L2"), c6)
                    route(m2, BANK["L2"], c6)
                if live(it, 1):
                    dve.wait_ge(sem("hT0"), c1)
                    rest(hTs, hT[:], "hTs")
                if live(it, 4):
                    dve.wait_ge(sem("acc_start1"), past((c4 - 1) * TILES + 1))
                    dve.wait_ge(sem("moe1"), past((c4 - 1) * GROUPS + 2))
                    combine(m1, 1, BANK["G1_1"], c4)
                    dve.wait_ge(sem("moe1"), past((c4 - 1) * GROUPS + 3))
                    combine(m1, 2, BANK["G1_2"], c4)
                if live(it, 3):
                    dve.wait_ge(sem("h2T0"), c3)
                    rest(h2Ts, h2T[:], "h2Ts")
                if live(it, 2):
                    dve.wait_ge(sem("osq"), c2)
                    v.tensor_reduce(oss[:], osq[:], AX.X, ALU.add).then_inc(sem("oss"), 1)
                if live(it, 4):
                    dve.wait_ge(sem("moe1"), past((c4 - 1) * GROUPS + 4))
                    combine(m1, 3, BANK["G1_3"], c4)
                if live(it, 1):
                    dve.wait_ge(sem("zb"), c1)
                    v.scalar_tensor_tensor(nz[:], zb[:], -1.0, zb[:], ALU.mult, ALU.min).then_inc(sem("nz"), 1)
                if live(it, 6):
                    dve.wait_ge(sem("p2"), c6)
                    weigh(m2, c6)
                if live(it, 4):
                    dve.wait_ge(sem("acc_start1"), c4 * TILES)
                    dve.wait_ge(sem("moe1"), past((c4 - 1) * GROUPS + 6))
                    combine(m1, 5, BANK["G1_5"], c4)
                if live(it, 2):
                    dve.wait_ge(sem("x_again"), c2 * 16 * B)
                    normed(xhat, xag, nrm[:, 0, :], nrm[:, 1, :]).then_inc(sem("xhat"), 1)
                if live(it, 4):
                    dve.wait_ge(sem("moe1"), past((c4 - 1) * GROUPS + 7))
                    combine(m1, 6, BANK["G1_6"], c4)
                    dve.wait_ge(sem("moe1"), c4 * GROUPS)
                    combine(m1, 7, BANK["G1_7"], c4)
                    dve.wait_ge(sem("acc1"), c4 * VECTOR_GROUPS * 2)
                    stats(m1.acc, st_r, mv_r, "r", c4)

            rounds(dve, body, split_experts)

        @block.tensor
        def _(pe):
            t = nc.tensor
            pe.wait_ge(sem("weights"), WEIGHTS)
            pe.wait_ge(sem("pads_zero"), 1)
            for c in range(KC):
                ins = t.matmul(ps[0:N, 0, 0:D], cT[:, c, :], woutT[:, c, :], start=(c == 0), stop=(c == KC - 1))
            ins.then_inc(sem("cw_psum"), 1)
            for c in range(KC):
                ins = t.matmul(ps[:, 1, c * P:(c + 1) * P], w1T[:, c * P:(c + 1) * P], w2g[:], start=True, stop=True)
            ins.then_inc(sem("wz_psum"), 1)
            pe.wait_ge(sem("wz_split"), 1)
            pe.wait_ge(sem("a_loaded"), 16)
            pe.wait_ge(sem("cw"), 1)
            pe.wait_ge(sem("wa_split"), 1)
            pe.wait_ge(sem("rw_split"), 1)

            def product(dst, left, right, chunks):
                n = 0
                for c in range(chunks):
                    for lp, rp in ((0, 0), (0, 1), (1, 0)):
                        n += 1
                        ins = t.matmul(dst, left(lp, c), right(rp, c), start=(n == 1), stop=(n == 3 * chunks))
                return ins

            def transposed(dst_bank, src, tiles=TILES):
                for c in range(KC):
                    for i in range(TILES):
                        ins = t.transpose(ps[:, dst_bank, c * TOK + i * P:c * TOK + (i + 1) * P], src[:, i, c * P:(c + 1) * P], ident)
                return ins

            def moe(m, k, bank):
                i, pr = k // PAIRS, k % PAIRS
                right = lambda p, c: we[:, p, c * E * D + pr * 2 * D:c * E * D + (pr + 1) * 2 * D]
                return product(ps[:, bank, :], lambda p, c: m.yT[:, p, c, i * P:(i + 1) * P], right, KC)

            def recur(k):
                return t.matmul(bt(ps[0:NP, BANK["RB"], 0:TOK])[:, :, k], aT[:],
                                hs[:, :, (k - 1) % TS], start=False, stop=True, skip_group_check=True)

            def logits(m, bank):
                for i in range(TILES):
                    for c in range(KC):
                        rows, o = slice(i * P, (i + 1) * P), i * 2 * E
                        t.matmul(ps[:, bank, o:o + 2 * E], m.yT[:, 0, c, rows], rws[:, c].rearrange("p s e -> p (s e)"),
                                 start=(c == 0), stop=False, skip_group_check=True)
                        ins = t.matmul(ps[:, bank, o:o + E], m.yT[:, 1, c, rows], rws[:, c, 0, :],
                                       start=False, stop=(c == KC - 1), skip_group_check=True)
                return ins

            def scores(i):
                for q in range(BQ):
                    b = i * BQ + q
                    for j in range(J):
                        r = slice(32 * j, 32 * j + 32)
                        ins = t.matmul(ps[q * 32:q * 32 + 32, SD + j, i * P:(i + 1) * P], kt[r, b * TS:(b + 1) * TS],
                                       qx[r, :, b * TS:(b + 1) * TS], start=True, stop=True)
                return ins

            def state_update(i):
                for q in range(BQ):
                    r = slice(q * 32, q * 32 + 32)
                    for j in range(J):
                        ins = t.matmul(ps[32 * j:32 * j + 32, SD + q, TOK + i * HQ * DV:TOK + (i + 1) * HQ * DV],
                                       ktok[r, i, 32 * j:32 * j + 32], vtok[r, i, j * HQ * DV:(j + 1) * HQ * DV], start=True, stop=True)
                return ins

            def attend(i, half):
                r = lambda q: slice(q * 32, q * 32 + 32)
                if half == 0:
                    for q in range(BQ):
                        b = i * BQ + q
                        t.matmul(ps[r(q), BANK["O"], i * D:(i + 1) * D], qt[:, b * TS:(b + 1) * TS], sx[:, b, :],
                                 start=True, stop=False, skip_group_check=True)
                for q in range(half * BQ // 2, (half + 1) * BQ // 2):
                    for h in range(HEADS):
                        ins = t.matmul(ps[r(q), BANK["O"], i * D + h * DV:i * D + (h + 1) * DV], att[r(q), h // HQ, i * HQ + h % HQ, :],
                                       vtok[r(q), i, h * DV:(h + 1) * DV], start=False, stop=(h == HEADS - 1), skip_group_check=True)
                return ins

            def body(it):
                c1, c2, c3, c4, c5, c6, c7 = (cnt(it, k) for k in (1, 2, 3, 4, 5, 6, 7))
                if live(it, 6):
                    target = value(pe, (c6 - 1) * TS + 16)
                    pe.wait_ge(sem("weights"), WEIGHTS)
                    pe.wait_ge(sem("rnn_h"), target)
                    recur(16).then_inc(sem("rnn_mm"), 1)
                if live(it, 3):
                    attend(1, 1).then_inc(sem("O11"), 1)
                if live(it, 6):
                    target = value(pe, (c6 - 1) * TS + 17)
                    pe.wait_ge(sem("weights"), WEIGHTS)
                    pe.wait_ge(sem("rnn_h"), target)
                    recur(17).then_inc(sem("rnn_mm"), 1)
                if live(it, 5):
                    for name, count in readers(it, "G1_5"):
                        pe.wait_ge(sem(name), count)
                    moe(m1, 5, BANK["G1_5"]).then_inc(sem("moe1"), 1)
                if live(it, 6):
                    target = value(pe, (c6 - 1) * TS + 18)
                    pe.wait_ge(sem("weights"), WEIGHTS)
                    pe.wait_ge(sem("rnn_h"), target)
                    recur(18).then_inc(sem("rnn_mm"), 1)
                if live(it, 2):
                    for name, count in readers(it, "Z"):
                        pe.wait_ge(sem(name), count)
                    pe.wait_ge(sem("hTs"), c2)
                    product(ps[:, BANK["Z"], 0:TOK], lambda p, c: wz[:, p, c, :], lambda p, c: hTs[:, p, c, :], KC).then_inc(sem("Z"), 1)
                if live(it, 6):
                    target = value(pe, (c6 - 1) * TS + 19)
                    pe.wait_ge(sem("weights"), WEIGHTS)
                    pe.wait_ge(sem("rnn_h"), target)
                    recur(19).then_inc(sem("rnn_mm"), 1)
                if live(it, 5):
                    moe(m1, 6, BANK["G1_6"]).then_inc(sem("moe1"), 1)
                if live(it, 6):
                    target = value(pe, (c6 - 1) * TS + 20)
                    pe.wait_ge(sem("weights"), WEIGHTS)
                    pe.wait_ge(sem("rnn_h"), target)
                    recur(20).then_inc(sem("rnn_mm"), 1)
                if live(it, 7):
                    for name, count in readers(it, "G2_0"):
                        pe.wait_ge(sem(name), count)
                    moe(m2, 0, BANK["G2_0"]).then_inc(sem("moe2"), 1)
                if live(it, 6):
                    target = value(pe, (c6 - 1) * TS + 21)
                    pe.wait_ge(sem("weights"), WEIGHTS)
                    pe.wait_ge(sem("rnn_h"), target)
                    recur(21).then_inc(sem("rnn_mm"), 1)
                if live(it, 5):
                    for name, count in readers(it, "G1_7"):
                        pe.wait_ge(sem(name), count)
                    moe(m1, 7, BANK["G1_7"]).then_inc(sem("moe1"), 1)
                if live(it, 4):
                    pe.wait_ge(sem("h2Ts"), c4)
                    for f in range(0, 2):
                        ins = product(ps[:, BANK["F1A"], f % 2 * TOK:(f % 2 + 1) * TOK], lambda p, c: wcols(W_1, p, c, FF, f * P, P),
                                      lambda p, c: h2Ts[:, p, c, :], KC)
                if live(it, 6):
                    target = value(pe, (c6 - 1) * TS + 22)
                    pe.wait_ge(sem("weights"), WEIGHTS)
                    pe.wait_ge(sem("rnn_h"), target)
                    recur(22).then_inc(sem("rnn_mm"), 1)
                if live(it, 4):
                    for name, count in readers(it, "F1B"):
                        pe.wait_ge(sem(name), count)
                    for f in range(2, 4):
                        ins = product(ps[:, BANK["F1B"], f % 2 * TOK:(f % 2 + 1) * TOK], lambda p, c: wcols(W_1, p, c, FF, f * P, P),
                                      lambda p, c: h2Ts[:, p, c, :], KC)
                    ins.then_inc(sem("F1B"), 1)
                if live(it, 6):
                    target = value(pe, (c6 - 1) * TS + 23)
                    pe.wait_ge(sem("weights"), WEIGHTS)
                    pe.wait_ge(sem("rnn_h"), target)
                    recur(23).then_inc(sem("rnn_mm"), 1)
                if live(it, 7):
                    for name, count in readers(it, "G2_1"):
                        pe.wait_ge(sem(name), count)
                    moe(m2, 1, BANK["G2_1"]).then_inc(sem("moe2"), 1)
                if live(it, 2):
                    for name, count in readers(it, "VG1"):
                        pe.wait_ge(sem(name), count)
                    product(ps[:, BANK["VG1"], :], lambda p, c: hTs[:, p, c, 1 * P:2 * P],
                                 lambda p, c: wcols(W_VG, p, c, 2 * D, 0, 2 * D), KC).then_inc(sem("VG1"), 1)
                if live(it, 6):
                    target = value(pe, (c6 - 1) * TS + 24)
                    pe.wait_ge(sem("weights"), WEIGHTS)
                    pe.wait_ge(sem("rnn_h"), target)
                    recur(24).then_inc(sem("rnn_mm"), 1)
                if live(it, 7):
                    for name, count in readers(it, "G2_2"):
                        pe.wait_ge(sem(name), count)
                    moe(m2, 2, BANK["G2_2"]).then_inc(sem("moe2"), 1)
                    for name, count in readers(it, "G2_3"):
                        pe.wait_ge(sem(name), count)
                    moe(m2, 3, BANK["G2_3"]).then_inc(sem("moe2"), 1)
                if live(it, 6):
                    target = value(pe, (c6 - 1) * TS + 25)
                    pe.wait_ge(sem("weights"), WEIGHTS)
                    pe.wait_ge(sem("rnn_h"), target)
                    recur(25).then_inc(sem("rnn_mm"), 1)
                if live(it, 7):
                    for name, count in readers(it, "G2_4"):
                        pe.wait_ge(sem(name), count)
                    moe(m2, 4, BANK["G2_4"]).then_inc(sem("moe2"), 1)
                if live(it, 6):
                    target = value(pe, (c6 - 1) * TS + 26)
                    pe.wait_ge(sem("weights"), WEIGHTS)
                    pe.wait_ge(sem("rnn_h"), target)
                    recur(26).then_inc(sem("rnn_mm"), 1)
                if live(it, 7):
                    for name, count in readers(it, "G2_5"):
                        pe.wait_ge(sem(name), count)
                    moe(m2, 5, BANK["G2_5"]).then_inc(sem("moe2"), 1)
                if live(it, 6):
                    target = value(pe, (c6 - 1) * TS + 27)
                    pe.wait_ge(sem("weights"), WEIGHTS)
                    pe.wait_ge(sem("rnn_h"), target)
                    recur(27).then_inc(sem("rnn_mm"), 1)
                if live(it, 2):
                    for name, count in readers(it, "QK"):
                        pe.wait_ge(sem(name), count)
                    for w, col in ((W_Q, 0), (W_K, TOK)):
                        ins = product(ps[:, BANK["QK"], col:col + TOK], lambda p, c: wcols(w, p, c, P, 0, P), lambda p, c: hTs[:, p, c, :], KC)
                    ins.then_inc(sem("QK"), 1)
                if live(it, 6):
                    target = value(pe, (c6 - 1) * TS + 28)
                    pe.wait_ge(sem("weights"), WEIGHTS)
                    pe.wait_ge(sem("rnn_h"), target)
                    recur(28).then_inc(sem("rnn_mm"), 1)
                if live(it, 5):
                    for name, count in readers(it, "TR"):
                        pe.wait_ge(sem(name), count)
                    pe.wait_ge(sem("yr"), c5)
                    transposed(BANK["TR"], yr).then_inc(sem("TR"), 1)
                if live(it, 6):
                    target = value(pe, (c6 - 1) * TS + 29)
                    pe.wait_ge(sem("weights"), WEIGHTS)
                    pe.wait_ge(sem("rnn_h"), target)
                    recur(29).then_inc(sem("rnn_mm"), 1)
                if live(it, 7):
                    for name, count in readers(it, "G2_6"):
                        pe.wait_ge(sem(name), count)
                    moe(m2, 6, BANK["G2_6"]).then_inc(sem("moe2"), 1)
                if live(it, 6):
                    target = value(pe, (c6 - 1) * TS + 30)
                    pe.wait_ge(sem("weights"), WEIGHTS)
                    pe.wait_ge(sem("rnn_h"), target)
                    recur(30).then_inc(sem("rnn_mm"), 1)
                if live(it, 3):
                    pe.wait_ge(sem("og"), c3)
                    transposed(BANK["OG"], og).then_inc(sem("OG"), 1)
                if live(it, 6):
                    target = value(pe, (c6 - 1) * TS + 31)
                    pe.wait_ge(sem("weights"), WEIGHTS)
                    pe.wait_ge(sem("rnn_h"), target)
                    recur(31).then_inc(sem("rnn_mm"), 1)
                if live(it, 2):
                    for name, count in readers(it, "VG0"):
                        pe.wait_ge(sem(name), count)
                    product(ps[:, BANK["VG0"], :], lambda p, c: hTs[:, p, c, 0 * P:1 * P],
                                 lambda p, c: wcols(W_VG, p, c, 2 * D, 0, 2 * D), KC).then_inc(sem("VG0"), 1)
                if live(it, 5):
                    for name, count in readers(it, "RB"):
                        pe.wait_ge(sem(name), count)
                    pe.wait_ge(sem("yrT"), c5)
                    for c in range(KC):
                        ins = t.matmul(ps[0:NP, BANK["RB"], 0:TOK], bin_[:, c, :], yrT[:, c, :], start=(c == 0), stop=(c == KC - 1), skip_group_check=True)
                if live(it, 6):
                    pe.wait_ge(sem("rnn_h"), c6 * TS)
                    for i in range(TILES):
                        ins = t.matmul(ps[:, BANK["RO"], i * D:(i + 1) * D],
                                       hs[0:N, i * BQ:(i + 1) * BQ, :].rearrange("p b t -> p (b t)"), cw[:], start=True, stop=True)
                    ins.then_inc(sem("RO"), 1)
                if live(it, 2):
                    for name, count in readers(it, "KT"):
                        pe.wait_ge(sem(name), count)
                    for i in range(TILES):
                        ins = t.transpose(ps[:, BANK["KT"], i * P:(i + 1) * P], kt[:, i * P:(i + 1) * P], ident)
                    ins.then_inc(sem("KT"), 1)
                if live(it, 3):
                    for name, count in readers(it, "WO"):
                        pe.wait_ge(sem(name), count)
                    for i in range(TILES):
                        ins = product(ps[:, BANK["WO"], i * D:(i + 1) * D], lambda p, c: oTs[:, p, c, i * P:(i + 1) * P],
                                      lambda p, c: wcols(W_O, p, c, D, 0, D), KC)
                if live(it, 5):
                    recur(0).then_inc(sem("rnn_mm"), 1)
                if live(it, 2):
                    free = [(name, value(pe, count)) for name, count in readers(it, "SD")]
                    pe.wait_ge(sem("weights"), WEIGHTS)
                    for name, count in free:
                        pe.wait_ge(sem(name), count)
                    scores(0)
                if live(it, 5):
                    target = value(pe, (c5 - 1) * TS + 1)
                    pe.wait_ge(sem("weights"), WEIGHTS)
                    pe.wait_ge(sem("rnn_h"), target)
                    recur(1).then_inc(sem("rnn_mm"), 1)
                if live(it, 4):
                    for name, count in readers(it, "F2"):
                        pe.wait_ge(sem(name), count)
                    pe.wait_ge(sem("gTs"), c4)
                    for i in range(TILES):
                        ins = product(ps[:, BANK["F2"], i * D:(i + 1) * D], lambda p, f: gTs[:, p, f, i * P:(i + 1) * P],
                                      lambda p, f: wcols(W_2, p, f, D, 0, D), FB)
                    ins.then_inc(sem("F2"), 1)
                if live(it, 5):
                    target = value(pe, (c5 - 1) * TS + 2)
                    pe.wait_ge(sem("weights"), WEIGHTS)
                    pe.wait_ge(sem("rnn_h"), target)
                    recur(2).then_inc(sem("rnn_mm"), 1)
                if live(it, 2):
                    scores(1)
                if live(it, 5):
                    target = value(pe, (c5 - 1) * TS + 3)
                    pe.wait_ge(sem("weights"), WEIGHTS)
                    pe.wait_ge(sem("rnn_h"), target)
                    recur(3).then_inc(sem("rnn_mm"), 1)
                if live(it, 2):
                    target = value(pe, c2)
                    pe.wait_ge(sem("weights"), WEIGHTS)
                    pe.wait_ge(sem("ktok"), target)
                    state_update(0)
                if live(it, 5):
                    target = value(pe, (c5 - 1) * TS + 4)
                    pe.wait_ge(sem("weights"), WEIGHTS)
                    pe.wait_ge(sem("rnn_h"), target)
                    recur(4).then_inc(sem("rnn_mm"), 1)
                if live(it, 2):
                    state_update(1).then_inc(sem("DS1"), 1)
                if live(it, 5):
                    target = value(pe, (c5 - 1) * TS + 5)
                    pe.wait_ge(sem("weights"), WEIGHTS)
                    pe.wait_ge(sem("rnn_h"), target)
                    recur(5).then_inc(sem("rnn_mm"), 1)
                if live(it, 7):
                    for name, count in readers(it, "G2_7"):
                        pe.wait_ge(sem(name), count)
                    moe(m2, 7, BANK["G2_7"]).then_inc(sem("moe2"), 1)
                if live(it, 5):
                    target = value(pe, (c5 - 1) * TS + 6)
                    pe.wait_ge(sem("weights"), WEIGHTS)
                    pe.wait_ge(sem("rnn_h"), target)
                    recur(6).then_inc(sem("rnn_mm"), 1)
                if live(it, 2):
                    pe.wait_ge(sem("dec"), c2)
                    pe.wait_ge(sem("att"), c2)
                    attend(0, 0)
                if live(it, 5):
                    target = value(pe, (c5 - 1) * TS + 7)
                    pe.wait_ge(sem("weights"), WEIGHTS)
                    pe.wait_ge(sem("rnn_h"), target)
                    recur(7).then_inc(sem("rnn_mm"), 1)
                if live(it, 4):
                    for name, count in readers(it, "T1"):
                        pe.wait_ge(sem(name), count)
                    pe.wait_ge(sem("ym1"), c4)
                    transposed(BANK["T1"], m1.y).then_inc(sem("T1"), 1)
                if live(it, 6):
                    pe.wait_ge(sem("ym2"), c6)
                    transposed(BANK["T2"], m2.y).then_inc(sem("T2"), 1)
                if live(it, 1):
                    for name, count in readers(it, "Y0"):
                        pe.wait_ge(sem(name), count)
                    pe.wait_ge(sem("y0"), c1)
                    transposed(BANK["Y0"], y0).then_inc(sem("Y0"), 1)
                if live(it, 5):
                    target = value(pe, (c5 - 1) * TS + 8)
                    pe.wait_ge(sem("weights"), WEIGHTS)
                    pe.wait_ge(sem("rnn_h"), target)
                    recur(8).then_inc(sem("rnn_mm"), 1)
                if live(it, 2):
                    attend(0, 1)
                if live(it, 4):
                    pe.wait_ge(sem("yT1"), c4)
                    pe.wait_ge(sem("we_split"), 1)
                    moe(m1, 0, BANK["G1_0"]).then_inc(sem("moe1"), 1)
                if live(it, 5):
                    target = value(pe, (c5 - 1) * TS + 9)
                    pe.wait_ge(sem("weights"), WEIGHTS)
                    pe.wait_ge(sem("rnn_h"), target)
                    recur(9).then_inc(sem("rnn_mm"), 1)
                if live(it, 4):
                    logits(m1, BANK["L1"]).then_inc(sem("L1"), 1)
                if live(it, 5):
                    target = value(pe, (c5 - 1) * TS + 10)
                    pe.wait_ge(sem("weights"), WEIGHTS)
                    pe.wait_ge(sem("rnn_h"), target)
                    recur(10).then_inc(sem("rnn_mm"), 1)
                if live(it, 4):
                    moe(m1, 1, BANK["G1_1"]).then_inc(sem("moe1"), 1)
                if live(it, 5):
                    target = value(pe, (c5 - 1) * TS + 11)
                    pe.wait_ge(sem("weights"), WEIGHTS)
                    pe.wait_ge(sem("rnn_h"), target)
                    recur(11).then_inc(sem("rnn_mm"), 1)
                if live(it, 6):
                    for name, count in readers(it, "L2"):
                        pe.wait_ge(sem(name), count)
                    logits(m2, BANK["L2"]).then_inc(sem("L2"), 1)
                if live(it, 5):
                    target = value(pe, (c5 - 1) * TS + 12)
                    pe.wait_ge(sem("weights"), WEIGHTS)
                    pe.wait_ge(sem("rnn_h"), target)
                    recur(12).then_inc(sem("rnn_mm"), 1)
                if live(it, 4):
                    for name, count in readers(it, "G1_2"):
                        pe.wait_ge(sem(name), count)
                    moe(m1, 2, BANK["G1_2"]).then_inc(sem("moe1"), 1)
                if live(it, 5):
                    target = value(pe, (c5 - 1) * TS + 13)
                    pe.wait_ge(sem("weights"), WEIGHTS)
                    pe.wait_ge(sem("rnn_h"), target)
                    recur(13).then_inc(sem("rnn_mm"), 1)
                if live(it, 4):
                    for name, count in readers(it, "G1_3"):
                        pe.wait_ge(sem(name), count)
                    moe(m1, 3, BANK["G1_3"]).then_inc(sem("moe1"), 1)
                if live(it, 5):
                    target = value(pe, (c5 - 1) * TS + 14)
                    pe.wait_ge(sem("weights"), WEIGHTS)
                    pe.wait_ge(sem("rnn_h"), target)
                    recur(14).then_inc(sem("rnn_mm"), 1)
                if live(it, 2):
                    attend(1, 0)
                if live(it, 5):
                    target = value(pe, (c5 - 1) * TS + 15)
                    pe.wait_ge(sem("weights"), WEIGHTS)
                    pe.wait_ge(sem("rnn_h"), target)
                    recur(15).then_inc(sem("rnn_mm"), 1)
                if live(it, 3):
                    for name, count in readers(it, "Y1"):
                        pe.wait_ge(sem(name), count)
                    pe.wait_ge(sem("y1"), c3)
                    transposed(BANK["Y1"], y1).then_inc(sem("Y1"), 1)
                if live(it, 4):
                    for name, count in readers(it, "G1_4"):
                        pe.wait_ge(sem(name), count)
                    moe(m1, 4, BANK["G1_4"]).then_inc(sem("moe1"), 1)

            rounds(pe, body)


def kernel(**inputs):
    import numpy as _np
    import concourse.bacc as _bacc
    from concourse import mybir as _mybir
    from concourse.bass_utils import run_bass_kernel_spmd as _run

    a = {k.replace("L0_attn_a_", "").replace("L0_attn_b_", "rnn_").replace("L0_ffn_", ""): _np.asarray(v) for k, v in inputs.items()}

    def rows(w):
        return _np.ascontiguousarray(w.reshape(-1, P, w.shape[1]).transpose(1, 0, 2))

    def cols(b):
        return _np.ascontiguousarray(b.reshape(-1, P).T)

    def everywhere(b):
        return _np.ascontiguousarray(_np.broadcast_to(b, (P, b.shape[0])))

    arrays = {
        "x": a["x"], "consts": constants(), "ln_w": cols(a["ln_w"]), "ln_b": cols(a["ln_b"]),
        "Wq": rows(a["Wq"]), "Wk": rows(a["Wk"]), "Wvg": rows(_np.concatenate([a["Wv"], a["Wg"]], axis=1)),
        "gk_w1T": _np.ascontiguousarray(a["gk_w1"].T), "gk_w2": a["gk_w2"], "gk_b2": cols(a["gk_b2"]),
        "rms_w": _np.ascontiguousarray(_np.broadcast_to(a["rms_w"], (P // DV, DV)).reshape(P, 1)),
        "Wo": rows(a["Wo"]), "W1": rows(a["W1"]), "b1": cols(a["b1"]), "W2": rows(a["W2"]), "b2": everywhere(a["b2"]),
        "router_w": rows(a["router_w"].T),
        "experts": _np.ascontiguousarray(a["expert_weights"].reshape(E, KC, P, D).transpose(2, 1, 0, 3)),
        "Bin": rows(a["rnn_B"]), "A": _np.ascontiguousarray(a["rnn_A"].T), "C": rows(a["rnn_C"].T),
        "W_out": rows(a["rnn_W_out"].T), "b_out": everywhere(a["rnn_b_out"]),
    }
    nc = _bacc.Bacc("TRN2", target_bir_lowering=False, num_devices=1)
    arrays = {f"in_{k}": _np.ascontiguousarray(v) for k, v in arrays.items()}
    drams = {k[3:]: nc.dram_tensor(k, v.shape, _mybir.dt.from_np(v.dtype), kind="ExternalInput").ap() for k, v in arrays.items()}
    out = nc.dram_tensor("out", (B, T, D), _mybir.dt.float32, kind="ExternalOutput").ap()
    x = drams.pop("x")
    build(nc, x, drams, out)
    r = _run(nc, [arrays], core_ids=[0])
    return r.results[0]["out"]
```
